# Optimizing a Trainium2 kernel written in Bass

```python
import numpy as np
import jax
import jax.numpy as jnp

def _softmax(x, axis=-1):
    return jax.nn.softmax(x, axis=axis)
def _gelu(x):
    return jax.nn.gelu(x, approximate=True)
def _silu(x):
    return jax.nn.silu(x)
def _sigmoid(x):
    return jax.nn.sigmoid(x)
def _layernorm(x, axis=-1, eps=1e-5):
    m = jnp.mean(x, axis=axis, keepdims=True)
    v = jnp.var(x, axis=axis, keepdims=True)
    return (x - m) / jnp.sqrt(v + eps)
def _scatter_add(tgt, idx, src, axis=0):
    return tgt.at[idx].add(src)
def _segment_sum(src, seg, n):
    return jax.ops.segment_sum(src, seg, n)

kernel_name = 'mk_conv_preact_d2_conv_nhwc192_4e6253'

def setup_inputs(seed: int = 0):
    np.random.seed(seed)
    _w = jnp.asarray
    def _rec_inputs():
        import jax
        import jax.numpy as jnp
        _gk = jax.random.key(seed)
        x = -9.309e-05 + 1 * jax.random.normal(jax.random.fold_in(_gk, 1), (8, 56, 56, 192), jnp.float32)
        return x
    x = _rec_inputs()
    def _L0_conv_setup():
        import jax, jax.numpy as jnp
        import numpy as np
        EMBED = 192
        EXPAND = 3
        D1 = EMBED * EXPAND
        RPE_IN = 32
        LAYERS = 3
        LAMBDA = 0.95

        def _rpe_mlp(t, w0, b0, ws, bs, wo, bo):
            h = t @ w0.T + b0
            for i in range(ws.shape[0]):
                h = jax.nn.relu(h) @ ws[i].T + bs[i]
            return jax.nn.relu(h) @ wo.T + bo

        def _toeplitz(x, a):
            n = x.shape[1]
            m = 2 * n
            xf = jnp.fft.rfft(x, m, axis=1)
            af = jnp.fft.rfft(a, m, axis=0)
            return jnp.fft.irfft(xf * af[None], m, axis=1)[:, :n]

        def _forward(x, p_w, p_b, q_w, q_b, v_w, v_b, o_w, o_b, slope, t1_w0, t1_b0, t1_ws, t1_bs, t1_wo, t1_bo, t2_w0, t2_b0, t2_ws, t2_bs, t2_wo, t2_bo):
            b, h, w, d = x.shape
            n = h
            dt = x.dtype
            pos = jnp.arange(1, n, dtype=dt).reshape(-1, 1)
            zero = jnp.zeros((1, 1), dt)
            rpe_input = jnp.concatenate([zero, pos, zero, -pos], axis=0)
            p = jax.nn.silu(x @ p_w.T + p_b)
            q = jax.nn.silu(x @ q_w.T + q_b)
            v = jax.nn.silu(x @ v_w.T + v_b)
            sl = LAMBDA + (1.0 - LAMBDA) * jnp.clip(slope, 0.0, 1.0)
            idx = jnp.arange(1, n, dtype=dt).reshape(1, -1, 1)
            gamma = sl ** idx
            one = jnp.ones((1, 1, D1), dt)
            decay = jnp.concatenate([one, gamma, one, gamma[:, ::-1]], axis=1)[0]
            a1 = _rpe_mlp(rpe_input, t1_w0, t1_b0, t1_ws, t1_bs, t1_wo, t1_bo) * decay
            a2 = _rpe_mlp(rpe_input, t2_w0, t2_b0, t2_ws, t2_bs, t2_wo, t2_bo) * decay
            qv = q * v
            o1 = _toeplitz(qv.reshape(b * h, w, D1), a1).reshape(b, h, w, D1)
            o2 = _toeplitz(jnp.transpose(qv, (0, 2, 1, 3)).reshape(b * w, h, D1), a2)
            o2 = jnp.transpose(o2.reshape(b, w, h, D1), (0, 2, 1, 3))
            out = p * (o1 + o2)
            return out @ o_w.T + o_b
        key = jax.random.key(seed)
        ks = jax.random.split(key, 8)

        def lin(k, out_d, in_d):
            k1, k2 = jax.random.split(k)
            s = 1.0 / np.sqrt(in_d)
            return (jax.random.uniform(k1, (out_d, in_d), jnp.float32, -s, s), jax.random.uniform(k2, (out_d,), jnp.float32, -s, s))
        x = jax.random.normal(ks[0], (8, 56, 56, EMBED), jnp.float32)
        p_w, p_b = lin(ks[1], D1, EMBED)
        q_w, q_b = lin(ks[2], D1, EMBED)
        v_w, v_b = lin(ks[3], D1, EMBED)
        o_w, o_b = lin(ks[4], EMBED, D1)
        slope = (1.0 / jnp.arange(1, D1 + 1, dtype=jnp.float32)).reshape(1, -1)

        def tno_params(kb):
            kk = jax.random.split(kb, 2 + LAYERS)
            w0, b0 = lin(kk[0], RPE_IN, 1)
            ws, bs = ([], [])
            for i in range(LAYERS):
                wi, bi = lin(kk[1 + i], RPE_IN, RPE_IN)
                ws.append(wi)
                bs.append(bi)
            wo, bo = lin(kk[1 + LAYERS], D1, RPE_IN)
            return (w0, b0, jnp.stack(ws), jnp.stack(bs), wo, bo)
        t1 = tno_params(ks[5])
        t2 = tno_params(ks[6])
        return {'x': x, 'p_w': p_w, 'p_b': p_b, 'q_w': q_w, 'q_b': q_b, 'v_w': v_w, 'v_b': v_b, 'o_w': o_w, 'o_b': o_b, 'slope': slope, 't1_w0': t1[0], 't1_b0': t1[1], 't1_ws': t1[2], 't1_bs': t1[3], 't1_wo': t1[4], 't1_bo': t1[5], 't2_w0': t2[0], 't2_b0': t2[1], 't2_ws': t2[2], 't2_bs': t2[3], 't2_wo': t2[4], 't2_bo': t2[5]}
    _L0_conv_all = _L0_conv_setup()
    _L0_conv_in = {k: v for k, v in _L0_conv_all.items() if k in ('p_w', 'p_b', 'q_w', 'q_b', 'v_w', 'v_b', 'o_w', 'o_b', 'slope', 't1_w0', 't1_b0', 't1_ws', 't1_bs', 't1_wo', 't1_bo', 't2_w0', 't2_b0', 't2_ws', 't2_bs', 't2_wo', 't2_bo', )}
    del _L0_conv_all

    def _L1_conv_setup():
        import jax, jax.numpy as jnp
        import numpy as np
        CHUNK = 64

        def _ssd_chunk_scan(x, dt, A, Bs, Cs, R):
            Bsz, L, Hh, P = x.shape
            K, N = (Bs.shape[2], Bs.shape[3])
            Nc = L // CHUNK
            Bh = jnp.repeat(Bs, R, axis=2)
            Ch = jnp.repeat(Cs, R, axis=2)
            xc = x.reshape(Bsz, Nc, CHUNK, Hh, P)
            dtc = dt.reshape(Bsz, Nc, CHUNK, Hh)
            Bc = Bh.reshape(Bsz, Nc, CHUNK, Hh, N)
            Cc = Ch.reshape(Bsz, Nc, CHUNK, Hh, N)
            dA = jnp.transpose(dtc, (0, 1, 3, 2)) * A[None, None, :, None]
            Acum = jnp.cumsum(dA, axis=-1)
            diff = Acum[..., :, None] - Acum[..., None, :]
            tri = jnp.tril(jnp.ones((CHUNK, CHUNK), bool))
            Lmat = jnp.where(tri, jnp.exp(diff), 0.0)
            xdt = xc * dtc[..., None]
            Y_diag = jnp.einsum('bcqhn,bcshn,bchqs,bcshp->bcqhp', Cc, Bc, Lmat, xdt)
            decay_last = jnp.exp(Acum[..., -1:] - Acum)
            states = jnp.einsum('bcqhn,bchq,bcqhp->bchpn', Bc, decay_last, xdt)
            chunk_decay = jnp.exp(Acum[..., -1])

            def step(S, inp):
                cd, st = inp
                return (cd[..., None, None] * S + st, S)
            S0 = jnp.zeros((Bsz, Hh, P, N), x.dtype)
            _, prev = jax.lax.scan(step, S0, (jnp.moveaxis(chunk_decay, 1, 0), jnp.moveaxis(states, 1, 0)))
            prev = jnp.moveaxis(prev, 0, 1)
            Y_off = jnp.einsum('bcqhn,bchpn,bchq->bcqhp', Cc, prev, jnp.exp(Acum))
            return (Y_diag + Y_off).reshape(Bsz, L, Hh, P)

        def _forward(x, in_proj_w, conv_w, conv_b, x_proj_w, A_logs, Ds, dt_bias, out_norm_g, out_norm_b, out_proj_w):
            B, H, W, Dm = x.shape
            K, R = A_logs.shape
            P = Ds.shape[2]
            d_inner = x_proj_w.shape[2]
            N = (x_proj_w.shape[1] - R) // 2
            L = H * W
            xz = jnp.einsum('bhwc,dc->bhwd', x, in_proj_w)
            xi, z = jnp.split(xz, 2, axis=-1)
            z = jax.nn.gelu(z, approximate=False)
            kern = jnp.transpose(conv_w, (2, 3, 1, 0))
            xi = jax.lax.conv_general_dilated(xi, kern, (1, 1), 'SAME', dimension_numbers=('NHWC', 'HWIO', 'NHWC'), feature_group_count=d_inner) + conv_b
            xi = jax.nn.gelu(xi, approximate=False)
            x0 = xi.reshape(B, L, d_inner)
            x1 = jnp.transpose(xi, (0, 2, 1, 3)).reshape(B, L, d_inner)
            xs = jnp.stack([x0, x1, x0[:, ::-1], x1[:, ::-1]], axis=2)
            x_dbl = jnp.einsum('blkd,kcd->blkc', xs, x_proj_w)
            dts = x_dbl[..., :R].reshape(B, L, K * R)
            Bs = x_dbl[..., R:R + N]
            Cs = x_dbl[..., R + N:]
            xs_h = xs.reshape(B, L, K * R, P)
            A = -jnp.exp(A_logs.astype(jnp.float32)).reshape(K * R)
            Dmat = Ds.astype(jnp.float32).reshape(K * R, P)
            dt = jax.nn.softplus(dts + dt_bias.reshape(K * R))
            ys = _ssd_chunk_scan(xs_h, dt, A, Bs, Cs, R) + xs_h * Dmat
            ys = ys.reshape(B, L, K, d_inner)

            def unT(y):
                return jnp.transpose(y.reshape(B, W, H, d_inner), (0, 2, 1, 3)).reshape(B, L, d_inner)
            y = ys[:, :, 0] + ys[:, ::-1, 2] + unT(ys[:, :, 1]) + unT(ys[:, ::-1, 3])
            y = y.reshape(B, H, W, d_inner)
            mu = y.mean(-1, keepdims=True)
            var = y.var(-1, keepdims=True)
            y = (y - mu) / jnp.sqrt(var + 1e-05) * out_norm_g + out_norm_b
            y = y * z
            return jnp.einsum('bhwd,cd->bhwc', y, out_proj_w)
        key = jax.random.key(seed)
        ks = jax.random.split(key, 10)
        B, H, W, Dm = (2, 64, 64, 192)
        d_inner, K, R, N = (384, 4, 12, 64)
        P = d_inner // R
        s = 0.02
        return {'x': jax.random.normal(ks[0], (B, H, W, Dm), jnp.float32), 'in_proj_w': s * jax.random.normal(ks[1], (2 * d_inner, Dm), jnp.float32), 'conv_w': s * jax.random.normal(ks[2], (d_inner, 1, 3, 3), jnp.float32), 'conv_b': s * jax.random.normal(ks[3], (d_inner,), jnp.float32), 'x_proj_w': s * jax.random.normal(ks[4], (K, R + 2 * N, d_inner), jnp.float32), 'A_logs': 0.5 * jax.random.normal(ks[5], (K, R), jnp.float32), 'Ds': jax.random.uniform(ks[6], (K, R, P), jnp.float32), 'dt_bias': 0.1 * jax.random.uniform(ks[7], (K, R), jnp.float32), 'out_norm_g': jnp.ones((d_inner,), jnp.float32), 'out_norm_b': jnp.zeros((d_inner,), jnp.float32), 'out_proj_w': s * jax.random.normal(ks[8], (Dm, d_inner), jnp.float32)}
    _L1_conv_all = _L1_conv_setup()
    _L1_conv_in = {k: v for k, v in _L1_conv_all.items() if k in ('in_proj_w', 'conv_w', 'conv_b', 'x_proj_w', 'A_logs', 'Ds', 'dt_bias', 'out_norm_g', 'out_norm_b', 'out_proj_w', )}
    del _L1_conv_all

    return {
        "x": x,
        "L0_conv_p_w": _L0_conv_in["p_w"],
        "L0_conv_p_b": _L0_conv_in["p_b"],
        "L0_conv_q_w": _L0_conv_in["q_w"],
        "L0_conv_q_b": _L0_conv_in["q_b"],
        "L0_conv_v_w": _L0_conv_in["v_w"],
        "L0_conv_v_b": _L0_conv_in["v_b"],
        "L0_conv_o_w": _L0_conv_in["o_w"],
        "L0_conv_o_b": _L0_conv_in["o_b"],
        "L0_conv_slope": _L0_conv_in["slope"],
        "L0_conv_t1_w0": _L0_conv_in["t1_w0"],
        "L0_conv_t1_b0": _L0_conv_in["t1_b0"],
        "L0_conv_t1_ws": _L0_conv_in["t1_ws"],
        "L0_conv_t1_bs": _L0_conv_in["t1_bs"],
        "L0_conv_t1_wo": _L0_conv_in["t1_wo"],
        "L0_conv_t1_bo": _L0_conv_in["t1_bo"],
        "L0_conv_t2_w0": _L0_conv_in["t2_w0"],
        "L0_conv_t2_b0": _L0_conv_in["t2_b0"],
        "L0_conv_t2_ws": _L0_conv_in["t2_ws"],
        "L0_conv_t2_bs": _L0_conv_in["t2_bs"],
        "L0_conv_t2_wo": _L0_conv_in["t2_wo"],
        "L0_conv_t2_bo": _L0_conv_in["t2_bo"],
        "L1_conv_in_proj_w": _L1_conv_in["in_proj_w"],
        "L1_conv_conv_w": _L1_conv_in["conv_w"],
        "L1_conv_conv_b": _L1_conv_in["conv_b"],
        "L1_conv_x_proj_w": _L1_conv_in["x_proj_w"],
        "L1_conv_A_logs": _L1_conv_in["A_logs"],
        "L1_conv_Ds": _L1_conv_in["Ds"],
        "L1_conv_dt_bias": _L1_conv_in["dt_bias"],
        "L1_conv_out_norm_g": _L1_conv_in["out_norm_g"],
        "L1_conv_out_norm_b": _L1_conv_in["out_norm_b"],
        "L1_conv_out_proj_w": _L1_conv_in["out_proj_w"],
    }

def reference(x, L0_conv_p_w, L0_conv_p_b, L0_conv_q_w, L0_conv_q_b, L0_conv_v_w, L0_conv_v_b, L0_conv_o_w, L0_conv_o_b, L0_conv_slope, L0_conv_t1_w0, L0_conv_t1_b0, L0_conv_t1_ws, L0_conv_t1_bs, L0_conv_t1_wo, L0_conv_t1_bo, L0_conv_t2_w0, L0_conv_t2_b0, L0_conv_t2_ws, L0_conv_t2_bs, L0_conv_t2_wo, L0_conv_t2_bo, L1_conv_in_proj_w, L1_conv_conv_w, L1_conv_conv_b, L1_conv_x_proj_w, L1_conv_A_logs, L1_conv_Ds, L1_conv_dt_bias, L1_conv_out_norm_g, L1_conv_out_norm_b, L1_conv_out_proj_w):
    import jax
    import jax.numpy as jnp
    def _L0_conv_ref(x, p_w, p_b, q_w, q_b, v_w, v_b, o_w, o_b, slope, t1_w0, t1_b0, t1_ws, t1_bs, t1_wo, t1_bo, t2_w0, t2_b0, t2_ws, t2_bs, t2_wo, t2_bo):
        import jax, jax.numpy as jnp
        import numpy as np
        EMBED = 192
        EXPAND = 3
        D1 = EMBED * EXPAND
        RPE_IN = 32
        LAYERS = 3
        LAMBDA = 0.95

        def _rpe_mlp(t, w0, b0, ws, bs, wo, bo):
            h = t @ w0.T + b0
            for i in range(ws.shape[0]):
                h = jax.nn.relu(h) @ ws[i].T + bs[i]
            return jax.nn.relu(h) @ wo.T + bo

        def _toeplitz(x, a):
            n = x.shape[1]
            m = 2 * n
            xf = jnp.fft.rfft(x, m, axis=1)
            af = jnp.fft.rfft(a, m, axis=0)
            return jnp.fft.irfft(xf * af[None], m, axis=1)[:, :n]

        def _forward(x, p_w, p_b, q_w, q_b, v_w, v_b, o_w, o_b, slope, t1_w0, t1_b0, t1_ws, t1_bs, t1_wo, t1_bo, t2_w0, t2_b0, t2_ws, t2_bs, t2_wo, t2_bo):
            b, h, w, d = x.shape
            n = h
            dt = x.dtype
            pos = jnp.arange(1, n, dtype=dt).reshape(-1, 1)
            zero = jnp.zeros((1, 1), dt)
            rpe_input = jnp.concatenate([zero, pos, zero, -pos], axis=0)
            p = jax.nn.silu(x @ p_w.T + p_b)
            q = jax.nn.silu(x @ q_w.T + q_b)
            v = jax.nn.silu(x @ v_w.T + v_b)
            sl = LAMBDA + (1.0 - LAMBDA) * jnp.clip(slope, 0.0, 1.0)
            idx = jnp.arange(1, n, dtype=dt).reshape(1, -1, 1)
            gamma = sl ** idx
            one = jnp.ones((1, 1, D1), dt)
            decay = jnp.concatenate([one, gamma, one, gamma[:, ::-1]], axis=1)[0]
            a1 = _rpe_mlp(rpe_input, t1_w0, t1_b0, t1_ws, t1_bs, t1_wo, t1_bo) * decay
            a2 = _rpe_mlp(rpe_input, t2_w0, t2_b0, t2_ws, t2_bs, t2_wo, t2_bo) * decay
            qv = q * v
            o1 = _toeplitz(qv.reshape(b * h, w, D1), a1).reshape(b, h, w, D1)
            o2 = _toeplitz(jnp.transpose(qv, (0, 2, 1, 3)).reshape(b * w, h, D1), a2)
            o2 = jnp.transpose(o2.reshape(b, w, h, D1), (0, 2, 1, 3))
            out = p * (o1 + o2)
            return out @ o_w.T + o_b
        return _forward(x, p_w, p_b, q_w, q_b, v_w, v_b, o_w, o_b, slope, t1_w0, t1_b0, t1_ws, t1_bs, t1_wo, t1_bo, t2_w0, t2_b0, t2_ws, t2_bs, t2_wo, t2_bo)

    def _L1_conv_ref(x, in_proj_w, conv_w, conv_b, x_proj_w, A_logs, Ds, dt_bias, out_norm_g, out_norm_b, out_proj_w):
        import jax, jax.numpy as jnp
        import numpy as np
        CHUNK = 64

        def _ssd_chunk_scan(x, dt, A, Bs, Cs, R):
            Bsz, L, Hh, P = x.shape
            K, N = (Bs.shape[2], Bs.shape[3])
            Nc = L // CHUNK
            Bh = jnp.repeat(Bs, R, axis=2)
            Ch = jnp.repeat(Cs, R, axis=2)
            xc = x.reshape(Bsz, Nc, CHUNK, Hh, P)
            dtc = dt.reshape(Bsz, Nc, CHUNK, Hh)
            Bc = Bh.reshape(Bsz, Nc, CHUNK, Hh, N)
            Cc = Ch.reshape(Bsz, Nc, CHUNK, Hh, N)
            dA = jnp.transpose(dtc, (0, 1, 3, 2)) * A[None, None, :, None]
            Acum = jnp.cumsum(dA, axis=-1)
            diff = Acum[..., :, None] - Acum[..., None, :]
            tri = jnp.tril(jnp.ones((CHUNK, CHUNK), bool))
            Lmat = jnp.where(tri, jnp.exp(diff), 0.0)
            xdt = xc * dtc[..., None]
            Y_diag = jnp.einsum('bcqhn,bcshn,bchqs,bcshp->bcqhp', Cc, Bc, Lmat, xdt)
            decay_last = jnp.exp(Acum[..., -1:] - Acum)
            states = jnp.einsum('bcqhn,bchq,bcqhp->bchpn', Bc, decay_last, xdt)
            chunk_decay = jnp.exp(Acum[..., -1])

            def step(S, inp):
                cd, st = inp
                return (cd[..., None, None] * S + st, S)
            S0 = jnp.zeros((Bsz, Hh, P, N), x.dtype)
            _, prev = jax.lax.scan(step, S0, (jnp.moveaxis(chunk_decay, 1, 0), jnp.moveaxis(states, 1, 0)))
            prev = jnp.moveaxis(prev, 0, 1)
            Y_off = jnp.einsum('bcqhn,bchpn,bchq->bcqhp', Cc, prev, jnp.exp(Acum))
            return (Y_diag + Y_off).reshape(Bsz, L, Hh, P)

        def _forward(x, in_proj_w, conv_w, conv_b, x_proj_w, A_logs, Ds, dt_bias, out_norm_g, out_norm_b, out_proj_w):
            B, H, W, Dm = x.shape
            K, R = A_logs.shape
            P = Ds.shape[2]
            d_inner = x_proj_w.shape[2]
            N = (x_proj_w.shape[1] - R) // 2
            L = H * W
            xz = jnp.einsum('bhwc,dc->bhwd', x, in_proj_w)
            xi, z = jnp.split(xz, 2, axis=-1)
            z = jax.nn.gelu(z, approximate=False)
            kern = jnp.transpose(conv_w, (2, 3, 1, 0))
            xi = jax.lax.conv_general_dilated(xi, kern, (1, 1), 'SAME', dimension_numbers=('NHWC', 'HWIO', 'NHWC'), feature_group_count=d_inner) + conv_b
            xi = jax.nn.gelu(xi, approximate=False)
            x0 = xi.reshape(B, L, d_inner)
            x1 = jnp.transpose(xi, (0, 2, 1, 3)).reshape(B, L, d_inner)
            xs = jnp.stack([x0, x1, x0[:, ::-1], x1[:, ::-1]], axis=2)
            x_dbl = jnp.einsum('blkd,kcd->blkc', xs, x_proj_w)
            dts = x_dbl[..., :R].reshape(B, L, K * R)
            Bs = x_dbl[..., R:R + N]
            Cs = x_dbl[..., R + N:]
            xs_h = xs.reshape(B, L, K * R, P)
            A = -jnp.exp(A_logs.astype(jnp.float32)).reshape(K * R)
            Dmat = Ds.astype(jnp.float32).reshape(K * R, P)
            dt = jax.nn.softplus(dts + dt_bias.reshape(K * R))
            ys = _ssd_chunk_scan(xs_h, dt, A, Bs, Cs, R) + xs_h * Dmat
            ys = ys.reshape(B, L, K, d_inner)

            def unT(y):
                return jnp.transpose(y.reshape(B, W, H, d_inner), (0, 2, 1, 3)).reshape(B, L, d_inner)
            y = ys[:, :, 0] + ys[:, ::-1, 2] + unT(ys[:, :, 1]) + unT(ys[:, ::-1, 3])
            y = y.reshape(B, H, W, d_inner)
            mu = y.mean(-1, keepdims=True)
            var = y.var(-1, keepdims=True)
            y = (y - mu) / jnp.sqrt(var + 1e-05) * out_norm_g + out_norm_b
            y = y * z
            return jnp.einsum('bhwd,cd->bhwc', y, out_proj_w)
        return _forward(x, in_proj_w, conv_w, conv_b, x_proj_w, A_logs, Ds, dt_bias, out_norm_g, out_norm_b, out_proj_w)

    def _gn(v, G=32, eps=1e-5):
        B_, H_, W_, C_ = v.shape
        g = v.reshape(B_, H_, W_, G, C_ // G)
        m = jnp.mean(g, axis=(1, 2, 4), keepdims=True)
        s = jnp.var(g, axis=(1, 2, 4), keepdims=True)
        return ((g - m) / jnp.sqrt(s + eps)).reshape(v.shape)

    def _ln_c(v, eps=1e-6):
        m = jnp.mean(v, axis=-1, keepdims=True)
        s = jnp.var(v, axis=-1, keepdims=True)
        return (v - m) / jnp.sqrt(s + eps)

    def _ln_t(v, eps=1e-5):
        m = jnp.mean(v, axis=-1, keepdims=True)
        s = jnp.var(v, axis=-1, keepdims=True)
        return (v - m) / jnp.sqrt(s + eps)

    def _to_tokens(v):
        B_, H_, W_, C_ = v.shape
        return v.reshape(B_, H_ * W_, C_)
    def _from_tokens(t, like):
        return t.reshape(like.shape)

    x = x + _L0_conv_ref(_gn(x), L0_conv_p_w, L0_conv_p_b, L0_conv_q_w, L0_conv_q_b, L0_conv_v_w, L0_conv_v_b, L0_conv_o_w, L0_conv_o_b, L0_conv_slope, L0_conv_t1_w0, L0_conv_t1_b0, L0_conv_t1_ws, L0_conv_t1_bs, L0_conv_t1_wo, L0_conv_t1_bo, L0_conv_t2_w0, L0_conv_t2_b0, L0_conv_t2_ws, L0_conv_t2_bs, L0_conv_t2_wo, L0_conv_t2_bo)
    x = x + _L1_conv_ref(_gn(x), L1_conv_in_proj_w, L1_conv_conv_w, L1_conv_conv_b, L1_conv_x_proj_w, L1_conv_A_logs, L1_conv_Ds, L1_conv_dt_bias, L1_conv_out_norm_g, L1_conv_out_norm_b, L1_conv_out_proj_w)
    return x


_drawn_inputs = setup_inputs


def setup_inputs(seed=0):
    import zlib

    import numpy as np

    out = dict(_drawn_inputs(seed))
    spreads = {'L1_conv_out_norm_g': (1.0, 0.6), 'L1_conv_out_norm_b': (0.0, 0.8)}
    factors = {'L0_conv_p_b': 8.0,
     'L0_conv_q_b': 8.0,
     'L0_conv_v_b': 8.0,
     'L0_conv_slope': 8.0,
     'L0_conv_t1_w0': 3.218,
     'L0_conv_t1_b0': 8.0,
     'L0_conv_t1_bs': 8.0,
     'L0_conv_t1_bo': 6.111,
     'L0_conv_t2_w0': 3.283,
     'L0_conv_t2_b0': 30.976,
     'L0_conv_t2_bs': 8.0,
     'L0_conv_t2_bo': 6.498,
     'L1_conv_x_proj_w': 24.878,
     'L1_conv_A_logs': 22.421,
     'L1_conv_Ds': 46.758,
     'L1_conv_dt_bias': 200.0,
     'L0_conv_o_b': 2.744}
    for name, (base, spread) in spreads.items():
        noise = np.random.default_rng([zlib.crc32(name.encode()), seed]).standard_normal(out[name].shape)
        drawn = base * np.exp(spread * noise) if base else spread * noise
        out[name] = jnp.asarray(drawn.astype(out[name].dtype))
    for name, factor in factors.items():
        out[name] = (out[name] * factor).astype(out[name].dtype)
    return out
```

```python
from contextlib import ExitStack

import numpy as np
import concourse.bass as bass
from concourse import mybir

F32 = mybir.dt.float32
ALU = mybir.AluOpType
ACT = mybir.ActivationFunctionType

PB = 2
SIDE = 56
TOK = PB * SIDE
C = 192
KC = 2
CP = C // KC
D1 = 576
DC = D1 // CP
LAGS = 2 * SIDE - 1
CW = 4
BLK = CW * TOK
NB = SIDE // CW
GC = 8
DI = 384
IK = DI // 128
NDIR = 4
HEADS = 12
HP = DI // HEADS
NS = 64
REC = 2 * NS + 2 * HEADS
GN_EPS = 1e-5
LN_EPS = 1e-5


class Scope:

    def __init__(self, nc, ctx, name):
        self.nc, self.ctx, self.name = nc, ctx, name
        self.sems = []
        ctx.callback(self.clear)

    def clear(self):
        self.nc.clear_and_free_semaphores(self.sems)
        self.nc.all_engine_barrier()

    def sb(self, name, shape):
        return self.ctx.enter_context(self.nc.sbuf_tensor(f"{self.name}_{name}", shape, F32))

    def sb2(self, name, shape, n=2):
        return [self.sb(f"{name}{i}", shape) for i in range(n)]

    def ps(self, name, shape):
        return self.ctx.enter_context(self.nc.psum_tensor(f"{self.name}_{name}", shape, F32))

    def sem(self, name):
        self.sems.append(self.nc.alloc_semaphore(name=f"{self.name}_{name}"))
        return self.sems[-1]

    def sem2(self, name, n=2):
        return [self.sem(f"{name}{i}") for i in range(n)]




def gn_stats(nc, name, src, scale_dram, group_avg, n_pairs):
    with ExitStack() as ctx:
        S = Scope(nc, ctx, name)
        sb, sem = S.sb, S.sem
        x = sb("x", [CP, KC, SIDE, PB, SIDE])
        gavg = sb("gavg", [CP, CP])
        stats = sb("stats", [CP, KC, PB, NB // 2, 6])
        mv = sb("mv", [CP, KC * PB, 2])
        mom = sb("mom", [CP, KC * PB, 2])
        grp = sb("grp", [CP, KC * PB, 2])
        var = sb("var", [CP, KC * PB])
        std = sb("std", [CP, KC * PB])
        sc = sb("sc", [CP, KC * PB, 2])
        grp_ps = ctx.enter_context(nc.psum_tensor(f"{name}_ps", [CP, KC * PB * 2], F32))
        gavg_in, x_in, x_used = sem("gavg_in"), sem("x_in"), sem("x_used")
        passed = sem("passed")
        stat, mom_ready, grp_ready, var_ready, std_ready, sc_ready, sc_out = (
            sem(n) for n in ("stat", "mom", "grpr", "varr", "stdr", "scr", "sco"))
        block = ctx.enter_context(nc.Block())
        HALF = SIDE // 2

        @block.sync
        def _(sp):
            sp.dma_start(gavg[:], group_avg[:]).then_inc(gavg_in, 16)
            with sp.Fori(0, n_pairs) as g:
                sp.wait_ge(x_used, g)
                for kc in range(KC):
                    for half in range(2):
                        sp.dma_start(x[:, kc, half * HALF:(half + 1) * HALF], src[g, kc, :, half * HALF:(half + 1) * HALF]).then_inc(x_in, 16)
                sp.wait_ge(sc_ready, (g + 1) * 2)
                sp.dma_start(scale_dram[g], sc[:]).then_inc(sc_out, 16)
            sp.wait_ge(sc_out, 16 * n_pairs)

        @block.vector
        def _(dve):
            with dve.Fori(0, n_pairs) as g:
                dve.wait_ge(x_in, (g + 1) * 64)
                for kc in range(KC):
                    for b in range(PB):
                        for j in range(7):
                            ins = dve.bn_stats(stats[:, kc, b, j], x[:, kc, j * 8:j * 8 + 8, b])
                ins.then_inc(x_used, 1)
                dve.wait_ge(x_used, g + 1)
                dve.sem_inc(passed, 1)
                for kb in range(KC * PB):
                    ins = dve.bn_aggr(mv[:, kb], stats[:, kb // PB, kb % PB].rearrange("c j s -> c (j s)"))
                ins.then_inc(stat, 1)
                dve.wait_ge(stat, g * 4 + 1)
                dve.tensor_tensor(mom[:, :, 1], mv[:, :, 0], mv[:, :, 0], ALU.mult).then_inc(stat, 1)
                dve.wait_ge(stat, g * 4 + 2)
                dve.tensor_tensor(mom[:, :, 1], mom[:, :, 1], mv[:, :, 1], ALU.add)
                dve.tensor_copy(mom[:, :, 0], mv[:, :, 0]).then_inc(mom_ready, 1)
                dve.wait_ge(grp_ready, g + 1)
                dve.tensor_copy(grp[:].rearrange("c k s -> c (k s)"), grp_ps[:]).then_inc(stat, 1)
                dve.wait_ge(stat, g * 4 + 3)
                dve.tensor_tensor(var[:], grp[:, :, 0], grp[:, :, 0], ALU.mult).then_inc(stat, 1)
                dve.wait_ge(stat, g * 4 + 4)
                dve.scalar_tensor_tensor(out=var[:], in0=grp[:, :, 1], scalar=GN_EPS, in1=var[:], op0=ALU.add, op1=ALU.subtract).then_inc(var_ready, 1)
                dve.wait_ge(std_ready, g + 1)
                dve.wait_ge(sc_out, g * 16)
                dve.reciprocal(sc[:, :, 0], std[:]).then_inc(sc_ready, 1)
                dve.wait_ge(sc_ready, g * 2 + 1)
                dve.scalar_tensor_tensor(out=sc[:, :, 1], in0=grp[:, :, 0], scalar=-1.0, in1=sc[:, :, 0], op0=ALU.mult, op1=ALU.mult).then_inc(sc_ready, 1)

        @block.tensor
        def _(pe):
            pe.wait_ge(gavg_in, 16)
            with pe.Fori(0, n_pairs) as g:
                pe.wait_ge(mom_ready, g + 1)
                pe.matmul(grp_ps[:], gavg[:], mom[:].rearrange("c k s -> c (k s)"), start=True, stop=True).then_inc(grp_ready, 1)

        @block.scalar
        def _(act):
            with act.Fori(0, n_pairs) as g:
                act.wait_ge(var_ready, g + 1)
                act.activation(std[:], var[:], ACT.Sqrt).then_inc(std_ready, 1)


def toeplitz_tables(nc, a, lag_const, a_dram, t_dram):
    with ExitStack() as ctx:
        R = a["t_w0"].shape[0]
        S = Scope(nc, ctx, "tt")
        sb, sem = S.sb, S.sem
        posr = sb("pos", [R, LAGS])
        absl = sb("absl", [CP, LAGS])
        w0 = sb("w0", [R, 2, 2])
        ws = sb("ws", [R, 2, 3, R])
        bs = sb("bs", [R, 2, 3])
        wo = sb("wo", [R, 2, D1])
        bo = sb("bo", [CP, 2, DC])
        slope = sb("slope", [CP, DC])
        hid = sb("hid", [R, 2, 4, LAGS])
        decay = sb("decay", [CP, DC, LAGS])
        tab = sb("tab", [CP, 2, DC, LAGS])
        h_ps = [ctx.enter_context(nc.psum_tensor(f"tt_h{i}", [R, LAGS], F32)) for i in range(2)]
        o_ps = [ctx.enter_context(nc.psum_tensor(f"tt_o{i}", [CP, 4, 128], F32)) for i in range(2)]
        loads, lin, hid_ready, sl_ready, ln_ready, dec_ready, out_ready, tab_ready, tab_out, t_out = (
            sem(n) for n in ("loads", "lin", "hid", "sl", "ln", "dec", "out", "tab", "tabo", "to"))
        block = ctx.enter_context(nc.Block())

        @block.sync
        def _(sp):
            sp.dma_start(posr[:], lag_const[0].partition_broadcast(R)).then_inc(loads, 16)
            sp.dma_start(absl[:], lag_const[1].partition_broadcast(CP)).then_inc(loads, 16)
            sp.dma_start(w0[:], a["t_w0"][:]).then_inc(loads, 16)
            for t in range(2):
                sp.dma_start(ws[:, t], a["t_ws"][t].rearrange("l i o -> i l o")).then_inc(loads, 16)
            sp.dma_start(wo[:], a["t_wo"].rearrange("t r d -> r t d")).then_inc(loads, 16)
            sp.dma_start(bs[:], a["t_bs"][:]).then_inc(loads, 16)
            sp.dma_start(bo[:], a["t_bo"][:]).then_inc(loads, 16)
            sp.dma_start(slope[:], a["slope"][:]).then_inc(loads, 16)
            sp.wait_ge(tab_ready, 2 * DC)
            for t in range(2):
                sp.dma_start(a_dram[t].rearrange("(k c) l -> c k l", c=CP), tab[:, t]).then_inc(tab_out, 16)
            sp.wait_ge(tab_out, 32)
            for t in range(2):
                with sp.Fori(0, SIDE) as row:
                    sp.dma_start(t_dram[t, row], a_dram[t, :, bass.ds(SIDE - 1 - row, SIDE)]).then_inc(t_out, 16)
            sp.wait_ge(t_out, 2 * SIDE * 16)

        n_loads = 16 * 9

        @block.vector
        def _(dve):
            dve.wait_ge(loads, n_loads)
            for t in range(2):
                dve.tensor_scalar(hid[:, t, 0], posr[:], w0[:, t, 0:1], w0[:, t, 1:2], ALU.mult, ALU.add).then_inc(lin, 1)
            dve.wait_ge(lin, 2)
            for t in range(2):
                dve.tensor_scalar(hid[:, t, 0], hid[:, t, 0], 0.0, None, ALU.max).then_inc(hid_ready, 1)
            dve.tensor_scalar(slope[:], slope[:], 0.0, 1.0, ALU.max, ALU.min).then_inc(lin, 1)
            dve.wait_ge(lin, 3)
            dve.tensor_scalar(slope[:], slope[:], 1.0 - 0.95, 0.95, ALU.mult, ALU.add).then_inc(sl_ready, 1)
            for layer in range(3):
                for t in range(2):
                    dve.wait_ge(out_ready, layer * 2 + t + 1)
                    dve.tensor_scalar(hid[:, t, layer + 1], h_ps[t][:], bs[:, t, layer:layer + 1], 0.0, ALU.add, ALU.max).then_inc(hid_ready, 1)
            dve.wait_ge(dec_ready, DC)
            for t in range(2):
                for k in range(DC):
                    dve.wait_ge(out_ready, 6 + t * 2 + k // 3 + 1)
                    dve.scalar_tensor_tensor(out=tab[:, t, k], in0=o_ps[k // 3][:, k % 3, 0:LAGS], scalar=bo[:, t, k:k + 1],
                                             in1=decay[:, k], op0=ALU.add, op1=ALU.mult).then_inc(tab_ready, 1)

        @block.tensor
        def _(pe):
            pe.wait_ge(loads, n_loads)
            for layer in range(3):
                for t in range(2):
                    pe.wait_ge(hid_ready, layer * 2 + t + 1)
                    pe.matmul(h_ps[t][:], ws[:, t, layer], hid[:, t, layer], start=True, stop=True).then_inc(out_ready, 1)
            for t in range(2):
                pe.wait_ge(hid_ready, 6 + t + 1)
                for half in range(2):
                    if t == 1:
                        pe.wait_ge(tab_ready, 3 * (half + 1))
                    for k in range(3 * half, 3 * half + 3):
                        ins = pe.matmul(o_ps[half][:, k % 3, 0:LAGS], wo[:, t, k * CP:(k + 1) * CP], hid[:, t, 3], start=True, stop=True)
                    ins.then_inc(out_ready, 1)

        @block.scalar
        def _(act):
            act.wait_ge(sl_ready, 1)
            act.activation(slope[:], slope[:], ACT.Ln).then_inc(ln_ready, 1)
            act.wait_ge(ln_ready, 1)
            for k in range(DC):
                act.activation(decay[:, k], absl[:], ACT.Exp, scale=slope[:, k:k + 1]).then_inc(dec_ready, 1)


def load_scale(sp, sc, scale_dram, g, sem):
    sp.dma_start(sc[:].rearrange("c k b s -> c (k b) s"), scale_dram[g]).then_inc(sem, 16)


def load_block(sp, dst, src, g, block, sem):
    sp.dma_start(dst[:], src[g, :, :, bass.ds(block * CW, CW)].rearrange("k c w b h -> c k w b h")).then_inc(sem, 16)


def normalise(eng, dst, src, sc):
    for kc in range(KC):
        for b in range(PB):
            ins = eng.tensor_scalar(dst[0:CP, kc, :, b], src[:, kc, :, b], sc[:, kc, b, 0:1], sc[:, kc, b, 1:2], ALU.mult, ALU.add)
    return ins


def mixer_qv(nc, x_dram, scale_dram, wqv_dram, gated_dram, n_pairs):
    with ExitStack() as ctx:
        S = Scope(nc, ctx, "qv")
        passed = S.sem("passed")
        wqv = S.sb("wqv", [CP + 1, KC, 2 * D1])
        sc = S.sb("sc", [CP, KC, PB, 2])
        xs = S.sb2("xs", [CP, KC, CW, PB, SIDE])
        xn = S.sb2("xn", [CP + 1, KC, CW, PB, SIDE])
        qv = S.sb2("qv", [TOK, 2 * D1])
        xo = S.sb2("xo", [TOK, CW, D1])
        NT = 3
        NW = 2 * D1 // NT
        ps = [S.ps(f"ps{i}", [TOK, NT, 512]) for i in range(2)]
        w_in, ones, sc_in = S.sem("w_in"), S.sem("ones"), S.sem("sc_in")
        x_in, normed, silu, gated, block_gated, stored, block_read = (
            S.sem2(n) for n in ("x_in", "normed", "silu", "gated", "bgated", "stored", "bread"))
        proj = S.sem2("proj")
        block = ctx.enter_context(nc.Block())
        NJ = NB // 2

        @block.sync
        def _(sp):
            sp.dma_start(wqv[:], wqv_dram[:]).then_inc(w_in, 16)
            with sp.Fori(0, n_pairs) as g:
                sp.wait_ge(normed[1], g * NJ)
                load_scale(sp, sc, scale_dram, g, sc_in)
                with sp.Fori(0, NJ) as j:
                    i = g * NJ + j
                    for s in range(2):
                        sp.wait_ge(normed[s], i)
                        load_block(sp, xs[s], x_dram, g, j * 2 + s, x_in[s])

        @block.gpsimd
        def _(pool):
            for s in range(2):
                pool.memset(xn[s][:], 1.0).then_inc(ones, 1)
            pool.wait_ge(ones, 2)
            with pool.Fori(0, n_pairs) as g:
                pool.wait_ge(sc_in, (g + 1) * 16)
                pool.sem_inc(passed, 1)
                with pool.Fori(0, NJ) as j:
                    i = g * NJ + j
                    for s in range(2):
                        pool.wait_ge(x_in[s], (i + 1) * 16)
                        pool.wait_ge(block_read[s], i)
                        pool.sem_inc(passed, 1)
                        normalise(pool, xn[s], xs[s], sc).then_inc(normed[s], 1)

        @block.tensor
        def _(pe):
            pe.wait_ge(w_in, 16)
            with pe.Fori(0, n_pairs * NJ) as i:
                for s in range(2):
                    pe.wait_ge(normed[s], i + 1)
                    for w in range(CW):
                        u = (s * CW + w) % 2
                        m = i * CW + (s * CW + w) // 2
                        pe.wait_ge(silu[u], m)
                        for kc in range(KC):
                            p = CP + kc
                            for n in range(NT):
                                ins = pe.matmul(ps[u][:, n, 0:NW], xn[s][0:p, kc, w].rearrange("p b h -> p (b h)"),
                                                wqv[0:p, kc, n * NW:(n + 1) * NW], start=(kc == 0), stop=(kc == KC - 1))
                        ins.then_inc(block_read[s] if w == CW - 1 else proj[s], 1)

        @block.scalar
        def _(act):
            with act.Fori(0, n_pairs * NJ) as i:
                g, j = i // NJ, i % NJ
                for s in range(2):
                    for w in range(CW):
                        u = (s * CW + w) % 2
                        m = i * CW + (s * CW + w) // 2
                        if w == CW - 1:
                            act.wait_ge(block_read[s], i + 1)
                        else:
                            act.wait_ge(proj[s], i * (CW - 1) + w + 1)
                        act.wait_ge(gated[u], m)
                        act.activation(qv[u][:].rearrange("t (n c) -> t n c", n=NT), ps[u][:, :, 0:NW], ACT.Silu).then_inc(silu[u], 1)
                    act.wait_ge(gated[1], i * CW + (s * CW + CW - 1) // 2 + 1)
                    act.wait_ge(gated[0], i * CW + (s * CW + CW - 1) // 2 + 1)
                    act.dma_start(gated_dram[g, :, bass.ds(j * 2 * CW + s * CW, CW)], xo[s][:]).then_inc(stored[s], 16)
            for s in range(2):
                act.wait_ge(stored[s], 16 * n_pairs * NJ)

        @block.vector
        def _(dve):
            with dve.Fori(0, n_pairs * NJ) as i:
                for s in range(2):
                    dve.wait_ge(stored[s], i * 16)
                    for w in range(CW):
                        u = (s * CW + w) % 2
                        m = i * CW + (s * CW + w) // 2
                        dve.wait_ge(silu[u], m + 1)
                        dve.tensor_tensor(xo[s][:, w], qv[u][:, 0:D1], qv[u][:, D1:2 * D1], ALU.mult).then_inc(gated[u], 1)


def mixer_toeplitz(nc, gated_dram, t_dram, ident_dram, mixed_dram, n_pairs):
    with ExitStack() as ctx:
        S = Scope(nc, ctx, "tp")
        passed = S.sem("passed")
        ident = S.sb("ident", [128, 128])
        x = S.sb2("x", [TOK, SIDE, CP])
        o = S.sb2("o", [TOK, SIDE, CP])
        t2 = S.sb2("t2", [TOK, GC, PB, SIDE])
        t1 = S.sb2("t1", [SIDE, GC, SIDE])
        xg = S.sb2("xg", [TOK, GC, SIDE])
        xt = S.sb2("xt", [SIDE, 2, GC // 2, TOK])
        tp = [S.ps(f"tps{i}", [SIDE, 2, 512]) for i in range(2)]
        op = [S.ps(f"ops{i}", [TOK, GC, SIDE]) for i in range(2)]
        id_in, zero = S.sem("id_in"), S.sem("zero")
        x_in, x_used, t_in, staged, turned, xt_ready, summed, o_ready, chunk_out, o_free = (
            S.sem2(n) for n in ("x_in", "x_used", "t_in", "staged", "turned", "xt_ready", "summed", "o_ready", "chunk_out", "o_free"))
        block = ctx.enter_context(nc.Block())
        NCH = n_pairs * DC // 2
        NG = CP // GC // 2

        @block.sync
        def _(sp):
            sp.dma_start(ident[:], ident_dram[:]).then_inc(id_in, 16)
            sp.wait_ge(zero, 2)
            with sp.Fori(0, NCH) as i:
                for s in range(2):
                    with sp.Fori(0, NG) as j:
                        m = (i * 2 + s) * NG + j
                        for q in range(2):
                            sp.wait_ge(summed[q], m)
                            c0 = ((i * 2 + s) % DC) * CP + (j * 2 + q) * GC
                            for b in range(PB):
                                sp.dma_start(t2[q][b * SIDE:(b + 1) * SIDE, :, b], t_dram[1, :, bass.ds(c0, GC)]).then_inc(t_in[q], 16)
                            sp.dma_start(t1[q][:], t_dram[0, :, bass.ds(c0, GC)]).then_inc(t_in[q], 16)

        @block.gpsimd
        def _(pool):
            for q in range(2):
                pool.memset(t2[q][:], 0.0).then_inc(zero, 1)
            with pool.Fori(0, NCH) as i:
                for s in range(2):
                    n = i * 2 + s
                    pool.wait_ge(x_used[s], i)
                    pool.dma_start(x[s][:], gated_dram[n // DC, :, :, bass.ds((n % DC) * CP, CP)]).then_inc(x_in[s], 16)

        @block.vector
        def _(dve):
            with dve.Fori(0, NCH) as i:
                for s in range(2):
                    dve.wait_ge(x_in[s], (i + 1) * 16)
                    dve.wait_ge(chunk_out[s], i * 16)
                    dve.sem_inc(passed, 1)
                    with dve.Fori(0, NG) as j:
                        m = (i * 2 + s) * NG + j
                        for q in range(2):
                            dve.wait_ge(summed[q], m)
                            dve.tensor_copy(xg[q][:], x[s][:, :, bass.ds((j * 2 + q) * GC, GC)].rearrange("t w c -> t c w")).then_inc(staged[q], 1)
                        for q in range(2):
                            dve.wait_ge(summed[q], m + 1)
                            dve.tensor_copy(o[s][:, :, bass.ds((j * 2 + q) * GC, GC)].rearrange("t w c -> t c w"), op[q][:]).then_inc(o_ready[q], 1)
                    dve.wait_ge(staged[0], (i * 2 + s + 1) * NG)
                    dve.wait_ge(staged[1], (i * 2 + s + 1) * NG)
                    dve.sem_inc(x_used[s], 1)

        @block.tensor
        def _(pe):
            pe.wait_ge(id_in, 16)
            with pe.Fori(0, NCH * 2 * NG) as m:
                for q in range(2):
                    pe.wait_ge(staged[q], m + 1)
                    pe.wait_ge(xt_ready[q], m)
                    pe.sem_inc(passed, 1)
                    for c in range(GC):
                        h, r = c // (GC // 2), c % (GC // 2)
                        ins = pe.transpose(tp[q][:, h, r * TOK:(r + 1) * TOK], xg[q][:, c], ident[0:TOK, 0:TOK])
                    ins.then_inc(turned[q], 1)
                for q in range(2):
                    pe.wait_ge(t_in[q], (m + 1) * 48)
                    pe.wait_ge(xt_ready[q], m + 1)
                    pe.wait_ge(o_ready[q], m)
                    for c in range(GC):
                        h, r = c // (GC // 2), c % (GC // 2)
                        pe.matmul(op[q][:, c], t2[q][:, c].rearrange("p b h -> p (b h)"), xg[q][:, c], start=True, stop=False)
                        ins = pe.matmul(op[q][:, c], xt[q][:, h, r], t1[q][:, c], start=False, stop=True)
                    ins.then_inc(summed[q], 1)

        @block.scalar
        def _(act):
            with act.Fori(0, NCH) as i:
                for s in range(2):
                    n = i * 2 + s
                    with act.Fori(0, NG) as j:
                        m = n * NG + j
                        for q in range(2):
                            act.wait_ge(turned[q], m + 1)
                            act.wait_ge(summed[q], m)
                            act.copy(xt[q][:].rearrange("w h r t -> w h (r t)"), tp[q][:, :, 0:GC // 2 * TOK]).then_inc(xt_ready[q], 1)
                    for q in range(2):
                        act.wait_ge(o_ready[q], (n + 1) * NG)
                    act.dma_start(mixed_dram[n // DC, :, :, bass.ds((n % DC) * CP, CP)], o[s][:]).then_inc(chunk_out[s], 16)
            for s in range(2):
                act.wait_ge(chunk_out[s], NCH * 16)


def mixer_out(nc, x_dram, scale_dram, mixed_dram, wp_dram, pb_dram, wo_dram, ob_dram, ident_dram, x2_dram, n_pairs):
    with ExitStack() as ctx:
        S = Scope(nc, ctx, "mo")
        passed = S.sem("passed")
        ident = S.sb("ident", [128, 128])
        wp = S.sb("wp", [CP, KC, D1])
        pb = S.sb("pb", [CP, DC])
        wo = S.sb("wo", [CP, DC, C])
        ob = S.sb("ob", [CP, KC])
        sc = S.sb("sc", [CP, KC, PB, 2])
        xs = S.sb2("xs", [CP, KC, CW, PB, SIDE])
        xn = S.sb2("xn", [CP, KC, CW, PB, SIDE])
        mx = S.sb2("mx", [TOK, CW, D1])
        p = S.sb("p", [CP, DC, BLK])
        gt = S.sb("gt", [CP, DC, BLK])
        y = S.sb2("y", [CP, KC, BLK])
        pp = [S.ps(f"pp{i}", [CP, BLK]) for i in range(2)]
        tp = [S.ps(f"tp{i}", [CP, BLK]) for i in range(2)]
        yp = [S.ps(f"yp{i}", [CP, BLK]) for i in range(KC)]
        w_in, sc_in = S.sem("w_in"), S.sem("sc_in")
        x_in, mx_in, normed, x_free, xn_read, mx_read, stored = (
            S.sem2(n) for n in ("x_in", "mx_in", "normed", "x_free", "xn_read", "mx_read", "stored"))
        p_ps, p_ready, turned, gate, y_ps, y_ready, gt_read = (
            S.sem2(n) for n in ("p_ps", "p_ready", "turned", "gate", "y_ps", "y_ready", "gt_read"))
        block = ctx.enter_context(nc.Block())
        NJ = NB // 2
        half = DC // 2

        @block.sync
        def _(sp):
            for t, d in ((ident, ident_dram), (wp, wp_dram), (pb, pb_dram), (wo, wo_dram), (ob, ob_dram)):
                sp.dma_start(t[:], d[:]).then_inc(w_in, 16)
            with sp.Fori(0, n_pairs) as g:
                sp.wait_ge(normed[1], g * NJ)
                load_scale(sp, sc, scale_dram, g, sc_in)
                with sp.Fori(0, NJ) as j:
                    i = g * NJ + j
                    for s in range(2):
                        sp.wait_ge(x_free[s], i)
                        load_block(sp, xs[s], x_dram, g, j * 2 + s, x_in[s])
                        sp.wait_ge(mx_read[s], i)
                        sp.dma_start(mx[s][:], mixed_dram[g, :, bass.ds((j * 2 + s) * CW, CW)]).then_inc(mx_in[s], 16)

        @block.gpsimd
        def _(pool):
            with pool.Fori(0, n_pairs) as g:
                pool.wait_ge(sc_in, (g + 1) * 16)
                pool.sem_inc(passed, 1)
                with pool.Fori(0, NJ) as j:
                    i = g * NJ + j
                    for s in range(2):
                        pool.wait_ge(x_in[s], (i + 1) * 16)
                        pool.wait_ge(xn_read[s], i)
                        pool.sem_inc(passed, 1)
                        normalise(pool, xn[s], xs[s], sc).then_inc(normed[s], 1)

        @block.tensor
        def _(pe):
            pe.wait_ge(w_in, 80)
            with pe.Fori(0, n_pairs * NJ) as i:
                for s in range(2):
                    n = i * 2 + s
                    pe.wait_ge(normed[s], i + 1)
                    for c in range(DC):
                        q, m = c % 2, n * half + c // 2
                        pe.wait_ge(p_ready[q], m)
                        for kc in range(KC):
                            ins = pe.matmul(pp[q][:], wp[:, kc, c * CP:(c + 1) * CP], xn[s][:, kc].rearrange("p w b h -> p (w b h)"),
                                            start=(kc == 0), stop=(kc == KC - 1))
                        ins.then_inc(p_ps[q], 1)
                    pe.wait_ge(p_ps[1], (n + 1) * half)
                    pe.sem_inc(xn_read[s], 1)
                    pe.wait_ge(mx_in[s], (i + 1) * 16)
                    for c in range(DC):
                        q, m = c % 2, n * half + c // 2
                        pe.wait_ge(gate[q], m)
                        for w in range(CW):
                            ins = pe.transpose(tp[q][:, w * TOK:(w + 1) * TOK], mx[s][:, w, c * CP:(c + 1) * CP], ident[0:TOK, 0:TOK])
                        ins.then_inc(turned[q], 1)
                    pe.wait_ge(turned[1], (n + 1) * half)
                    pe.sem_inc(mx_read[s], 1)
                    for q in range(2):
                        pe.wait_ge(gate[q], (n + 1) * half)
                    for oc in range(KC):
                        pe.wait_ge(y_ready[oc], n)
                        for c in range(DC):
                            ins = pe.matmul(yp[oc][:], wo[:, c, oc * CP:(oc + 1) * CP], gt[:, c], start=(c == 0), stop=(c == DC - 1))
                        ins.then_inc(y_ps[oc], 1)

        @block.scalar
        def _(act):
            act.wait_ge(w_in, 80)
            with act.Fori(0, n_pairs * NJ) as i:
                g, j = i // NJ, i % NJ
                for s in range(2):
                    n = i * 2 + s
                    for c in range(DC):
                        q, m = c % 2, n * half + c // 2
                        act.wait_ge(p_ps[q], m + 1)
                        act.wait_ge(gate[q], n * half)
                        act.activation(p[:, c], pp[q][:], ACT.Silu, bias=pb[:, c:c + 1]).then_inc(p_ready[q], 1)
                    for oc in range(KC):
                        act.wait_ge(y_ready[oc], n + 1)
                    act.dma_start(x2_dram[g, :, :, bass.ds((j * 2 + s) * CW, CW)].rearrange("k c w b h -> c k (w b h)"), y[s][:]).then_inc(stored[s], 16)
            for s in range(2):
                act.wait_ge(stored[s], 16 * n_pairs * NJ)

        @block.vector
        def _(dve):
            dve.wait_ge(w_in, 80)
            with dve.Fori(0, n_pairs * NJ) as i:
                for s in range(2):
                    n = i * 2 + s
                    for oc in range(KC):
                        dve.wait_ge(y_ps[oc], n)
                    for c in range(DC):
                        q, m = c % 2, n * half + c // 2
                        dve.wait_ge(p_ready[q], m + 1)
                        dve.wait_ge(turned[q], m + 1)
                        dve.tensor_tensor(gt[:, c], tp[q][:], p[:, c], ALU.mult).then_inc(gate[q], 1)
                    dve.wait_ge(stored[s], i * 16)
                    for oc in range(KC):
                        dve.wait_ge(y_ps[oc], n + 1)
                        dve.scalar_tensor_tensor(out=y[s][:, oc], in0=yp[oc][:], scalar=ob[:, oc:oc + 1], in1=xs[s][:, oc].rearrange("p w b h -> p (w b h)"),
                                                 op0=ALU.add, op1=ALU.add).then_inc(y_ready[oc], 1)
                    dve.wait_ge(y_ready[1], n + 1)
                    dve.wait_ge(normed[s], i + 1)
                    dve.sem_inc(x_free[s], 1)


def scan_inputs(nc, x_dram, scale_dram, a, z_dram, u_dram, bc_dram, n_pairs):
    with ExitStack() as ctx:
        S = Scope(nc, ctx, "si")
        passed = S.sem("passed")
        N4 = NDIR * HEADS
        ROW = SIDE + 2
        ident = S.sb("ident", [128, 128])
        w_in = S.sb("w_in", [CP, KC, 2 * DI])
        cw = S.sb("cw", [128, IK, 3, 3])
        taps = S.sb("taps", [128, IK, 9, 128])
        cb = S.sb("cb", [128, IK])
        wx = S.sb("wx", [128, IK, NDIR * 2 * NS + N4])
        dtb = S.sb("dtb", [TOK, N4])
        aneg = S.sb("aneg", [TOK, N4])
        sc = S.sb("sc", [CP, KC, PB, 2])
        xs = S.sb2("xs", [CP, KC, CW, PB, SIDE])
        xn = S.sb2("xn", [CP, KC, CW, PB, SIDE])
        z = S.sb("z", [128, IK, BLK])
        xi = S.sb("xi", [128, IK, ROW, PB, ROW])
        u = S.sb2("u", [128, IK, BLK])
        ut = S.sb2("ut", [TOK, CW, DI + 2 * N4])
        raw = S.sb2("raw", [TOK, CW, N4])
        bc = S.sb2("bc", [TOK, CW, NDIR * 2 * NS])
        sp_ = {n: S.sb("sp_" + n, [TOK, CW, N4]) for n in ("t", "neg", "e", "ln", "ser", "small")}
        bank = [S.ps(f"bank{i}", [128, 512]) for i in range(8)]
        CONV = bank[0:IK]
        w_loaded, consts, sc_in, built = S.sem("w_loaded"), S.sem("consts"), S.sem("sc_in"), S.sem("built")
        x_in, normed, xn_read = S.sem2("x_in"), S.sem2("normed"), S.sem2("xn_read")
        z_ps, z_done, xi_ps, xi_done = (S.sem2(n, IK) for n in ("z_ps", "z_done", "xi_ps", "xi_done"))
        z_out = S.sem("z_out")
        c_ps, c_done = S.sem2("c_ps", IK), S.sem2("c_done", IK)
        bc_ps, t_ps, bc_done, t_done = (S.sem2(n) for n in ("bc_ps", "t_ps", "bc_done", "t_done"))
        ut_out, bc_out = S.sem2("ut_out"), S.sem2("bc_out")
        link, neg_ready, e_ready, ln_ready, raw_ready, dt_done = (S.sem(n) for n in ("link", "neg_ready", "e_ready", "ln_ready", "raw_ready", "dt_done"))
        block = ctx.enter_context(nc.Block())
        NJ = NB // 2
        n_w = 16 * 7

        @block.sync
        def _(sp):
            for t, d in ((ident, a["ident"]), (w_in, a["w_in"]), (cw, a["cw"]), (cb, a["cb"]), (wx, a["wx"])):
                sp.dma_start(t[:], d[:]).then_inc(w_loaded, 16)
            sp.dma_start(dtb[:], a["dtb"][0].partition_broadcast(TOK)).then_inc(w_loaded, 16)
            sp.dma_start(aneg[:], a["alog"][0].partition_broadcast(TOK)).then_inc(w_loaded, 16)
            with sp.Fori(0, n_pairs) as g:
                sp.wait_ge(normed[1], g * NJ)
                load_scale(sp, sc, scale_dram, g, sc_in)
                with sp.Fori(0, NJ) as j:
                    i = g * NJ + j
                    for s in range(2):
                        sp.wait_ge(normed[s], i)
                        load_block(sp, xs[s], x_dram, g, j * 2 + s, x_in[s])
                with sp.Fori(0, NJ) as j:
                    i = g * NJ + j
                    for s in range(2):
                        cols = bass.ds((j * 2 + s) * CW, CW)
                        for q in range(2):
                            sp.wait_ge(bc_done[q], (i * 2 + s + 1) * 2)
                        sp.dma_start(bc_dram[g, cols].rearrange("w p c -> p w c"), bc[s][:]).then_inc(bc_out[s], 16)
                        for q in range(2):
                            sp.wait_ge(t_done[q], (i * 2 + s + 1) * 2)
                        sp.wait_ge(dt_done, i * 2 + s + 1)
                        sp.dma_start(u_dram[g, cols].rearrange("w p c -> p w c"), ut[s][:]).then_inc(ut_out[s], 16)
            sp.wait_ge(z_out, 16 * n_pairs * NB)
            for s in range(2):
                sp.wait_ge(bc_out[s], 16 * n_pairs * NJ)
                sp.wait_ge(ut_out[s], 16 * n_pairs * NJ)

        @block.gpsimd
        def _(pool):
            pool.memset(xi[:].rearrange("p k w b h -> p (k w b h)"), 0.0).then_inc(consts, 1)
            with pool.Fori(0, n_pairs) as g:
                pool.wait_ge(sc_in, (g + 1) * 16)
                pool.sem_inc(passed, 1)
                with pool.Fori(0, NJ) as j:
                    i = g * NJ + j
                    for s in range(2):
                        pool.wait_ge(x_in[s], (i + 1) * 16)
                        pool.wait_ge(xn_read[s], i)
                        pool.sem_inc(passed, 1)
                        normalise(pool, xn[s], xs[s], sc).then_inc(normed[s], 1)

        @block.tensor
        def _(pe):
            pe.wait_ge(w_loaded, n_w)
            pe.wait_ge(consts, 1)
            pe.wait_ge(built, 2)
            with pe.Fori(0, n_pairs) as g:
                with pe.Fori(0, NJ) as j:
                    i = g * NJ + j
                    for s in range(2):
                        n = i * 2 + s
                        pe.wait_ge(normed[s], i + 1)
                        rhs = lambda kc: xn[s][:, kc].rearrange("p w b h -> p (w b h)")
                        if s == 0:
                            for k in range(IK):
                                pe.wait_ge(c_done[k], g * NB)
                        for out, ps, done, off in ((CONV, xi_ps, xi_done, 0), (bank[3:6], z_ps, z_done, DI)):
                            if out is not CONV and s == 0:
                                for q in range(2):
                                    pe.wait_ge(bc_done[q], g * NB * 2)
                                    pe.wait_ge(t_done[q], g * NB * 2)
                            for k in range(IK):
                                pe.wait_ge(done[k], n)
                                for kc in range(KC):
                                    ins = pe.matmul(out[k][:, 0:BLK], w_in[:, kc, off + k * 128:off + (k + 1) * 128], rhs(kc), start=(kc == 0), stop=(kc == KC - 1))
                                ins.then_inc(ps[k], 1)
                        pe.wait_ge(z_ps[IK - 1], n + 1)
                        pe.sem_inc(xn_read[s], 1)
                for k in range(IK):
                    pe.wait_ge(xi_done[k], (g + 1) * NB)
                    pe.wait_ge(z_done[k], (g + 1) * NB)
                pe.sem_inc(passed, 1)
                with pe.Fori(0, NJ) as j:
                    i = g * NJ + j
                    for s in range(2):
                        n = i * 2 + s
                        w0 = (j * 2 + s) * CW
                        for k in range(IK):
                            pe.wait_ge(c_done[k], n)
                            for tap in range(9):
                                dh, dw = tap // 3, tap % 3
                                ins = pe.matmul(CONV[k][:, 0:BLK].rearrange("p (w b h) -> p (w b) h", w=CW, b=PB), taps[:, k, tap],
                                                xi[:, k, bass.ds(w0 + dw, CW), :, dh:dh + SIDE].rearrange("p w b h -> p (w b) h"),
                                                start=(tap == 0), stop=(tap == 8))
                            ins.then_inc(c_ps[k], 1)
                    for s in range(2):
                        n = i * 2 + s
                        for k in range(IK):
                            pe.wait_ge(c_done[k], n + 1)
                        for w in range(CW):
                            q, m = w % 2, n * 2 + w // 2
                            pe.wait_ge(bc_done[q], m)
                            tok = lambda k: u[s][:, k, w * TOK:(w + 1) * TOK]
                            for k in range(IK):
                                ins = pe.matmul(bank[4 + 2 * q][0:TOK, 0:512], tok(k), wx[:, k, 0:512], start=(k == 0), stop=(k == IK - 1))
                            ins.then_inc(bc_ps[q], 1)
                            pe.wait_ge(t_done[q], m)
                            for k in range(IK):
                                pe.matmul(bank[5 + 2 * q][0:TOK, DI:DI + N4], tok(k), wx[:, k, 512:512 + N4], start=(k == 0), stop=(k == IK - 1))
                            for k in range(IK):
                                ins = pe.transpose(bank[5 + 2 * q][0:TOK, k * 128:(k + 1) * 128], tok(k), ident[:])
                            ins.then_inc(t_ps[q], 1)

        @block.scalar
        def _(act):
            act.wait_ge(w_loaded, n_w)
            act.activation(aneg[:], aneg[:], ACT.Exp).then_inc(built, 1)
            with act.Fori(0, n_pairs) as g:
                with act.Fori(0, NJ) as j:
                    i = g * NJ + j
                    for s in range(2):
                        n = i * 2 + s
                        act.wait_ge(z_out, n * 16)
                        for k in range(IK):
                            act.wait_ge(z_ps[k], n + 1)
                            act.activation(z[:, k], bank[3 + k][:, 0:BLK], ACT.Gelu).then_inc(z_done[k], 1)
                        for k in range(IK):
                            act.wait_ge(z_done[k], n + 1)
                        act.dma_start(z_dram[g, :, :, bass.ds((j * 2 + s) * CW, CW)].rearrange("k c w b h -> c k (w b h)"), z[:]).then_inc(z_out, 16)
                with act.Fori(0, NJ) as j:
                    i = g * NJ + j
                    for s in range(2):
                        n = i * 2 + s
                        for k in range(IK):
                            act.wait_ge(c_ps[k], n + 1)
                            for q in range(2):
                                act.wait_ge(t_ps[q], i * 4)
                            act.activation(u[s][:, k], CONV[k][:, 0:BLK], ACT.Gelu, bias=cb[:, k:k + 1]).then_inc(c_done[k], 1)
                    for s in range(2):
                        n = i * 2 + s
                        act.wait_ge(ut_out[s], i * 16)
                        for w in range(CW):
                            q, m = w % 2, n * 2 + w // 2
                            act.wait_ge(t_ps[q], m + 1)
                            act.copy(ut[s][:, w, 0:DI + N4], bank[5 + 2 * q][0:TOK, 0:DI + N4]).then_inc(t_done[q], 1)
                        act.wait_ge(neg_ready, n + 1)
                        act.activation(sp_["e"][:], sp_["neg"][:], ACT.Exp).then_inc(e_ready, 1)
                        act.wait_ge(e_ready, n + 1)
                        act.activation(sp_["ln"][:], sp_["e"][:], ACT.Ln, bias=1.0).then_inc(ln_ready, 1)

        @block.vector
        def _(dve):
            dve.wait_ge(w_loaded, n_w)
            for k in range(IK):
                for tap in range(9):
                    ins = dve.tensor_scalar(taps[:, k, tap], ident[:], cw[:, k, tap // 3, tap % 3:tap % 3 + 1], None, ALU.mult)
            dve.wait_ge(built, 1)
            dve.tensor_scalar(aneg[:], aneg[:], -1.0, None, ALU.mult).then_inc(built, 1)
            dve.wait_ge(built, 2)
            dve.wait_ge(consts, 1)
            with dve.Fori(0, n_pairs) as g:
                with dve.Fori(0, NJ) as j:
                    i = g * NJ + j
                    for s in range(2):
                        n = i * 2 + s
                        if s == 0:
                            for k in range(IK):
                                dve.wait_ge(c_ps[k], g * NB)
                        for k in range(IK):
                            dve.wait_ge(xi_ps[k], n + 1)
                            dve.tensor_copy(xi[:, k, bass.ds((j * 2 + s) * CW + 1, CW), :, 1:1 + SIDE].rearrange("p w b h -> p (w b) h"),
                                            CONV[k][:, 0:BLK].rearrange("p (w b h) -> p (w b) h", w=CW, b=PB)).then_inc(xi_done[k], 1)
                with dve.Fori(0, NJ) as j:
                    i = g * NJ + j
                    for s in range(2):
                        n = i * 2 + s
                        dve.wait_ge(bc_out[s], i * 16)
                        for w in range(CW):
                            q, m = w % 2, n * 2 + w // 2
                            dve.wait_ge(bc_ps[q], m + 1)
                            dve.tensor_copy(bc[s][:, w], bank[4 + 2 * q][0:TOK, 0:512]).then_inc(bc_done[q], 1)
                        L = 11
                        base = n * L
                        step = [0]

                        def chain(ins):
                            step[0] += 1
                            ins.then_inc(link, 1)
                            dve.wait_ge(link, base + step[0])

                        t, neg, e, ln, ser, small = (sp_[k] for k in ("t", "neg", "e", "ln", "ser", "small"))
                        for q in range(2):
                            dve.wait_ge(t_done[q], (n + 1) * 2)
                        chain(dve.tensor_tensor(t[:], ut[s][:, :, DI:DI + N4], dtb[:].unsqueeze(1).to_broadcast([TOK, CW, N4]), ALU.add))
                        chain(dve.tensor_scalar(neg[:], t[:], -1.0, None, ALU.mult))
                        dve.tensor_tensor(neg[:], neg[:], t[:], ALU.min).then_inc(neg_ready, 1)
                        dve.wait_ge(e_ready, n + 1)
                        chain(dve.tensor_scalar(ser[:], e[:], -1.0 / 6.0, None, ALU.mult))
                        for c in (1.0 / 5.0, -1.0 / 4.0, 1.0 / 3.0, -1.0 / 2.0, 1.0):
                            chain(dve.scalar_tensor_tensor(out=ser[:], in0=ser[:], scalar=c, in1=e[:], op0=ALU.add, op1=ALU.mult))
                        dve.wait_ge(ln_ready, n + 1)
                        dve.tensor_scalar(small[:], e[:], 0.1, None, ALU.is_lt)
                        chain(dve.tensor_tensor(ser[:], ser[:], ln[:], ALU.subtract))
                        chain(dve.tensor_tensor(ser[:], ser[:], small[:], ALU.mult))
                        chain(dve.tensor_tensor(ser[:], ser[:], ln[:], ALU.add))
                        assert step[0] == L
                        rows = ut[s][:, :, DI:DI + 2 * N4].rearrange("p w (k t h) -> p w k t h", k=NDIR, t=2)
                        for w in range(CW):
                            dve.scalar_tensor_tensor(out=raw[s][:, w], in0=t[:, w], scalar=0.0, in1=ser[:, w], op0=ALU.max, op1=ALU.add).then_inc(raw_ready, 1)
                        dve.wait_ge(raw_ready, (n + 1) * CW)
                        for w in range(CW):
                            dtw = raw[s][:, w].rearrange("p (k h) -> p k h", k=NDIR)
                            dve.tensor_copy(rows[:, w, :, 0], dtw)
                            ins = dve.tensor_tensor(rows[:, w, :, 1], dtw, aneg[:].rearrange("p (k h) -> p k h", k=NDIR), ALU.mult)
                        ins.then_inc(dt_done, 1)


def scans(nc, a, u_dram, bc_dram, y_drams, n_pairs):
    with ExitStack() as ctx:
        S = Scope(nc, ctx, "sc")
        passed = S.sem("passed")
        UC = DI + NDIR * 2 * HEADS
        ident = S.sb("ident", [128, 128])
        later = S.sb2("later", [128, 128])
        upto = S.sb2("upto", [128, 128])
        seen = S.sb2("seen", [128, SIDE])
        same = S.sb("same", [128, 128])
        u = S.sb2("u", [128, UC], NDIR)
        bz = S.sb2("bz", [128, 2, PB, NS], NDIR)
        state = S.sb2("state", [128, DI], NDIR)
        w = S.sb2("w", [128, HEADS, SIDE])
        xdt = S.sb2("xdt", [128, DI])
        xdd = S.sb2("xdd", [128, DI])
        e = S.sb2("e", [128, HEADS, SIDE])
        m_ = S.sb2("m", [128, HEADS, SIDE])
        bct = S.sb2("bct", [128, 2, 128])
        ctc = S.sb2("ctc", [128, SIDE])
        ecum = S.sb2("ecum", [128, 2 * HEADS])
        gm = S.sb2("gm", [128, SIDE])
        toff = S.sb2("toff", [128, DI])
        y = S.sb2("y", [128, DI])
        diff_ps = [S.ps(f"diff{i}", [128, 2, 512]) for i in range(2)]
        misc_ps = S.ps("misc", [128, 512])
        off_ps, st_ps, yd_ps = S.ps("off", [128, 512]), S.ps("st", [128, 512]), S.ps("yd", [128, 512])
        c_in, zero, s_init, yd_clear = S.sem("c_in"), S.sem("zero"), S.sem("s_init"), S.sem("yd_clear")
        loaded, st_ready, s_ready = (S.sem2(n, NDIR) for n in ("loaded", "st_ready", "s_ready"))
        w_ready, xdt_ready, tr, diff_ready, e_ready, xdd_ready, m_ready = (
            S.sem2(n) for n in ("w_ready", "xdt_ready", "tr", "diff_ready", "e_ready", "xdd_ready", "m_ready"))
        off_ready, toff_ready, scd_ready, yd_ready, y_ready, stored = (
            S.sem2(n) for n in ("off_ready", "toff_ready", "scd_ready", "yd_ready", "y_ready", "stored"))
        bct_ready, ecum_ready, ctc_ready, g_ready, gm_ready = (
            S.sem(n) for n in ("bct_ready", "ecum_ready", "ctc_ready", "g_ready", "gm_ready"))
        block = ctx.enter_context(nc.Block())
        STEPS = SIDE
        heads = lambda t: t.rearrange("p (h c) -> p h c", h=HEADS)
        per_head = lambda t, n: t.unsqueeze(2).to_broadcast([128, HEADS, n])
        dt_of = lambda k: u[k][:, DI + k * 2 * HEADS:DI + k * 2 * HEADS + HEADS]
        da_of = lambda k: u[k][:, DI + k * 2 * HEADS + HEADS:DI + (k + 1) * 2 * HEADS]
        back = lambda k: k // 2

        def chunk(ten, g, k, c, b):
            at = (STEPS - 1) - c if back(k) else c
            if k % 2:
                return ten[g, at, b * SIDE:(b + 1) * SIDE]
            return ten[g, :, b * SIDE + at]

        def slot(t, k):
            return k % 2, t * 2 + k // 2

        def before(t, k):
            return (1 - k % 2, t * 2 + k // 2 + (k % 2))

        def run(eng, first, second, start=None):
            with eng.Fori(0, n_pairs) as g:
                if start:
                    start(g)
                first(g, 0, 0)
                with eng.Fori(0, STEPS - 1) as c:
                    for k in range(NDIR):
                        first(g, c + (k + 1) // NDIR, (k + 1) % NDIR)
                        second(g, c, k)
                for k in range(NDIR):
                    if k + 1 < NDIR:
                        first(g, STEPS - 1, k + 1)
                    second(g, STEPS - 1, k)

        @block.sync
        def _(sp):
            for t, d in ((ident, a["ident"][:]), (later[0], a["later"][0]), (later[1], a["later"][1]), (upto[0], a["upto"][0]),
                         (upto[1], a["upto"][1]), (seen[0], a["seen"][0]), (seen[1], a["seen"][1]), (same, a["same"][:])):
                sp.dma_start(t[:], d).then_inc(c_in, 16)
            sp.wait_ge(zero, 2 * NDIR)

            def load(g, c, k):
                t = g * STEPS + c
                sp.wait_ge(st_ready[k], t)
                sp.sem_inc(passed, 1)
                for b in range(PB):
                    rows = slice(b * 64, b * 64 + SIDE)
                    sp.dma_start(u[k][rows], chunk(u_dram, g, k, c, b)).then_inc(loaded[k], 16)
                    sp.dma_start(bz[k][rows, :, b], chunk(bc_dram, g, k, c, b)[:, k * 2 * NS:(k + 1) * 2 * NS].rearrange("p (s n) -> p s n", s=2)).then_inc(loaded[k], 16)

            def store(g, c, k):
                p, m = slot(g * STEPS + c, k)
                sp.wait_ge(y_ready[p], m + 1)
                sp.sem_inc(passed, 1)
                for b in range(PB):
                    sp.dma_start(chunk(y_drams[k], g, k, c, b), y[p][b * 64:b * 64 + SIDE]).then_inc(stored[p], 16)

            with sp.Fori(0, n_pairs) as g:
                for k in range(NDIR):
                    load(g, 0, k)
                with sp.Fori(0, STEPS - 1) as c:
                    for k in range(NDIR):
                        store(g, c, k)
                        load(g, c + 1, k)
                for k in range(NDIR):
                    store(g, STEPS - 1, k)
            for p in range(2):
                sp.wait_ge(stored[p], n_pairs * STEPS * 2 * 32)

        @block.gpsimd
        def _(pool):
            for k in range(NDIR):
                pool.memset(u[k][:], 0.0).then_inc(zero, 1)
                pool.memset(bz[k][:], 0.0).then_inc(zero, 1)
            pool.wait_ge(c_in, 16 * 8)

            def start(g):
                for k in range(NDIR):
                    pool.wait_ge(s_ready[k], g * STEPS)
                pool.sem_inc(passed, 1)
                for k in range(NDIR):
                    pool.memset(state[k][:], 0.0).then_inc(s_init, 1)

            def first(g, c, k):
                t = g * STEPS + c
                p, m = slot(t, k)
                pool.wait_ge(loaded[k], (t + 1) * 64)
                pool.wait_ge(diff_ready[p], m)
                pool.tensor_tensor(w[p][:], per_head(da_of(k), SIDE), seen[back(k)][:].unsqueeze(1).to_broadcast([128, HEADS, SIDE]), ALU.mult).then_inc(w_ready[p], 1)
                pool.wait_ge(yd_ready[p], m)
                pool.tensor_tensor(heads(xdt[p][:]), heads(u[k][:, 0:DI]), per_head(dt_of(k), HP), ALU.mult).then_inc(xdt_ready[p], 1)

            def second(g, c, k):
                t = g * STEPS + c
                p, m = slot(t, k)
                pool.wait_ge(s_init, (g + 1) * NDIR)
                pool.wait_ge(s_ready[k], t)
                pool.wait_ge(ecum_ready, t * NDIR + k + 1)
                pool.wait_ge(off_ready[p], m + 1)
                pool.tensor_tensor(heads(state[k][:]), heads(state[k][:]), per_head(ecum[p][:, HEADS:], HP), ALU.mult).then_inc(scd_ready[p], 1)

            run(pool, first, second, start)

        @block.tensor
        def _(pe):
            pe.wait_ge(c_in, 16 * 8)
            pe.wait_ge(yd_clear, 1)

            def first(g, c, k):
                t = g * STEPS + c
                n = t * NDIR + k
                p, m = slot(t, k)
                pe.wait_ge(loaded[k], (t + 1) * 64)
                pe.wait_ge(gm_ready, n)
                pe.transpose(misc_ps[:, 0:128], bz[k][:, 0].rearrange("p b n -> p (b n)"), ident[:])
                pe.transpose(misc_ps[:, 128:256], bz[k][:, 1].rearrange("p b n -> p (b n)"), ident[:])
                pe.matmul(misc_ps[:, 256:256 + HEADS], upto[back(k)][:], da_of(k), start=True, stop=True)
                pe.matmul(misc_ps[:, 256 + HEADS:256 + 2 * HEADS], same[:], da_of(k), start=True, stop=True).then_inc(tr[p], 1)
                pe.wait_ge(w_ready[p], m + 1)
                pe.wait_ge(e_ready[p], m)
                for half in range(2):
                    ins = pe.matmul(diff_ps[p][:, half, 0:HEADS // 2 * SIDE], later[back(k)][:],
                                    w[p][:, half * HEADS // 2:(half + 1) * HEADS // 2].rearrange("p h q -> p (h q)"), start=True, stop=True)
                ins.then_inc(diff_ready[p], 1)
                pe.wait_ge(bct_ready, n + 1)
                pe.wait_ge(ecum_ready, n + 1)
                pe.wait_ge(ctc_ready, n + 1)
                pe.matmul(misc_ps[:, 288:288 + SIDE], bct[p][:, 0], ctc[p][:], start=True, stop=True).then_inc(g_ready, 1)

            def second(g, c, k):
                t = g * STEPS + c
                p, m = slot(t, k)
                q, mq = before(t, k)
                pe.wait_ge(s_init, (g + 1) * NDIR)
                pe.wait_ge(s_ready[k], t)
                pe.wait_ge(toff_ready[q], mq)
                pe.matmul(off_ps[:, 0:DI], bct[p][:, 1], state[k][:], start=True, stop=True).then_inc(off_ready[p], 1)
                pe.wait_ge(xdd_ready[p], m + 1)
                pe.wait_ge(s_ready[(k - 1) % NDIR], t + (1 if k else 0))
                pe.matmul(st_ps[:, 0:DI], bz[k][:, 0].rearrange("p b n -> p (b n)"), xdd[p][:], start=True, stop=True).then_inc(st_ready[k], 1)
                pe.wait_ge(xdt_ready[p], m + 1)
                pe.wait_ge(m_ready[p], m + 1)
                pe.wait_ge(y_ready[q], mq)
                pe.sem_inc(passed, 1)
                for h in range(HEADS):
                    for b in range(PB):
                        rows = slice(b * 64, b * 64 + SIDE)
                        ins = pe.matmul(yd_ps[rows, h * HP:(h + 1) * HP], m_[p][rows, h], xdt[p][rows, h * HP:(h + 1) * HP], start=True, stop=True)
                ins.then_inc(yd_ready[p], 1)

            run(pe, first, second)

        @block.scalar
        def _(act):
            def first(g, c, k):
                t = g * STEPS + c
                n = t * NDIR + k
                p, m = slot(t, k)
                act.wait_ge(tr[p], m + 1)
                act.wait_ge(off_ready[p], m)
                act.copy(bct[p][:].rearrange("p s n -> p (s n)"), misc_ps[:, 0:256]).then_inc(bct_ready, 1)
                act.wait_ge(toff_ready[p], m)
                act.wait_ge(scd_ready[p], m)
                act.activation(ecum[p][:], misc_ps[:, 256:256 + 2 * HEADS], ACT.Exp).then_inc(ecum_ready, 1)
                act.wait_ge(diff_ready[p], m + 1)
                act.wait_ge(m_ready[p], m)
                act.wait_ge(xdd_ready[p], m)
                act.activation(e[p][:].rearrange("p (t h) q -> p t (h q)", t=2), diff_ps[p][:, :, 0:HEADS // 2 * SIDE], ACT.Exp).then_inc(e_ready[p], 1)

            run(act, first, lambda g, c, k: None)

        @block.vector
        def _(dve):
            dve.memset(yd_ps[:], 0.0).then_inc(yd_clear, 1)
            dve.wait_ge(c_in, 16 * 8)

            def first(g, c, k):
                t = g * STEPS + c
                n = t * NDIR + k
                p, m = slot(t, k)
                dve.wait_ge(bct_ready, n + 1)
                dve.tensor_copy(ctc[p][0:64], bct[p][0:64, 1, 0:SIDE])
                dve.tensor_copy(ctc[p][64:128], bct[p][64:128, 1, 64:64 + SIDE]).then_inc(ctc_ready, 1)
                dve.wait_ge(g_ready, n + 1)
                dve.tensor_tensor(gm[p][:], misc_ps[:, 288:288 + SIDE], seen[back(k)][:], ALU.mult).then_inc(gm_ready, 1)
                dve.wait_ge(e_ready[p], m + 1)
                dve.wait_ge(xdt_ready[p], m + 1)
                last = 0 if back(k) else SIDE - 1
                dve.tensor_tensor(heads(xdd[p][:]), heads(xdt[p][:]), per_head(e[p][:, :, last], HP), ALU.mult).then_inc(xdd_ready[p], 1)
                dve.wait_ge(gm_ready, n + 1)
                dve.tensor_tensor(m_[p][:], e[p][:], gm[p][:].unsqueeze(1).to_broadcast([128, HEADS, SIDE]), ALU.mult).then_inc(m_ready[p], 1)

            def second(g, c, k):
                t = g * STEPS + c
                p, m = slot(t, k)
                dve.wait_ge(off_ready[p], m + 1)
                dve.wait_ge(ecum_ready, t * NDIR + k + 1)
                dve.tensor_tensor(heads(toff[p][:]), heads(off_ps[:, 0:DI]), per_head(ecum[p][:, 0:HEADS], HP), ALU.mult).then_inc(toff_ready[p], 1)
                dve.wait_ge(scd_ready[p], m + 1)
                dve.wait_ge(st_ready[k], t + 1)
                dve.tensor_tensor(state[k][:], st_ps[:, 0:DI], state[k][:], ALU.add).then_inc(s_ready[k], 1)
                dve.wait_ge(yd_ready[p], m + 1)
                dve.wait_ge(toff_ready[p], m + 1)
                dve.wait_ge(stored[p], m * 32)
                dve.tensor_tensor(y[p][:], yd_ps[:, 0:DI], toff[p][:], ALU.add).then_inc(y_ready[p], 1)

            run(dve, first, second)


def scan_out(nc, a, x_dram, z_dram, u_dram, y_drams, out, n_pairs):
    with ExitStack() as ctx:
        S = Scope(nc, ctx, "so")
        passed = S.sem("passed")
        UC = DI + NDIR * 2 * HEADS
        ident = S.sb("ident", [128, 128])
        dsk = S.sb("dsk", [TOK, NDIR, DI])
        ng, nb = S.sb("ng", [128, IK]), S.sb("nb", [128, IK])
        wo = S.sb("wo", [128, IK, C])
        eps = S.sb("eps", [TOK, 1])
        u = S.sb2("u", [TOK, CW, DI])
        ys = [S.sb2(f"y{s}", [TOK, CW, DI], NDIR) for s in range(1)]
        ys.append(ys[0])
        skip = S.sb("skip", [TOK, CW, DI])
        acc = S.sb("acc", [TOK, CW, DI])
        nrm = S.sb2("nrm", [TOK, CW, DI])
        stats = S.sb("stats", [TOK, CW, 6])
        mv = S.sb("mv", [TOK, CW, 2])
        std = S.sb("std", [TOK, CW])
        rstd = S.sb("rstd", [TOK, CW])
        z = S.sb2("z", [128, IK, BLK])
        x = S.sb2("x", [CP, KC, BLK])
        g_ = S.sb("g", [128, IK, BLK])
        o = S.sb2("o", [CP, KC, BLK])
        t_ps = [[S.ps(f"tps{s}{k}", [128, BLK]) for k in range(IK)] for s in range(2)]
        o_ps = [S.ps(f"ops{k}", [CP, BLK]) for k in range(KC)]
        c_in, built, eps_ready = S.sem("c_in"), S.sem("built"), S.sem("eps_ready")
        in_, xz_in, stored = (S.sem2(n) for n in ("in", "xz_in", "stored"))
        half_sum, sum_all, pl, link, mv_ready, std_ready, nrm_ready = (S.sem(n) for n in ("half", "sum_all", "pl", "link", "mvr", "stdr", "nrmr"))
        turned_s = S.sem2("turned")
        aff_ready, g_ready = S.sem2("aff", IK), S.sem2("g_ready", IK)
        o_psr, o_ready, xz_free = S.sem2("o_psr", KC), S.sem2("o_ready", KC), S.sem2("xz_free")
        block = ctx.enter_context(nc.Block())
        NJ = NB // 2

        @block.sync
        def _(sp):
            for t, d in ((ident, a["ident"][:]), (ng, a["ng"][:]), (nb, a["nb"][:]), (wo, a["w_out"][:])):
                sp.dma_start(t[:], d).then_inc(c_in, 16)
            sp.dma_start(dsk[:], a["ds"][0].partition_broadcast(TOK)).then_inc(c_in, 16)
            with sp.Fori(0, n_pairs * NJ) as i:
                g, j = i // NJ, i % NJ
                for s in range(2):
                    n = i * 2 + s
                    cols = bass.ds((j * 2 + s) * CW, CW)
                    sp.wait_ge(half_sum, n)
                    sp.wait_ge(sum_all, n)
                    for k in range(NDIR):
                        sp.dma_start(ys[s][k][:], y_drams[k][g, cols].rearrange("w p c -> p w c")).then_inc(in_[s], 16)
                    sp.dma_start(u[s][:], u_dram[g, cols, :, 0:DI].rearrange("w p c -> p w c")).then_inc(in_[s], 16)
                    sp.wait_ge(xz_free[s], i)
                    sp.dma_start(z[s][:], z_dram[g, :, :, cols].rearrange("k c w b h -> c k (w b h)")).then_inc(xz_in[s], 16)
                    sp.dma_start(x[s][:], x_dram[g, :, :, cols].rearrange("k c w b h -> c k (w b h)")).then_inc(xz_in[s], 16)

        @block.gpsimd
        def _(pool):
            pool.memset(eps[:], LN_EPS).then_inc(eps_ready, 1)
            pool.wait_ge(built, 3)
            with pool.Fori(0, n_pairs * NJ) as i:
                for s in range(2):
                    n = i * 2 + s
                    pool.wait_ge(in_[s], (i + 1) * 80)
                    pool.wait_ge(sum_all, n)
                    pool.tensor_tensor(skip[:], u[s][:], dsk[:, 0].unsqueeze(1).to_broadcast([TOK, CW, DI]), ALU.mult).then_inc(pl, 1)
                    pool.wait_ge(pl, n * 1 + n + 1)
                    pool.tensor_tensor(skip[:], skip[:], ys[s][3][:], ALU.add).then_inc(pl, 1)
                    pool.wait_ge(pl, n * 2 + 2)
                    pool.sem_inc(half_sum, 1)

        @block.vector
        def _(dve):
            dve.wait_ge(c_in, 80)
            for k in range(1, NDIR):
                dve.tensor_tensor(dsk[:, 0], dsk[:, 0], dsk[:, k], ALU.add).then_inc(built, 1)
                dve.wait_ge(built, k)

            def sums(i, s):
                n = i * 2 + s
                L = 6
                step = [0]

                def chain(ins):
                    step[0] += 1
                    ins.then_inc(link, 1)
                    dve.wait_ge(link, n * L + step[0])

                dve.wait_ge(in_[s], (i + 1) * 80)
                chain(dve.tensor_tensor(acc[:], ys[s][0][:], ys[s][1][:], ALU.add))
                chain(dve.tensor_tensor(acc[:], acc[:], ys[s][2][:], ALU.add))
                dve.wait_ge(half_sum, n + 1)
                chain(dve.tensor_tensor(acc[:], acc[:], skip[:], ALU.add))
                dve.sem_inc(sum_all, 1)
                for w in range(CW):
                    ins = dve.bn_stats(stats[:, w], acc[:, w])
                chain(ins)
                dve.sem_inc(passed, 1)
                for w in range(CW):
                    ins = dve.bn_aggr(mv[:, w], stats[:, w])
                ins.then_inc(mv_ready, 1)
                dve.wait_ge(std_ready, n + 1)
                chain(dve.reciprocal(rstd[:], std[:]))
                dve.wait_ge(turned_s[s], i)
                for w in range(CW):
                    ins = dve.tensor_scalar(nrm[s][:, w], acc[:, w], mv[:, w, 0:1], rstd[:, w:w + 1], ALU.subtract, ALU.mult)
                chain(ins)
                assert step[0] == L
                dve.sem_inc(nrm_ready, 1)

            def gate(i, s):
                n = i * 2 + s
                dve.wait_ge(xz_in[s], (i + 1) * 32)
                for k in range(IK):
                    dve.wait_ge(aff_ready[k], n + 1)
                    dve.tensor_tensor(g_[:, k], g_[:, k], z[s][:, k], ALU.mult).then_inc(g_ready[k], 1)
                dve.wait_ge(stored[s], i * 16)
                for oc in range(KC):
                    dve.wait_ge(o_psr[oc], n + 1)
                    dve.tensor_tensor(o[s][:, oc], o_ps[oc][:], x[s][:, oc], ALU.add).then_inc(o_ready[oc], 1)
                dve.wait_ge(o_ready[KC - 1], n + 1)
                dve.sem_inc(xz_free[s], 1)

            with dve.Fori(0, n_pairs * NJ) as i:
                sums(i, 0)
                sums(i, 1)
                gate(i, 0)
                gate(i, 1)

        @block.tensor
        def _(pe):
            pe.wait_ge(c_in, 80)
            with pe.Fori(0, n_pairs * NJ) as i:
                for s in range(2):
                    n = i * 2 + s
                    pe.wait_ge(nrm_ready, n + 1)
                    for k in range(IK):
                        pe.wait_ge(aff_ready[k], i * 2)
                    for k in range(IK):
                        for w in range(CW):
                            ins = pe.transpose(t_ps[s][k][:, w * TOK:(w + 1) * TOK], nrm[s][:, w, k * 128:(k + 1) * 128], ident[0:TOK, 0:TOK])
                    ins.then_inc(turned_s[s], 1)
                for s in range(2):
                    n = i * 2 + s
                    for k in range(IK):
                        pe.wait_ge(g_ready[k], n + 1)
                    for oc in range(KC):
                        pe.wait_ge(o_ready[oc], n)
                        for k in range(IK):
                            ins = pe.matmul(o_ps[oc][:], wo[:, k, oc * CP:(oc + 1) * CP], g_[:, k], start=(k == 0), stop=(k == IK - 1))
                        ins.then_inc(o_psr[oc], 1)

        @block.scalar
        def _(act):
            act.wait_ge(c_in, 80)
            act.wait_ge(eps_ready, 1)
            with act.Fori(0, n_pairs * NJ) as i:
                g, j = i // NJ, i % NJ
                for s in range(2):
                    act.wait_ge(mv_ready, i * 2 + s + 1)
                    act.activation(std[:], mv[:, :, 1], ACT.Sqrt, bias=eps[:, 0:1]).then_inc(std_ready, 1)
                for s in range(2):
                    n = i * 2 + s
                    act.wait_ge(turned_s[s], i + 1)
                    for oc in range(KC):
                        act.wait_ge(o_psr[oc], n)
                    for k in range(IK):
                        act.activation(g_[:, k], t_ps[s][k][:], ACT.Identity, bias=nb[:, k:k + 1], scale=ng[:, k:k + 1]).then_inc(aff_ready[k], 1)
                for s in range(2):
                    n = i * 2 + s
                    for oc in range(KC):
                        act.wait_ge(o_ready[oc], n + 1)
                    act.dma_start(out[g, :, :, bass.ds((j * 2 + s) * CW, CW)].rearrange("k c w b h -> c k (w b h)"), o[s][:]).then_inc(stored[s], 16)
            for s in range(2):
                act.wait_ge(stored[s], 16 * n_pairs * NJ)


def build(nc, a, out, n_pairs):
    d = lambda n, s: nc.dram_tensor(n, s, F32, kind="Internal").ap()
    scale1, scale2 = d("scale1", (n_pairs, CP, KC * PB, 2)), d("scale2", (n_pairs, CP, KC * PB, 2))
    lag_tables, toeplitz = d("lag_tables", (2, D1, LAGS)), d("toeplitz", (2, SIDE, D1, SIDE))
    gated, mixed = d("gated", (n_pairs, TOK, SIDE, D1)), d("mixed", (n_pairs, TOK, SIDE, D1))
    x2 = d("x2", (n_pairs, KC, CP, SIDE, PB, SIDE))
    z = d("z", (n_pairs, IK, 128, SIDE, PB, SIDE))
    u = d("u", (n_pairs, SIDE, TOK, DI + NDIR * 2 * HEADS))
    bc = d("bc", (n_pairs, SIDE, TOK, NDIR * 2 * NS))
    ys = [d(f"y{k}", (n_pairs, SIDE, TOK, DI)) for k in range(NDIR)]
    toeplitz_tables(nc, a, a["lag"], lag_tables, toeplitz)
    gn_stats(nc, "gn1", a["x"], scale1, a["gavg"], n_pairs)
    mixer_qv(nc, a["x"], scale1, a["wqv"], gated, n_pairs)
    mixer_toeplitz(nc, gated, toeplitz, a["ident"], mixed, n_pairs)
    mixer_out(nc, a["x"], scale1, mixed, a["wp"], a["pb"], a["wo"], a["ob"], a["ident"], x2, n_pairs)
    gn_stats(nc, "gn2", x2, scale2, a["gavg"], n_pairs)
    scan_inputs(nc, x2, scale2, a, z, u, bc, n_pairs)
    scans(nc, a, u, bc, ys, n_pairs)
    scan_out(nc, a, x2, z, u, ys, out, n_pairs)


def lay_out_inputs(n):
    f = lambda k: np.ascontiguousarray(np.asarray(n[k]))
    x = f("x")
    pairs = x.shape[0] // PB
    arr = {}
    arr["x"] = x.reshape(pairs, PB, SIDE, SIDE, KC, CP).transpose(0, 4, 5, 3, 1, 2)
    qv = np.zeros((CP + 1, KC, 2 * D1), x.dtype)
    qv[:CP] = np.concatenate([f("L0_conv_q_w"), f("L0_conv_v_w")], 0).T.reshape(KC, CP, 2 * D1).transpose(1, 0, 2)
    qv[CP, KC - 1] = np.concatenate([f("L0_conv_q_b"), f("L0_conv_v_b")])
    arr["wqv"] = qv
    arr["wp"] = f("L0_conv_p_w").T.reshape(KC, CP, D1).transpose(1, 0, 2)
    arr["pb"] = f("L0_conv_p_b").reshape(DC, CP).T
    arr["wo"] = f("L0_conv_o_w").T.reshape(DC, CP, C).transpose(1, 0, 2)
    arr["ob"] = f("L0_conv_o_b").reshape(KC, CP).T
    arr["slope"] = f("L0_conv_slope").reshape(DC, CP).T
    t = lambda k: [f(f"L0_conv_t{i}_{k}") for i in (1, 2)]
    arr["t_w0"] = np.stack([np.stack([w[:, 0], b], 1) for w, b in zip(t("w0"), t("b0"))], 1)
    arr["t_ws"] = np.stack([w.transpose(0, 2, 1) for w in t("ws")])
    arr["t_bs"] = np.stack([b.T for b in t("bs")], 1)
    arr["t_wo"] = np.stack([w.T for w in t("wo")])
    arr["t_bo"] = np.stack([b.reshape(DC, CP).T for b in t("bo")], 1)
    arr["w_in"] = f("L1_conv_in_proj_w").T.reshape(KC, CP, 2 * DI).transpose(1, 0, 2)
    arr["cw"] = f("L1_conv_conv_w").reshape(IK, 128, 3, 3).transpose(1, 0, 2, 3)
    arr["cb"] = f("L1_conv_conv_b").reshape(IK, 128).T
    xp = f("L1_conv_x_proj_w")
    bc = xp[:, HEADS:].reshape(NDIR * 2 * NS, DI)
    dts = xp[:, :HEADS].reshape(NDIR * HEADS, DI)
    arr["wx"] = np.concatenate([bc, dts], 0).T.reshape(IK, 128, -1).transpose(1, 0, 2)
    arr["alog"] = f("L1_conv_A_logs").reshape(1, -1)
    arr["dtb"] = f("L1_conv_dt_bias").reshape(1, -1)
    arr["ds"] = f("L1_conv_Ds").reshape(1, NDIR, DI)
    arr["ng"] = f("L1_conv_out_norm_g").reshape(IK, 128).T
    arr["nb"] = f("L1_conv_out_norm_b").reshape(IK, 128).T
    arr["w_out"] = f("L1_conv_out_proj_w").T.reshape(IK, 128, C).transpose(1, 0, 2)
    lag = np.arange(-(SIDE - 1), SIDE, dtype=np.float32)
    arr["lag"] = np.stack([np.where(lag >= 0, lag, -(SIDE + lag)), np.abs(lag)])
    c = np.arange(CP)
    arr["gavg"] = (c[:, None] // 6 == c[None] // 6).astype(np.float32) / np.float32(6)
    arr["ident"] = np.eye(128, dtype=np.float32)
    i = np.arange(128)
    same = (i[:, None] // 64 == i[None] // 64)
    pos = i % 64
    q = np.arange(SIDE)
    arr["later"] = np.stack([same & (pos[:, None] > pos[None]), same & (pos[:, None] < pos[None])]).astype(np.float32)
    arr["upto"] = np.stack([same & (pos[:, None] <= pos[None]), same & (pos[:, None] >= pos[None])]).astype(np.float32)
    arr["seen"] = np.stack([pos[:, None] <= q[None], pos[:, None] >= q[None]]).astype(np.float32)
    arr["same"] = same.astype(np.float32)
    return {k: np.ascontiguousarray(v) for k, v in arr.items()}


def kernel(**inputs):
    import concourse.bacc as _bacc
    from concourse.bass_utils import run_bass_kernel_spmd as _run

    arrays = lay_out_inputs(inputs)
    nc = _bacc.Bacc("TRN2", target_bir_lowering=False, num_devices=1)
    aps = {k: nc.dram_tensor(k, v.shape, F32, kind="ExternalInput").ap() for k, v in arrays.items()}
    n_pairs = arrays["x"].shape[0]
    out = nc.dram_tensor("out", (n_pairs, KC, CP, SIDE, PB, SIDE), F32, kind="ExternalOutput").ap()
    build(nc, aps, out, n_pairs)
    r = _run(nc, [arrays], core_ids=[0])
    got = r.results[0]["out"]
    return got.transpose(0, 4, 5, 3, 1, 2).reshape(n_pairs * PB, SIDE, SIDE, C)
```

```python
from contextlib import ExitStack

import numpy as np
import concourse.bass as bass
from concourse import mybir

F32 = mybir.dt.float32
ALU = mybir.AluOpType
ACT = mybir.ActivationFunctionType

PB = 2
SIDE = 56
TOK = PB * SIDE
C = 192
KC = 2
CP = C // KC
D1 = 576
DC = D1 // CP
LAGS = 2 * SIDE - 1
CW = 4
BLK = CW * TOK
NB = SIDE // CW
GC = 8
DI = 384
IK = DI // 128
NDIR = 4
HEADS = 12
HP = DI // HEADS
NS = 64
REC = 2 * NS + 2 * HEADS
GN_EPS = 1e-5
LN_EPS = 1e-5


class Scope:

    def __init__(self, nc, ctx, name):
        self.nc, self.ctx, self.name = nc, ctx, name
        self.sems = []
        ctx.callback(self.clear)

    def clear(self):
        self.nc.clear_and_free_semaphores(self.sems)
        self.nc.all_engine_barrier()

    def sb(self, name, shape):
        return self.ctx.enter_context(self.nc.sbuf_tensor(f"{self.name}_{name}", shape, F32))

    def sb2(self, name, shape, n=2):
        return [self.sb(f"{name}{i}", shape) for i in range(n)]

    def ps(self, name, shape):
        return self.ctx.enter_context(self.nc.psum_tensor(f"{self.name}_{name}", shape, F32))

    def sem(self, name):
        self.sems.append(self.nc.alloc_semaphore(name=f"{self.name}_{name}"))
        return self.sems[-1]

    def sem2(self, name, n=2):
        return [self.sem(f"{name}{i}") for i in range(n)]




def gn_stats(nc, name, src, scale_dram, group_avg, n_pairs):
    with ExitStack() as ctx:
        S = Scope(nc, ctx, name)
        sb, sem = S.sb, S.sem
        x = sb("x", [CP, KC, SIDE, PB, SIDE])
        gavg = sb("gavg", [CP, CP])
        stats = sb("stats", [CP, KC, PB, NB // 2, 6])
        mv = sb("mv", [CP, KC * PB, 2])
        mom = sb("mom", [CP, KC * PB, 2])
        grp = sb("grp", [CP, KC * PB, 2])
        var = sb("var", [CP, KC * PB])
        std = sb("std", [CP, KC * PB])
        sc = sb("sc", [CP, KC * PB, 2])
        grp_ps = ctx.enter_context(nc.psum_tensor(f"{name}_ps", [CP, KC * PB * 2], F32))
        gavg_in, x_in, x_used = sem("gavg_in"), sem("x_in"), sem("x_used")
        passed = sem("passed")
        stat, mom_ready, grp_ready, var_ready, std_ready, sc_ready, sc_out = (
            sem(n) for n in ("stat", "mom", "grpr", "varr", "stdr", "scr", "sco"))
        block = ctx.enter_context(nc.Block())
        HALF = SIDE // 2

        @block.sync
        def _(sp):
            sp.dma_start(gavg[:], group_avg[:]).then_inc(gavg_in, 16)
            with sp.Fori(0, n_pairs) as g:
                sp.wait_ge(x_used, g)
                for kc in range(KC):
                    for half in range(2):
                        sp.dma_start(x[:, kc, half * HALF:(half + 1) * HALF], src[g, kc, :, half * HALF:(half + 1) * HALF]).then_inc(x_in, 16)
                sp.wait_ge(sc_ready, (g + 1) * 2)
                sp.dma_start(scale_dram[g], sc[:]).then_inc(sc_out, 16)
            sp.wait_ge(sc_out, 16 * n_pairs)

        @block.vector
        def _(dve):
            with dve.Fori(0, n_pairs) as g:
                dve.wait_ge(x_in, (g + 1) * 64)
                for kc in range(KC):
                    for b in range(PB):
                        for j in range(7):
                            ins = dve.bn_stats(stats[:, kc, b, j], x[:, kc, j * 8:j * 8 + 8, b])
                ins.then_inc(x_used, 1)
                dve.wait_ge(x_used, g + 1)
                dve.sem_inc(passed, 1)
                for kb in range(KC * PB):
                    ins = dve.bn_aggr(mv[:, kb], stats[:, kb // PB, kb % PB].rearrange("c j s -> c (j s)"))
                ins.then_inc(stat, 1)
                dve.wait_ge(stat, g * 4 + 1)
                dve.tensor_tensor(mom[:, :, 1], mv[:, :, 0], mv[:, :, 0], ALU.mult).then_inc(stat, 1)
                dve.wait_ge(stat, g * 4 + 2)
                dve.tensor_tensor(mom[:, :, 1], mom[:, :, 1], mv[:, :, 1], ALU.add)
                dve.tensor_copy(mom[:, :, 0], mv[:, :, 0]).then_inc(mom_ready, 1)
                dve.wait_ge(grp_ready, g + 1)
                dve.tensor_copy(grp[:].rearrange("c k s -> c (k s)"), grp_ps[:]).then_inc(stat, 1)
                dve.wait_ge(stat, g * 4 + 3)
                dve.tensor_tensor(var[:], grp[:, :, 0], grp[:, :, 0], ALU.mult).then_inc(stat, 1)
                dve.wait_ge(stat, g * 4 + 4)
                dve.scalar_tensor_tensor(out=var[:], in0=grp[:, :, 1], scalar=GN_EPS, in1=var[:], op0=ALU.add, op1=ALU.subtract).then_inc(var_ready, 1)
                dve.wait_ge(std_ready, g + 1)
                dve.wait_ge(sc_out, g * 16)
                dve.reciprocal(sc[:, :, 0], std[:]).then_inc(sc_ready, 1)
                dve.wait_ge(sc_ready, g * 2 + 1)
                dve.scalar_tensor_tensor(out=sc[:, :, 1], in0=grp[:, :, 0], scalar=-1.0, in1=sc[:, :, 0], op0=ALU.mult, op1=ALU.mult).then_inc(sc_ready, 1)

        @block.tensor
        def _(pe):
            pe.wait_ge(gavg_in, 16)
            with pe.Fori(0, n_pairs) as g:
                pe.wait_ge(mom_ready, g + 1)
                pe.matmul(grp_ps[:], gavg[:], mom[:].rearrange("c k s -> c (k s)"), start=True, stop=True).then_inc(grp_ready, 1)

        @block.scalar
        def _(act):
            with act.Fori(0, n_pairs) as g:
                act.wait_ge(var_ready, g + 1)
                act.activation(std[:], var[:], ACT.Sqrt).then_inc(std_ready, 1)


def toeplitz_tables(nc, a, lag_const, a_dram, t_dram):
    with ExitStack() as ctx:
        R = a["t_w0"].shape[0]
        S = Scope(nc, ctx, "tt")
        sb, sem = S.sb, S.sem
        posr = sb("pos", [R, LAGS])
        absl = sb("absl", [CP, LAGS])
        w0 = sb("w0", [R, 2, 2])
        ws = sb("ws", [R, 2, 3, R])
        bs = sb("bs", [R, 2, 3])
        wo = sb("wo", [R, 2, D1])
        bo = sb("bo", [CP, 2, DC])
        slope = sb("slope", [CP, DC])
        hid = sb("hid", [R, 2, 4, LAGS])
        decay = sb("decay", [CP, DC, LAGS])
        tab = sb("tab", [CP, 2, DC, LAGS])
        h_ps = [ctx.enter_context(nc.psum_tensor(f"tt_h{i}", [R, LAGS], F32)) for i in range(2)]
        o_ps = [ctx.enter_context(nc.psum_tensor(f"tt_o{i}", [CP, 4, 128], F32)) for i in range(2)]
        loads, lin, hid_ready, sl_ready, ln_ready, dec_ready, out_ready, tab_ready, tab_out, t_out = (
            sem(n) for n in ("loads", "lin", "hid", "sl", "ln", "dec", "out", "tab", "tabo", "to"))
        block = ctx.enter_context(nc.Block())

        @block.sync
        def _(sp):
            sp.dma_start(posr[:], lag_const[0].partition_broadcast(R)).then_inc(loads, 16)
            sp.dma_start(absl[:], lag_const[1].partition_broadcast(CP)).then_inc(loads, 16)
            sp.dma_start(w0[:], a["t_w0"][:]).then_inc(loads, 16)
            for t in range(2):
                sp.dma_start(ws[:, t], a["t_ws"][t].rearrange("l i o -> i l o")).then_inc(loads, 16)
            sp.dma_start(wo[:], a["t_wo"].rearrange("t r d -> r t d")).then_inc(loads, 16)
            sp.dma_start(bs[:], a["t_bs"][:]).then_inc(loads, 16)
            sp.dma_start(bo[:], a["t_bo"][:]).then_inc(loads, 16)
            sp.dma_start(slope[:], a["slope"][:]).then_inc(loads, 16)
            sp.wait_ge(tab_ready, 2 * DC)
            for t in range(2):
                sp.dma_start(a_dram[t].rearrange("(k c) l -> c k l", c=CP), tab[:, t]).then_inc(tab_out, 16)
            sp.wait_ge(tab_out, 32)
            for t in range(2):
                with sp.Fori(0, SIDE) as row:
                    sp.dma_start(t_dram[t, row], a_dram[t, :, bass.ds(SIDE - 1 - row, SIDE)]).then_inc(t_out, 16)
            sp.wait_ge(t_out, 2 * SIDE * 16)

        n_loads = 16 * 9

        @block.vector
        def _(dve):
            dve.wait_ge(loads, n_loads)
            for t in range(2):
                dve.tensor_scalar(hid[:, t, 0], posr[:], w0[:, t, 0:1], w0[:, t, 1:2], ALU.mult, ALU.add).then_inc(lin, 1)
            dve.wait_ge(lin, 2)
            for t in range(2):
                dve.tensor_scalar(hid[:, t, 0], hid[:, t, 0], 0.0, None, ALU.max).then_inc(hid_ready, 1)
            dve.tensor_scalar(slope[:], slope[:], 0.0, 1.0, ALU.max, ALU.min).then_inc(lin, 1)
            dve.wait_ge(lin, 3)
            dve.tensor_scalar(slope[:], slope[:], 1.0 - 0.95, 0.95, ALU.mult, ALU.add).then_inc(sl_ready, 1)
            for layer in range(3):
                for t in range(2):
                    dve.wait_ge(out_ready, layer * 2 + t + 1)
                    dve.tensor_scalar(hid[:, t, layer + 1], h_ps[t][:], bs[:, t, layer:layer + 1], 0.0, ALU.add, ALU.max).then_inc(hid_ready, 1)
            dve.wait_ge(dec_ready, DC)
            for t in range(2):
                for k in range(DC):
                    dve.wait_ge(out_ready, 6 + t * 2 + k // 3 + 1)
                    dve.scalar_tensor_tensor(out=tab[:, t, k], in0=o_ps[k // 3][:, k % 3, 0:LAGS], scalar=bo[:, t, k:k + 1],
                                             in1=decay[:, k], op0=ALU.add, op1=ALU.mult).then_inc(tab_ready, 1)

        @block.tensor
        def _(pe):
            pe.wait_ge(loads, n_loads)
            for layer in range(3):
                for t in range(2):
                    pe.wait_ge(hid_ready, layer * 2 + t + 1)
                    pe.matmul(h_ps[t][:], ws[:, t, layer], hid[:, t, layer], start=True, stop=True).then_inc(out_ready, 1)
            for t in range(2):
                pe.wait_ge(hid_ready, 6 + t + 1)
                for half in range(2):
                    if t == 1:
                        pe.wait_ge(tab_ready, 3 * (half + 1))
                    for k in range(3 * half, 3 * half + 3):
                        ins = pe.matmul(o_ps[half][:, k % 3, 0:LAGS], wo[:, t, k * CP:(k + 1) * CP], hid[:, t, 3], start=True, stop=True)
                    ins.then_inc(out_ready, 1)

        @block.scalar
        def _(act):
            act.wait_ge(sl_ready, 1)
            act.activation(slope[:], slope[:], ACT.Ln).then_inc(ln_ready, 1)
            act.wait_ge(ln_ready, 1)
            for k in range(DC):
                act.activation(decay[:, k], absl[:], ACT.Exp, scale=slope[:, k:k + 1]).then_inc(dec_ready, 1)


def load_scale(sp, sc, scale_dram, g, sem):
    sp.dma_start(sc[:].rearrange("c k b s -> c (k b) s"), scale_dram[g]).then_inc(sem, 16)


def load_block(sp, dst, src, g, block, sem):
    sp.dma_start(dst[:], src[g, :, :, bass.ds(block * CW, CW)].rearrange("k c w b h -> c k w b h")).then_inc(sem, 16)


def normalise(eng, dst, src, sc):
    for kc in range(KC):
        for b in range(PB):
            ins = eng.tensor_scalar(dst[0:CP, kc, :, b], src[:, kc, :, b], sc[:, kc, b, 0:1], sc[:, kc, b, 1:2], ALU.mult, ALU.add)
    return ins


def mixer_qv(nc, x_dram, scale_dram, wqv_dram, gated_dram, n_pairs):
    with ExitStack() as ctx:
        S = Scope(nc, ctx, "qv")
        passed = S.sem("passed")
        wqv = S.sb("wqv", [CP + 1, KC, 2 * D1])
        sc = S.sb("sc", [CP, KC, PB, 2])
        xs = S.sb2("xs", [CP, KC, CW, PB, SIDE])
        xn = S.sb2("xn", [CP + 1, KC, CW, PB, SIDE])
        qv = S.sb2("qv", [TOK, 2 * D1])
        xo = S.sb2("xo", [TOK, CW, D1])
        NT = 3
        NW = 2 * D1 // NT
        ps = [S.ps(f"ps{i}", [TOK, NT, 512]) for i in range(2)]
        w_in, ones, sc_in = S.sem("w_in"), S.sem("ones"), S.sem("sc_in")
        x_in, normed, silu, gated, block_gated, stored, block_read = (
            S.sem2(n) for n in ("x_in", "normed", "silu", "gated", "bgated", "stored", "bread"))
        proj = S.sem2("proj")
        block = ctx.enter_context(nc.Block())
        NJ = NB // 2

        @block.sync
        def _(sp):
            sp.dma_start(wqv[:], wqv_dram[:]).then_inc(w_in, 16)
            with sp.Fori(0, n_pairs) as g:
                sp.wait_ge(normed[1], g * NJ)
                load_scale(sp, sc, scale_dram, g, sc_in)
                with sp.Fori(0, NJ) as j:
                    i = g * NJ + j
                    for s in range(2):
                        sp.wait_ge(normed[s], i)
                        load_block(sp, xs[s], x_dram, g, j * 2 + s, x_in[s])

        @block.gpsimd
        def _(pool):
            for s in range(2):
                pool.memset(xn[s][:], 1.0).then_inc(ones, 1)
            pool.wait_ge(ones, 2)
            with pool.Fori(0, n_pairs) as g:
                pool.wait_ge(sc_in, (g + 1) * 16)
                pool.sem_inc(passed, 1)
                with pool.Fori(0, NJ) as j:
                    i = g * NJ + j
                    for s in range(2):
                        pool.wait_ge(x_in[s], (i + 1) * 16)
                        pool.wait_ge(block_read[s], i)
                        pool.sem_inc(passed, 1)
                        normalise(pool, xn[s], xs[s], sc).then_inc(normed[s], 1)

        @block.tensor
        def _(pe):
            pe.wait_ge(w_in, 16)
            with pe.Fori(0, n_pairs * NJ) as i:
                for s in range(2):
                    pe.wait_ge(normed[s], i + 1)
                    for w in range(CW):
                        u = (s * CW + w) % 2
                        m = i * CW + (s * CW + w) // 2
                        pe.wait_ge(silu[u], m)
                        for kc in range(KC):
                            p = CP + kc
                            for n in range(NT):
                                ins = pe.matmul(ps[u][:, n, 0:NW], xn[s][0:p, kc, w].rearrange("p b h -> p (b h)"),
                                                wqv[0:p, kc, n * NW:(n + 1) * NW], start=(kc == 0), stop=(kc == KC - 1))
                        ins.then_inc(block_read[s] if w == CW - 1 else proj[s], 1)

        @block.scalar
        def _(act):
            with act.Fori(0, n_pairs * NJ) as i:
                g, j = i // NJ, i % NJ
                for s in range(2):
                    for w in range(CW):
                        u = (s * CW + w) % 2
                        m = i * CW + (s * CW + w) // 2
                        if w == CW - 1:
                            act.wait_ge(block_read[s], i + 1)
                        else:
                            act.wait_ge(proj[s], i * (CW - 1) + w + 1)
                        act.wait_ge(gated[u], m)
                        act.activation(qv[u][:].rearrange("t (n c) -> t n c", n=NT), ps[u][:, :, 0:NW], ACT.Silu).then_inc(silu[u], 1)
                    act.wait_ge(gated[1], i * CW + (s * CW + CW - 1) // 2 + 1)
                    act.wait_ge(gated[0], i * CW + (s * CW + CW - 1) // 2 + 1)
                    act.dma_start(gated_dram[g, :, bass.ds(j * 2 * CW + s * CW, CW)], xo[s][:]).then_inc(stored[s], 16)
            for s in range(2):
                act.wait_ge(stored[s], 16 * n_pairs * NJ)

        @block.vector
        def _(dve):
            with dve.Fori(0, n_pairs * NJ) as i:
                for s in range(2):
                    dve.wait_ge(stored[s], i * 16)
                    for w in range(CW):
                        u = (s * CW + w) % 2
                        m = i * CW + (s * CW + w) // 2
                        dve.wait_ge(silu[u], m + 1)
                        dve.tensor_tensor(xo[s][:, w], qv[u][:, 0:D1], qv[u][:, D1:2 * D1], ALU.mult).then_inc(gated[u], 1)


def mixer_toeplitz(nc, gated_dram, t_dram, ident_dram, mixed_dram, n_pairs):
    with ExitStack() as ctx:
        S = Scope(nc, ctx, "tp")
        passed = S.sem("passed")
        GS = 4
        HG = GC // 2
        ident = S.sb("ident", [128, 128])
        x = S.sb2("x", [TOK, SIDE, CP])
        o = S.sb2("o", [SIDE, TOK, CP])
        t2 = S.sb2("t2", [128, GC, PB, SIDE], GS)
        t1 = S.sb2("t1", [128, GC, SIDE], GS)
        xg = S.sb2("xg", [128, GC, SIDE], GS)
        xt = S.sb2("xt", [128, 2, HG, TOK], GS)
        tp = [S.ps(f"tps{i}", [SIDE, 2, 512]) for i in range(2)]
        op = [S.ps(f"ops{i}", [SIDE, 2, 512]) for i in range(2)]
        id_in, zero = S.sem("id_in"), S.sem("zero")
        x_in, chunk_out = S.sem2("x_in"), S.sem2("chunk_out")
        t_in, staged, turned, xt_ready, summed, o_ready = (S.sem2(n, GS) for n in ("t_in", "staged", "turned", "xt_ready", "summed", "o_ready"))
        block = ctx.enter_context(nc.Block())
        NCH = n_pairs * DC // 2
        NG = CP // GC // GS
        PADS = 4 * GS

        def earlier(m, q, by):
            return (q - by) % GS, m + (1 if q >= by else 0)

        @block.sync
        def _(sp):
            sp.dma_start(ident[:], ident_dram[:]).then_inc(id_in, 16)
            sp.wait_ge(zero, PADS)
            with sp.Fori(0, NCH) as i:
                for s in range(2):
                    with sp.Fori(0, NG) as j:
                        m = (i * 2 + s) * NG + j
                        for q in range(GS):
                            sp.wait_ge(summed[q], m)
                            c0 = ((i * 2 + s) % DC) * CP + (j * GS + q) * GC
                            for b in range(PB):
                                sp.dma_start(t2[q][b * SIDE:(b + 1) * SIDE, :, b], t_dram[1, :, bass.ds(c0, GC)]).then_inc(t_in[q], 16)
                            sp.dma_start(t1[q][0:SIDE], t_dram[0, :, bass.ds(c0, GC)]).then_inc(t_in[q], 16)

        @block.gpsimd
        def _(pool):
            def load(n, s):
                pool.dma_start(x[s][:], gated_dram[n // DC, :, :, bass.ds((n % DC) * CP, CP)]).then_inc(x_in[s], 16)

            def chunks(i, last):
                for s in range(2):
                    n = i * 2 + s
                    for q in range(GS):
                        pool.wait_ge(staged[q], n * NG)
                    if not (last and s):
                        load(n + 1, 1 - s)
                    pool.wait_ge(x_in[s], (i + 1) * 16)
                    pool.sem_inc(passed, 1)
                    with pool.Fori(0, NG) as j:
                        m = n * NG + j
                        for q in range(GS):
                            pool.wait_ge(summed[q], m)
                            pool.tensor_copy(xg[q][0:TOK], x[s][:, :, bass.ds((j * GS + q) * GC, GC)].rearrange("t w c -> t c w")).then_inc(staged[q], 1)

            load(0, 0)
            for q in range(GS):
                for t in (t2, t1, xg, xt):
                    pool.memset(t[q][:], 0.0).then_inc(zero, 1)
            pool.wait_ge(zero, PADS)
            with pool.Fori(0, NCH - 1) as i:
                chunks(i, False)
            chunks(NCH - 1, True)

        @block.vector
        def _(dve):
            with dve.Fori(0, NCH) as i:
                for s in range(2):
                    dve.wait_ge(chunk_out[s], i * 16)
                    dve.sem_inc(passed, 1)
                    with dve.Fori(0, NG) as j:
                        m = (i * 2 + s) * NG + j
                        for q in range(GS):
                            dve.wait_ge(summed[q], m + 1)
                            dve.tensor_copy(o[s][:, :, bass.ds((j * GS + q) * GC, GC)].rearrange("w t (h r) -> w h r t", h=2),
                                            op[q % 2][:, :, 0:HG * TOK].rearrange("w h (r t) -> w h r t", t=TOK)).then_inc(o_ready[q], 1)

        @block.tensor
        def _(pe):
            def turn(m, q):
                pe.wait_ge(staged[q], m + 1)
                at, count = earlier(m, q, 2)
                pe.wait_ge(xt_ready[at], count)
                pe.sem_inc(passed, 1)
                for c in range(GC):
                    h, r = c // HG, c % HG
                    ins = pe.transpose(tp[q % 2][:, h, r * TOK:(r + 1) * TOK], xg[q][0:TOK, c], ident[0:TOK, 0:TOK])
                ins.then_inc(turned[q], 1)

            def products(m, q):
                pe.wait_ge(t_in[q], (m + 1) * 48)
                pe.wait_ge(xt_ready[q], m + 1)
                at, count = earlier(m, q, 2)
                pe.wait_ge(o_ready[at], count)
                for c in range(GC):
                    h, r = c // HG, c % HG
                    sums = op[q % 2][:, h, r * TOK:(r + 1) * TOK]
                    pe.matmul(sums, xg[q][:, c], t2[q][:, c].rearrange("p b h -> p (b h)"), start=True, stop=False)
                    ins = pe.matmul(sums, t1[q][:, c], xt[q][:, h, r], start=False, stop=True)
                ins.then_inc(summed[q], 1)

            pe.wait_ge(id_in, 16)
            rounds = NCH * 2 * NG
            turn(0, 0)
            with pe.Fori(0, rounds - 1) as m:
                for q in range(GS):
                    turn(m + (q + 1) // GS, (q + 1) % GS)
                    products(m, q)
            for q in range(GS):
                if q + 1 < GS:
                    turn(rounds - 1, q + 1)
                products(rounds - 1, q)

        @block.scalar
        def _(act):
            act.wait_ge(zero, PADS)
            with act.Fori(0, NCH) as i:
                for s in range(2):
                    n = i * 2 + s
                    with act.Fori(0, NG) as j:
                        m = n * NG + j
                        for q in range(GS):
                            act.wait_ge(turned[q], m + 1)
                            act.wait_ge(summed[q], m)
                            act.copy(xt[q][0:SIDE].rearrange("w h r t -> w h (r t)"), tp[q % 2][:, :, 0:HG * TOK]).then_inc(xt_ready[q], 1)
                    for q in range(GS):
                        act.wait_ge(o_ready[q], (n + 1) * NG)
                    act.dma_start(mixed_dram[n // DC, :, :, bass.ds((n % DC) * CP, CP)], o[s][:]).then_inc(chunk_out[s], 16)
            for s in range(2):
                act.wait_ge(chunk_out[s], NCH * 16)


def mixer_out(nc, x_dram, scale_dram, mixed_dram, wp_dram, pb_dram, wo_dram, ob_dram, ident_dram, x2_dram, n_pairs):
    with ExitStack() as ctx:
        S = Scope(nc, ctx, "mo")
        passed = S.sem("passed")
        ident = S.sb("ident", [128, 128])
        wp = S.sb("wp", [CP, KC, D1])
        pb = S.sb("pb", [CP, DC])
        wo = S.sb("wo", [CP, DC, C])
        ob = S.sb("ob", [CP, KC])
        sc = S.sb("sc", [CP, KC, PB, 2])
        xs = S.sb2("xs", [CP, KC, CW, PB, SIDE])
        xn = S.sb2("xn", [CP, KC, CW, PB, SIDE])
        mx = S.sb2("mx", [TOK, CW, D1])
        p = S.sb("p", [CP, DC, BLK])
        gt = S.sb("gt", [CP, DC, BLK])
        y = S.sb2("y", [CP, KC, BLK])
        pp = [S.ps(f"pp{i}", [CP, BLK]) for i in range(2)]
        tp = [S.ps(f"tp{i}", [CP, BLK]) for i in range(2)]
        yp = [S.ps(f"yp{i}", [CP, BLK]) for i in range(KC)]
        w_in, sc_in = S.sem("w_in"), S.sem("sc_in")
        x_in, mx_in, normed, x_free, xn_read, mx_read, stored = (
            S.sem2(n) for n in ("x_in", "mx_in", "normed", "x_free", "xn_read", "mx_read", "stored"))
        p_ps, p_ready, turned, gate, y_ps, y_ready, gt_read = (
            S.sem2(n) for n in ("p_ps", "p_ready", "turned", "gate", "y_ps", "y_ready", "gt_read"))
        block = ctx.enter_context(nc.Block())
        NJ = NB // 2
        half = DC // 2

        @block.sync
        def _(sp):
            for t, d in ((ident, ident_dram), (wp, wp_dram), (pb, pb_dram), (wo, wo_dram), (ob, ob_dram)):
                sp.dma_start(t[:], d[:]).then_inc(w_in, 16)
            with sp.Fori(0, n_pairs) as g:
                sp.wait_ge(normed[1], g * NJ)
                load_scale(sp, sc, scale_dram, g, sc_in)
                with sp.Fori(0, NJ) as j:
                    i = g * NJ + j
                    for s in range(2):
                        sp.wait_ge(x_free[s], i)
                        load_block(sp, xs[s], x_dram, g, j * 2 + s, x_in[s])
                        sp.wait_ge(mx_read[s], i)
                        sp.dma_start(mx[s][:], mixed_dram[g, bass.ds((j * 2 + s) * CW, CW)].rearrange("w t c -> t w c")).then_inc(mx_in[s], 16)

        @block.gpsimd
        def _(pool):
            with pool.Fori(0, n_pairs) as g:
                pool.wait_ge(sc_in, (g + 1) * 16)
                pool.sem_inc(passed, 1)
                with pool.Fori(0, NJ) as j:
                    i = g * NJ + j
                    for s in range(2):
                        pool.wait_ge(x_in[s], (i + 1) * 16)
                        pool.wait_ge(xn_read[s], i)
                        pool.sem_inc(passed, 1)
                        normalise(pool, xn[s], xs[s], sc).then_inc(normed[s], 1)

        @block.tensor
        def _(pe):
            pe.wait_ge(w_in, 80)
            with pe.Fori(0, n_pairs * NJ) as i:
                for s in range(2):
                    n = i * 2 + s
                    pe.wait_ge(normed[s], i + 1)
                    for c in range(DC):
                        q, m = c % 2, n * half + c // 2
                        pe.wait_ge(p_ready[q], m)
                        for kc in range(KC):
                            ins = pe.matmul(pp[q][:], wp[:, kc, c * CP:(c + 1) * CP], xn[s][:, kc].rearrange("p w b h -> p (w b h)"),
                                            start=(kc == 0), stop=(kc == KC - 1))
                        ins.then_inc(p_ps[q], 1)
                    pe.wait_ge(p_ps[1], (n + 1) * half)
                    pe.sem_inc(xn_read[s], 1)
                    pe.wait_ge(mx_in[s], (i + 1) * 16)
                    for c in range(DC):
                        q, m = c % 2, n * half + c // 2
                        pe.wait_ge(gate[q], m)
                        for w in range(CW):
                            ins = pe.transpose(tp[q][:, w * TOK:(w + 1) * TOK], mx[s][:, w, c * CP:(c + 1) * CP], ident[0:TOK, 0:TOK])
                        ins.then_inc(turned[q], 1)
                    pe.wait_ge(turned[1], (n + 1) * half)
                    pe.sem_inc(mx_read[s], 1)
                    for q in range(2):
                        pe.wait_ge(gate[q], (n + 1) * half)
                    for oc in range(KC):
                        pe.wait_ge(y_ready[oc], n)
                        for c in range(DC):
                            ins = pe.matmul(yp[oc][:], wo[:, c, oc * CP:(oc + 1) * CP], gt[:, c], start=(c == 0), stop=(c == DC - 1))
                        ins.then_inc(y_ps[oc], 1)

        @block.scalar
        def _(act):
            act.wait_ge(w_in, 80)
            with act.Fori(0, n_pairs * NJ) as i:
                g, j = i // NJ, i % NJ
                for s in range(2):
                    n = i * 2 + s
                    for c in range(DC):
                        q, m = c % 2, n * half + c // 2
                        act.wait_ge(p_ps[q], m + 1)
                        act.wait_ge(gate[q], n * half)
                        act.activation(p[:, c], pp[q][:], ACT.Silu, bias=pb[:, c:c + 1]).then_inc(p_ready[q], 1)
                    for oc in range(KC):
                        act.wait_ge(y_ready[oc], n + 1)
                    act.dma_start(x2_dram[g, :, :, bass.ds((j * 2 + s) * CW, CW)].rearrange("k c w b h -> c k (w b h)"), y[s][:]).then_inc(stored[s], 16)
            for s in range(2):
                act.wait_ge(stored[s], 16 * n_pairs * NJ)

        @block.vector
        def _(dve):
            dve.wait_ge(w_in, 80)
            with dve.Fori(0, n_pairs * NJ) as i:
                for s in range(2):
                    n = i * 2 + s
                    for oc in range(KC):
                        dve.wait_ge(y_ps[oc], n)
                    for c in range(DC):
                        q, m = c % 2, n * half + c // 2
                        dve.wait_ge(p_ready[q], m + 1)
                        dve.wait_ge(turned[q], m + 1)
                        dve.tensor_tensor(gt[:, c], tp[q][:], p[:, c], ALU.mult).then_inc(gate[q], 1)
                    dve.wait_ge(stored[s], i * 16)
                    for oc in range(KC):
                        dve.wait_ge(y_ps[oc], n + 1)
                        dve.scalar_tensor_tensor(out=y[s][:, oc], in0=yp[oc][:], scalar=ob[:, oc:oc + 1], in1=xs[s][:, oc].rearrange("p w b h -> p (w b h)"),
                                                 op0=ALU.add, op1=ALU.add).then_inc(y_ready[oc], 1)
                    dve.wait_ge(y_ready[1], n + 1)
                    dve.wait_ge(normed[s], i + 1)
                    dve.sem_inc(x_free[s], 1)


def scan_inputs(nc, x_dram, scale_dram, a, z_dram, u_dram, bc_dram, n_pairs):
    with ExitStack() as ctx:
        S = Scope(nc, ctx, "si")
        passed = S.sem("passed")
        N4 = NDIR * HEADS
        ROW = SIDE + 2
        ident = S.sb("ident", [128, 128])
        w_in = S.sb("w_in", [CP, KC, 2 * DI])
        cw = S.sb("cw", [128, IK, 3, 3])
        PE_TAPS = {1: 2, 2: 3}
        POOL_FROM = 4
        taps = S.sb("taps", [128, sum(PE_TAPS.values()), 128])
        cb = S.sb("cb", [128, IK])
        wx = S.sb("wx", [128, IK, NDIR * 2 * NS + N4])
        dtb = S.sb("dtb", [TOK, N4])
        aneg = S.sb("aneg", [TOK, N4])
        sc = S.sb("sc", [CP, KC, PB, 2])
        xs = S.sb2("xs", [CP, KC, CW, PB, SIDE])
        xn = S.sb2("xn", [CP, KC, CW, PB, SIDE])
        z = S.sb("z", [128, IK, BLK])
        xi = S.sb("xi", [128, IK, ROW, PB, ROW])
        part = S.sb2("part", [128, BLK])
        acc = S.sb2("acc", [128, IK, BLK])
        u = S.sb2("u", [128, IK, BLK])
        ut = S.sb("ut", [TOK, 2, CW, DI + N4])
        dts = S.sb("dts", [TOK, 2 * CW, NDIR, 2, HEADS])
        raw = S.sb("raw", [TOK, 2 * CW, N4])
        bc = S.sb2("bc", [TOK, CW, NDIR * 2 * NS])
        sp_ = {n: S.sb("sp_" + n, [TOK, 2 * CW, N4]) for n in ("t", "neg", "e", "ln", "ser", "small")}
        bank = [S.ps(f"bank{i}", [128, 512]) for i in range(8)]
        w_loaded, consts, sc_in, built = S.sem("w_loaded"), S.sem("consts"), S.sem("sc_in"), S.sem("built")
        x_in, normed, xn_read = S.sem2("x_in"), S.sem2("normed"), S.sem2("xn_read")
        z_ps, z_done, xi_ps, xi_done = (S.sem2(n, IK) for n in ("z_ps", "z_done", "xi_ps", "xi_done"))
        z_out = S.sem("z_out")
        c_ps, v_taps, c1_ready, p_taps, u_ready, u_read = (S.sem2(n) for n in ("c_ps", "v_taps", "c1_ready", "p_taps", "u_ready", "u_read"))
        N_V, N_1, N_P = 2 * 9 - PE_TAPS[2], POOL_FROM - PE_TAPS[1], 2 * (9 - POOL_FROM)
        bc_ps, t_ps, bc_done, t_done = (S.sem2(n) for n in ("bc_ps", "t_ps", "bc_done", "t_done"))
        ut_out, bc_out = S.sem2("ut_out"), S.sem2("bc_out")
        taken = S.sem2("taken")
        link, neg_ready, e_ready, ln_ready, raw_ready, dt_done, dt_out = (
            S.sem(n) for n in ("link", "neg_ready", "e_ready", "ln_ready", "raw_ready", "dt_done", "dt_out"))
        block = ctx.enter_context(nc.Block())
        NJ = NB // 2
        n_w = 16 * 7

        def window(k, g_cols, dh):
            return xi[:, k, g_cols, :, dh:dh + SIDE].rearrange("p w b h -> p (w b) h")

        def lines(t):
            return t.rearrange("p (w b h) -> p (w b) h", w=CW, b=PB)

        def blocks(eng, g, convolve, project, take, softplus, early=()):
            late = tuple(w for w in range(CW) if w not in early)

            def step(cj, cs, pj, ps):
                project(g, pj, ps, early)
                convolve(g, cj, cs)
                if ps == 0:
                    take(g, pj - 1, 1)
                    softplus(g, pj - 1)
                else:
                    take(g, pj, 0)
                project(g, pj, ps, late)

            convolve(g, 0, 0)
            project(g, 0, 0, early)
            convolve(g, 0, 1)
            project(g, 0, 0, late)
            step(1, 0, 0, 1)
            with eng.Fori(0, NJ - 2) as j:
                step(j + 1, 1, j + 1, 0)
                step(j + 2, 0, j + 1, 1)
            step(NJ - 1, 1, NJ - 1, 0)
            project(g, NJ - 1, 1, range(CW))
            take(g, NJ - 1, 0)
            take(g, NJ - 1, 1)
            softplus(g, NJ - 1)

        idle = lambda *_: None

        @block.sync
        def _(sp):
            for t, d in ((ident, a["ident"]), (w_in, a["w_in"]), (cw, a["cw"]), (cb, a["cb"]), (wx, a["wx"])):
                sp.dma_start(t[:], d[:]).then_inc(w_loaded, 16)
            sp.dma_start(dtb[:], a["dtb"][0].partition_broadcast(TOK)).then_inc(w_loaded, 16)
            sp.dma_start(aneg[:], a["alog"][0].partition_broadcast(TOK)).then_inc(w_loaded, 16)
            with sp.Fori(0, n_pairs) as g:
                sp.wait_ge(normed[1], g * NJ)
                load_scale(sp, sc, scale_dram, g, sc_in)
                with sp.Fori(0, NJ) as j:
                    i = g * NJ + j
                    for s in range(2):
                        sp.wait_ge(normed[s], i)
                        load_block(sp, xs[s], x_dram, g, j * 2 + s, x_in[s])
                with sp.Fori(0, NJ) as j:
                    i = g * NJ + j
                    for s in range(2):
                        cols = bass.ds((j * 2 + s) * CW, CW)
                        for q in range(2):
                            sp.wait_ge(bc_done[q], (i * 2 + s + 1) * 2)
                        sp.dma_start(bc_dram[g, cols].rearrange("w p c -> p w c"), bc[s][:]).then_inc(bc_out[s], 16)
                        for q in range(2):
                            sp.wait_ge(t_done[q], (i * 2 + s + 1) * 2)
                        sp.dma_start(u_dram[g, cols, :, 0:DI].rearrange("w p c -> p w c"), ut[:, s, :, 0:DI]).then_inc(ut_out[s], 16)
                    sp.wait_ge(dt_done, i + 1)
                    sp.dma_start(u_dram[g, bass.ds(j * 2 * CW, 2 * CW), :, DI:DI + 2 * N4].rearrange("w p c -> p w c"),
                                 dts[:].rearrange("p w k t h -> p w (k t h)")).then_inc(dt_out, 16)
            sp.wait_ge(z_out, 16 * n_pairs * NB)
            sp.wait_ge(dt_out, 16 * n_pairs * NJ)
            for s in range(2):
                sp.wait_ge(bc_out[s], 16 * n_pairs * NJ)
                sp.wait_ge(ut_out[s], 16 * n_pairs * NJ)

        @block.gpsimd
        def _(pool):
            pool.memset(xi[:].rearrange("p k w b h -> p (k w b h)"), 0.0).then_inc(consts, 1)
            pool.wait_ge(w_loaded, n_w)

            def convolve(g, j, s):
                i = g * NJ + j
                steps = [(what, tap) for at in range(POOL_FROM, 10) for what, tap in (("times", at), ("plus", at - 1)) if POOL_FROM <= tap < 9]
                count = lambda step: i * N_P + steps.index(step) + 1
                for what, tap in steps:
                    dh, dw = tap // 3, tap % 3
                    if what == "times":
                        if tap >= POOL_FROM + 2:
                            pool.wait_ge(p_taps[s], count(("plus", tap - 2)))
                        xin = window(1, bass.ds((j * 2 + s) * CW + dw, CW), dh)
                        ins = pool.tensor_tensor(lines(part[tap % 2][:]), xin, cw[:, 1, dh, dw:dw + 1].unsqueeze(2).to_broadcast([128, CW * PB, SIDE]), ALU.mult)
                    else:
                        if tap == POOL_FROM:
                            pool.wait_ge(c1_ready[s], (i + 1) * N_1)
                        else:
                            pool.wait_ge(p_taps[s], count(("plus", tap - 1)))
                        pool.wait_ge(p_taps[s], count(("times", tap)))
                        ins = pool.tensor_tensor(acc[s][:, 1], acc[s][:, 1], part[tap % 2][:], ALU.add)
                    ins.then_inc(p_taps[s], 1)
                pool.wait_ge(p_taps[s], (i + 1) * N_P)
                pool.sem_inc(passed, 1)

            with pool.Fori(0, n_pairs) as g:
                pool.wait_ge(sc_in, (g + 1) * 16)
                pool.sem_inc(passed, 1)
                with pool.Fori(0, NJ) as j:
                    i = g * NJ + j
                    for s in range(2):
                        pool.wait_ge(x_in[s], (i + 1) * 16)
                        pool.wait_ge(xn_read[s], i)
                        pool.sem_inc(passed, 1)
                        normalise(pool, xn[s], xs[s], sc).then_inc(normed[s], 1)
                for k in range(IK):
                    pool.wait_ge(xi_done[k], (g + 1) * NB)
                pool.sem_inc(passed, 1)
                blocks(pool, g, convolve, idle, idle, idle)

        @block.tensor
        def _(pe):
            pe.wait_ge(w_loaded, n_w)
            pe.wait_ge(consts, 1)
            pe.wait_ge(built, 2)

            def convolve(g, j, s):
                i = g * NJ + j
                pe.wait_ge(v_taps[s], i * N_V)
                pe.wait_ge(c1_ready[s], i * N_1)
                at = 0
                for k, count in PE_TAPS.items():
                    for tap in range(count):
                        dh, dw = tap // 3, tap % 3
                        ins = pe.matmul(lines(bank[2 * s + k - 1][:, 0:BLK]), taps[:, at], window(k, bass.ds((j * 2 + s) * CW + dw, CW), dh),
                                        start=(tap == 0), stop=(tap == count - 1))
                        at += 1
                ins.then_inc(c_ps[s], 1)

            def project(g, j, s, ws):
                i = g * NJ + j
                n = i * 2 + s
                if 0 in ws:
                    pe.wait_ge(u_ready[s], (i + 1) * IK)
                for w in ws:
                    q, m = w % 2, n * 2 + w // 2
                    pe.wait_ge(bc_done[q], m)
                    tok = lambda k: u[s][:, k, w * TOK:(w + 1) * TOK]
                    for k in range(IK):
                        ins = pe.matmul(bank[4 + 2 * q][0:TOK, 0:512], tok(k), wx[:, k, 0:512], start=(k == 0), stop=(k == IK - 1))
                    ins.then_inc(bc_ps[q], 1)
                    pe.wait_ge(t_done[q], m)
                    for k in range(IK):
                        pe.matmul(bank[5 + 2 * q][0:TOK, DI:DI + N4], tok(k), wx[:, k, 512:512 + N4], start=(k == 0), stop=(k == IK - 1))
                    for k in range(IK):
                        ins = pe.transpose(bank[5 + 2 * q][0:TOK, k * 128:(k + 1) * 128], tok(k), ident[:])
                    ins.then_inc(u_read[s] if w == CW - 1 else t_ps[q], 1)

            with pe.Fori(0, n_pairs) as g:
                for s in range(2):
                    pe.wait_ge(v_taps[s], g * NJ * N_V)
                    pe.wait_ge(c1_ready[s], g * NJ * N_1)
                    pe.wait_ge(bc_done[s], g * NB * 2)
                    pe.wait_ge(t_done[s], g * NB * 2)
                pe.sem_inc(passed, 1)
                with pe.Fori(0, NJ) as j:
                    i = g * NJ + j
                    for s in range(2):
                        n = i * 2 + s
                        pe.wait_ge(normed[s], i + 1)
                        rhs = lambda kc: xn[s][:, kc].rearrange("p w b h -> p (w b h)")
                        for out, ps, done, off in ((bank[0:3], xi_ps, xi_done, 0), (bank[3:6], z_ps, z_done, DI)):
                            for k in range(IK):
                                pe.wait_ge(done[k], n)
                                for kc in range(KC):
                                    ins = pe.matmul(out[k][:, 0:BLK], w_in[:, kc, off + k * 128:off + (k + 1) * 128], rhs(kc), start=(kc == 0), stop=(kc == KC - 1))
                                ins.then_inc(ps[k], 1)
                        pe.wait_ge(z_ps[IK - 1], n + 1)
                        pe.sem_inc(xn_read[s], 1)
                for k in range(IK):
                    pe.wait_ge(xi_done[k], (g + 1) * NB)
                    pe.wait_ge(z_done[k], (g + 1) * NB)
                pe.sem_inc(passed, 1)
                blocks(pe, g, convolve, project, idle, idle)

        @block.scalar
        def _(act):
            act.wait_ge(w_loaded, n_w)
            act.activation(aneg[:], aneg[:], ACT.Exp).then_inc(built, 1)

            def convolve(g, j, s):
                i = g * NJ + j
                act.wait_ge(u_read[s], i)
                act.wait_ge(v_taps[s], (i + 1) * N_V)
                for k in (0, 2):
                    act.activation(u[s][:, k], acc[s][:, k], ACT.Gelu, bias=cb[:, k:k + 1]).then_inc(u_ready[s], 1)
                act.wait_ge(p_taps[s], (i + 1) * N_P)
                act.activation(u[s][:, 1], acc[s][:, 1], ACT.Gelu, bias=cb[:, 1:2]).then_inc(u_ready[s], 1)

            def project(g, j, s, ws):
                i = g * NJ + j
                n = i * 2 + s
                if 0 in ws:
                    act.wait_ge(bc_out[s], i * 16)
                    act.wait_ge(ut_out[s], i * 16)
                    act.wait_ge(taken[s], i)
                for w in ws:
                    q, m = w % 2, n * 2 + w // 2
                    act.wait_ge(bc_ps[q], m + 1)
                    act.copy(bc[s][:, w], bank[4 + 2 * q][0:TOK, 0:512]).then_inc(bc_done[q], 1)
                    if w == CW - 1:
                        act.wait_ge(u_read[s], i + 1)
                    else:
                        act.wait_ge(t_ps[q], m + 1 if q == 0 else n + 1)
                    act.copy(ut[:, s, w], bank[5 + 2 * q][0:TOK, 0:DI + N4]).then_inc(t_done[q], 1)

            def softplus(g, j):
                i = g * NJ + j
                act.wait_ge(neg_ready, i + 1)
                act.activation(sp_["e"][:], sp_["neg"][:], ACT.Exp).then_inc(e_ready, 1)
                act.wait_ge(e_ready, i + 1)
                act.activation(sp_["ln"][:], sp_["e"][:], ACT.Ln, bias=1.0).then_inc(ln_ready, 1)

            with act.Fori(0, n_pairs) as g:
                with act.Fori(0, NJ) as j:
                    i = g * NJ + j
                    for s in range(2):
                        n = i * 2 + s
                        act.wait_ge(z_out, n * 16)
                        for k in range(IK):
                            act.wait_ge(z_ps[k], n + 1)
                            act.activation(z[:, k], bank[3 + k][:, 0:BLK], ACT.Gelu).then_inc(z_done[k], 1)
                        for k in range(IK):
                            act.wait_ge(z_done[k], n + 1)
                        act.dma_start(z_dram[g, :, :, bass.ds((j * 2 + s) * CW, CW)].rearrange("k c w b h -> c k (w b h)"), z[:]).then_inc(z_out, 16)
                blocks(act, g, convolve, project, idle, softplus, early=(0, 1))

        @block.vector
        def _(dve):
            dve.wait_ge(w_loaded, n_w)
            for at, (k, tap) in enumerate([(k, tap) for k in PE_TAPS for tap in range(PE_TAPS[k])]):
                dve.tensor_scalar(taps[:, at], ident[:], cw[:, k, tap // 3, tap % 3:tap % 3 + 1], None, ALU.mult)
            dve.wait_ge(built, 1)
            dve.tensor_scalar(aneg[:], aneg[:], -1.0, None, ALU.mult).then_inc(built, 1)
            dve.wait_ge(built, 2)
            dve.wait_ge(consts, 1)

            def convolve(g, j, s):
                i = g * NJ + j
                dve.wait_ge(u_ready[s], i * IK)
                dve.wait_ge(c_ps[s], i + 1)
                order = [(k, tap) for at in range(9) for k, tap in ((1, PE_TAPS[1] + at), (0, at), (2, PE_TAPS[2] + at)) if tap < (POOL_FROM if k == 1 else 9)]
                mine = [x for x in order if x[0] != 1]
                for k, tap in order:
                    dh, dw = tap // 3, tap % 3
                    out, xin, weight = lines(acc[s][:, k]), window(k, bass.ds((j * 2 + s) * CW + dw, CW), dh), cw[:, k, dh, dw:dw + 1]
                    if k == 1 and tap > PE_TAPS[1]:
                        dve.wait_ge(c1_ready[s], i * N_1 + tap - PE_TAPS[1])
                    elif (k, tap - 1) in mine:
                        dve.wait_ge(v_taps[s], i * N_V + mine.index((k, tap - 1)) + 1)
                    if k == 0 and tap == 0:
                        ins = dve.tensor_scalar(out, xin, weight, None, ALU.mult)
                    else:
                        before = lines(bank[2 * s + k - 1][:, 0:BLK]) if k and tap == PE_TAPS[k] else out
                        ins = dve.scalar_tensor_tensor(out=out, in0=xin, scalar=weight, in1=before, op0=ALU.mult, op1=ALU.add)
                    ins.then_inc(c1_ready[s] if k == 1 else v_taps[s], 1)

            def take(g, j, s):
                i = g * NJ + j
                for q in range(2):
                    dve.wait_ge(t_done[q], i * 4 + s * 2 + 2)
                dve.wait_ge(raw_ready, i)
                dve.tensor_tensor(sp_["t"][:, s * CW:(s + 1) * CW], ut[:, s, :, DI:DI + N4], dtb[:].unsqueeze(1).to_broadcast([TOK, CW, N4]), ALU.add).then_inc(taken[s], 1)

            def softplus(g, j):
                i = g * NJ + j
                L = 10
                base = i * L
                step = [0]

                def chain(ins):
                    step[0] += 1
                    ins.then_inc(link, 1)
                    dve.wait_ge(link, base + step[0])

                t, neg, e, ln, ser, small = (sp_[k] for k in ("t", "neg", "e", "ln", "ser", "small"))
                for s in range(2):
                    dve.wait_ge(taken[s], i + 1)
                chain(dve.tensor_scalar(neg[:], t[:], -1.0, None, ALU.mult))
                dve.tensor_tensor(neg[:], neg[:], t[:], ALU.min).then_inc(neg_ready, 1)
                dve.wait_ge(e_ready, i + 1)
                dve.tensor_scalar(small[:], e[:], 0.1, None, ALU.is_lt)
                chain(dve.tensor_scalar(ser[:], e[:], -1.0 / 6.0, None, ALU.mult))
                for c in (1.0 / 5.0, -1.0 / 4.0, 1.0 / 3.0, -1.0 / 2.0, 1.0):
                    chain(dve.scalar_tensor_tensor(out=ser[:], in0=ser[:], scalar=c, in1=e[:], op0=ALU.add, op1=ALU.mult))
                dve.wait_ge(ln_ready, i + 1)
                chain(dve.tensor_tensor(ser[:], ser[:], ln[:], ALU.subtract))
                chain(dve.tensor_tensor(ser[:], ser[:], small[:], ALU.mult))
                chain(dve.tensor_tensor(ser[:], ser[:], ln[:], ALU.add))
                assert step[0] == L
                dve.scalar_tensor_tensor(out=raw[:], in0=t[:], scalar=0.0, in1=ser[:], op0=ALU.max, op1=ALU.add).then_inc(raw_ready, 1)
                dve.wait_ge(raw_ready, i + 1)
                dve.wait_ge(dt_out, i * 16)
                split = lambda x: x.rearrange("p w (k h) -> p w k h", k=NDIR)
                for w in range(2 * CW):
                    dve.tensor_copy(dts[:, w, :, 0], split(raw[:])[:, w])
                    ins = dve.tensor_tensor(dts[:, w, :, 1], split(raw[:])[:, w], aneg[:].rearrange("p (k h) -> p k h", k=NDIR), ALU.mult)
                ins.then_inc(dt_done, 1)

            with dve.Fori(0, n_pairs) as g:
                for s in range(2):
                    dve.wait_ge(c_ps[s], g * NJ)
                    dve.wait_ge(v_taps[s], g * NJ * N_V)
                    dve.wait_ge(c1_ready[s], g * NJ * N_1)
                    dve.wait_ge(p_taps[s], g * NJ * N_P)
                dve.sem_inc(passed, 1)
                with dve.Fori(0, NJ) as j:
                    i = g * NJ + j
                    for s in range(2):
                        n = i * 2 + s
                        for k in range(IK):
                            dve.wait_ge(xi_ps[k], n + 1)
                            dve.tensor_copy(xi[:, k, bass.ds((j * 2 + s) * CW + 1, CW), :, 1:1 + SIDE].rearrange("p w b h -> p (w b) h"),
                                            bank[k][:, 0:BLK].rearrange("p (w b h) -> p (w b) h", w=CW, b=PB)).then_inc(xi_done[k], 1)
                for k in range(IK):
                    dve.wait_ge(xi_done[k], (g + 1) * NB)
                dve.sem_inc(passed, 1)
                blocks(dve, g, convolve, idle, take, softplus)


def scans(nc, a, u_dram, bc_dram, y_drams, n_pairs):
    with ExitStack() as ctx:
        S = Scope(nc, ctx, "sc")
        passed = S.sem("passed")
        UC = DI + NDIR * 2 * HEADS
        ident = S.sb("ident", [128, 128])
        later = S.sb2("later", [128, 128])
        upto = S.sb2("upto", [128, 128])
        seen = S.sb2("seen", [128, SIDE])
        same = S.sb("same", [128, 128])
        u = S.sb2("u", [128, UC], NDIR)
        bz = S.sb2("bz", [128, 2, PB, NS], NDIR)
        state = S.sb2("state", [128, DI], NDIR)
        w = S.sb2("w", [128, HEADS, SIDE])
        xdt = S.sb2("xdt", [128, DI])
        xbd = S.sb2("xbd", [128, HEADS, PB, HP])
        xdd = S.sb2("xdd", [128, DI])
        e = S.sb2("e", [128, HEADS, SIDE])
        m_ = S.sb2("m", [128, HEADS, SIDE])
        bct = S.sb2("bct", [128, 2, 128])
        ctc = S.sb2("ctc", [128, SIDE])
        ecum = S.sb2("ecum", [128, 2 * HEADS])
        gm = S.sb2("gm", [128, SIDE])
        toff = S.sb2("toff", [128, DI])
        y = S.sb2("y", [128, DI])
        HH = HEADS // 2
        diff_ps = S.ps("diff", [128, 2, 512])
        misc_ps = S.ps("misc", [128, 512])
        off_ps, st_ps, yd_ps = S.ps("off", [128, 512]), S.ps("st", [128, 512]), S.ps("yd", [SIDE, 2, 512])
        c_in, zero, s_init = S.sem("c_in"), S.sem("zero"), S.sem("s_init")
        loaded, st_ready, s_ready = (S.sem2(n, NDIR) for n in ("loaded", "st_ready", "s_ready"))
        w_ready, xdt_ready, xbd_ready, tr, diff_ready, e_ready, xdd_ready, m_ready = (
            S.sem2(n) for n in ("w_ready", "xdt_ready", "xbd_ready", "tr", "diff_ready", "e_ready", "xdd_ready", "m_ready"))
        off_ready, toff_ready, scd_ready, yd_ready, y_ready, stored = (
            S.sem2(n) for n in ("off_ready", "toff_ready", "scd_ready", "yd_ready", "y_ready", "stored"))
        bct_ready, ecum_ready, ctc_ready, g_ready, gm_ready = (
            S.sem(n) for n in ("bct_ready", "ecum_ready", "ctc_ready", "g_ready", "gm_ready"))
        block = ctx.enter_context(nc.Block())
        STEPS = SIDE
        heads = lambda t: t.rearrange("p (h c) -> p h c", h=HEADS)
        per_head = lambda t, n: t.unsqueeze(2).to_broadcast([128, HEADS, n])
        dt_of = lambda k: u[k][:, DI + k * 2 * HEADS:DI + k * 2 * HEADS + HEADS]
        da_of = lambda k: u[k][:, DI + k * 2 * HEADS + HEADS:DI + (k + 1) * 2 * HEADS]
        back = lambda k: k // 2

        def chunk(ten, g, k, c, b):
            at = (STEPS - 1) - c if back(k) else c
            if k % 2:
                return ten[g, at, b * SIDE:(b + 1) * SIDE]
            return ten[g, :, b * SIDE + at]

        def slot(t, k):
            return k % 2, t * 2 + k // 2

        def before(t, k):
            return (1 - k % 2, t * 2 + k // 2 + (k % 2))

        def run(eng, first, second, start=None):
            with eng.Fori(0, n_pairs) as g:
                if start:
                    start(g)
                first(g, 0, 0)
                with eng.Fori(0, STEPS - 1) as c:
                    for k in range(NDIR):
                        first(g, c + (k + 1) // NDIR, (k + 1) % NDIR)
                        second(g, c, k)
                for k in range(NDIR):
                    if k + 1 < NDIR:
                        first(g, STEPS - 1, k + 1)
                    second(g, STEPS - 1, k)

        @block.sync
        def _(sp):
            for t, d in ((ident, a["ident"][:]), (later[0], a["later"][0]), (later[1], a["later"][1]), (upto[0], a["upto"][0]),
                         (upto[1], a["upto"][1]), (seen[0], a["seen"][0]), (seen[1], a["seen"][1]), (same, a["same"][:])):
                sp.dma_start(t[:], d).then_inc(c_in, 16)
            sp.wait_ge(zero, 2 * NDIR + 2)

            def load(g, c, k):
                t = g * STEPS + c
                sp.wait_ge(st_ready[k], t)
                sp.sem_inc(passed, 1)
                for b in range(PB):
                    rows = slice(b * 64, b * 64 + SIDE)
                    sp.dma_start(u[k][rows], chunk(u_dram, g, k, c, b)).then_inc(loaded[k], 16)
                    sp.dma_start(bz[k][rows, :, b], chunk(bc_dram, g, k, c, b)[:, k * 2 * NS:(k + 1) * 2 * NS].rearrange("p (s n) -> p s n", s=2)).then_inc(loaded[k], 16)

            def store(g, c, k):
                p, m = slot(g * STEPS + c, k)
                sp.wait_ge(y_ready[p], m + 1)
                sp.sem_inc(passed, 1)
                for b in range(PB):
                    sp.dma_start(chunk(y_drams[k], g, k, c, b), y[p][b * 64:b * 64 + SIDE]).then_inc(stored[p], 16)

            with sp.Fori(0, n_pairs) as g:
                for k in range(NDIR):
                    load(g, 0, k)
                with sp.Fori(0, STEPS - 1) as c:
                    for k in range(NDIR):
                        store(g, c, k)
                        load(g, c + 1, k)
                for k in range(NDIR):
                    store(g, STEPS - 1, k)
            for p in range(2):
                sp.wait_ge(stored[p], n_pairs * STEPS * 2 * 32)

        @block.gpsimd
        def _(pool):
            for k in range(NDIR):
                pool.memset(u[k][:], 0.0).then_inc(zero, 1)
                pool.memset(bz[k][:], 0.0).then_inc(zero, 1)
            for p in range(2):
                pool.memset(xbd[p][:], 0.0).then_inc(zero, 1)
            pool.wait_ge(c_in, 16 * 8)

            def start(g):
                for k in range(NDIR):
                    pool.wait_ge(s_ready[k], g * STEPS)
                pool.sem_inc(passed, 1)
                for k in range(NDIR):
                    pool.memset(state[k][:], 0.0).then_inc(s_init, 1)

            def first(g, c, k):
                t = g * STEPS + c
                p, m = slot(t, k)
                pool.wait_ge(loaded[k], (t + 1) * 64)
                pool.wait_ge(diff_ready[p], m)
                pool.tensor_tensor(w[p][:], per_head(da_of(k), SIDE), seen[back(k)][:].unsqueeze(1).to_broadcast([128, HEADS, SIDE]), ALU.mult).then_inc(w_ready[p], 1)
                pool.wait_ge(xbd_ready[p], m)
                pool.wait_ge(xdd_ready[p], m)
                pool.tensor_tensor(heads(xdt[p][:]), heads(u[k][:, 0:DI]), per_head(dt_of(k), HP), ALU.mult).then_inc(xdt_ready[p], 1)

            def second(g, c, k):
                t = g * STEPS + c
                p, m = slot(t, k)
                pool.wait_ge(s_init, (g + 1) * NDIR)
                pool.wait_ge(s_ready[k], t)
                pool.wait_ge(ecum_ready, t * NDIR + k + 1)
                pool.wait_ge(off_ready[p], m + 1)
                pool.tensor_tensor(heads(state[k][:]), heads(state[k][:]), per_head(ecum[p][:, HEADS:], HP), ALU.mult).then_inc(scd_ready[p], 1)

            run(pool, first, second, start)

        @block.tensor
        def _(pe):
            pe.wait_ge(c_in, 16 * 8)

            def first(g, c, k):
                t = g * STEPS + c
                n = t * NDIR + k
                p, m = slot(t, k)
                pe.wait_ge(loaded[k], (t + 1) * 64)
                pe.wait_ge(gm_ready, n)
                pe.transpose(misc_ps[:, 0:128], bz[k][:, 0].rearrange("p b n -> p (b n)"), ident[:])
                pe.transpose(misc_ps[:, 128:256], bz[k][:, 1].rearrange("p b n -> p (b n)"), ident[:])
                pe.matmul(misc_ps[:, 256:256 + HEADS], upto[back(k)][:], da_of(k), start=True, stop=True)
                pe.matmul(misc_ps[:, 256 + HEADS:256 + 2 * HEADS], same[:], da_of(k), start=True, stop=True).then_inc(tr[p], 1)
                pe.wait_ge(w_ready[p], m + 1)
                q, mq = before(t, k)
                pe.wait_ge(e_ready[q], mq)
                for half in range(2):
                    ins = pe.matmul(diff_ps[:, half, 0:HH * SIDE], later[back(k)][:],
                                    w[p][:, half * HH:(half + 1) * HH].rearrange("p h q -> p (h q)"), start=True, stop=True)
                ins.then_inc(diff_ready[p], 1)
                pe.wait_ge(bct_ready, n + 1)
                pe.wait_ge(ecum_ready, n + 1)
                pe.wait_ge(ctc_ready, n + 1)
                pe.matmul(misc_ps[:, 288:288 + SIDE], bct[p][:, 0], ctc[p][:], start=True, stop=True).then_inc(g_ready, 1)

            def second(g, c, k):
                t = g * STEPS + c
                p, m = slot(t, k)
                q, mq = before(t, k)
                pe.wait_ge(s_init, (g + 1) * NDIR)
                pe.wait_ge(s_ready[k], t)
                pe.wait_ge(toff_ready[q], mq)
                pe.matmul(off_ps[:, 0:DI], bct[p][:, 1], state[k][:], start=True, stop=True).then_inc(off_ready[p], 1)
                pe.wait_ge(xdd_ready[p], m + 1)
                pe.wait_ge(s_ready[(k - 1) % NDIR], t + (1 if k else 0))
                pe.matmul(st_ps[:, 0:DI], bz[k][:, 0].rearrange("p b n -> p (b n)"), xdd[p][:], start=True, stop=True).then_inc(st_ready[k], 1)
                pe.wait_ge(xbd_ready[p], m + 1)
                pe.wait_ge(m_ready[p], m + 1)
                pe.wait_ge(y_ready[q], mq)
                pe.sem_inc(passed, 1)
                for h in range(HEADS):
                    ins = pe.matmul(yd_ps[:, h // HH, h % HH * PB * HP:(h % HH + 1) * PB * HP], m_[p][:, h], xbd[p][:, h].rearrange("p b c -> p (b c)"),
                                    start=True, stop=True)
                ins.then_inc(yd_ready[p], 1)

            run(pe, first, second)

        @block.scalar
        def _(act):
            def first(g, c, k):
                t = g * STEPS + c
                n = t * NDIR + k
                p, m = slot(t, k)
                act.wait_ge(tr[p], m + 1)
                act.wait_ge(off_ready[p], m)
                act.copy(bct[p][:].rearrange("p s n -> p (s n)"), misc_ps[:, 0:256]).then_inc(bct_ready, 1)
                act.wait_ge(toff_ready[p], m)
                act.wait_ge(scd_ready[p], m)
                act.activation(ecum[p][:], misc_ps[:, 256:256 + 2 * HEADS], ACT.Exp).then_inc(ecum_ready, 1)
                act.wait_ge(diff_ready[p], m + 1)
                act.wait_ge(m_ready[p], m)
                act.wait_ge(xdd_ready[p], m)
                act.activation(e[p][:].rearrange("p (t h) q -> p t (h q)", t=2), diff_ps[:, :, 0:HH * SIDE], ACT.Exp).then_inc(e_ready[p], 1)
                act.wait_ge(xdt_ready[p], m + 1)
                act.wait_ge(yd_ready[p], m)
                for b in range(PB):
                    rows = slice(b * 64, (b + 1) * 64)
                    ins = act.copy(xbd[p][rows, :, b], heads(xdt[p][rows]))
                ins.then_inc(xbd_ready[p], 1)

            run(act, first, lambda g, c, k: None)

        @block.vector
        def _(dve):
            dve.wait_ge(c_in, 16 * 8)

            def first(g, c, k):
                t = g * STEPS + c
                n = t * NDIR + k
                p, m = slot(t, k)
                dve.wait_ge(bct_ready, n + 1)
                dve.tensor_copy(ctc[p][0:64], bct[p][0:64, 1, 0:SIDE])
                dve.tensor_copy(ctc[p][64:128], bct[p][64:128, 1, 64:64 + SIDE]).then_inc(ctc_ready, 1)
                dve.wait_ge(g_ready, n + 1)
                dve.tensor_tensor(gm[p][:], misc_ps[:, 288:288 + SIDE], seen[back(k)][:], ALU.mult).then_inc(gm_ready, 1)
                dve.wait_ge(e_ready[p], m + 1)
                dve.wait_ge(xdt_ready[p], m + 1)
                last = 0 if back(k) else SIDE - 1
                dve.tensor_tensor(heads(xdd[p][:]), heads(xdt[p][:]), per_head(e[p][:, :, last], HP), ALU.mult).then_inc(xdd_ready[p], 1)
                dve.wait_ge(gm_ready, n + 1)
                dve.tensor_tensor(m_[p][:], e[p][:], gm[p][:].unsqueeze(1).to_broadcast([128, HEADS, SIDE]), ALU.mult).then_inc(m_ready[p], 1)

            def second(g, c, k):
                t = g * STEPS + c
                p, m = slot(t, k)
                dve.wait_ge(off_ready[p], m + 1)
                dve.wait_ge(ecum_ready, t * NDIR + k + 1)
                dve.tensor_tensor(heads(toff[p][:]), heads(off_ps[:, 0:DI]), per_head(ecum[p][:, 0:HEADS], HP), ALU.mult).then_inc(toff_ready[p], 1)
                dve.wait_ge(scd_ready[p], m + 1)
                dve.wait_ge(st_ready[k], t + 1)
                dve.tensor_tensor(state[k][:], st_ps[:, 0:DI], state[k][:], ALU.add).then_inc(s_ready[k], 1)
                dve.wait_ge(yd_ready[p], m + 1)
                dve.wait_ge(toff_ready[p], m + 1)
                dve.wait_ge(stored[p], m * 32)
                for b in range(PB):
                    rows = slice(b * 64, b * 64 + SIDE)
                    banks = lambda x: x.rearrange("q (t h c) -> q t h c", t=2, h=HH)
                    ins = dve.tensor_tensor(banks(y[p][rows]), yd_ps[:, :, 0:HH * PB * HP].rearrange("q t (h b c) -> q t h b c", h=HH, b=PB)[:, :, :, b],
                                            banks(toff[p][rows]), ALU.add)
                ins.then_inc(y_ready[p], 1)

            run(dve, first, second)


def scan_out(nc, a, x_dram, z_dram, u_dram, y_drams, out, n_pairs):
    with ExitStack() as ctx:
        S = Scope(nc, ctx, "so")
        passed = S.sem("passed")
        UC = DI + NDIR * 2 * HEADS
        ident = S.sb("ident", [128, 128])
        dsk = S.sb("dsk", [TOK, NDIR, DI])
        ng, nb = S.sb("ng", [128, IK]), S.sb("nb", [128, IK])
        wo = S.sb("wo", [128, IK, C])
        eps = S.sb("eps", [TOK, 1])
        u = S.sb2("u", [TOK, CW, DI])
        ys = [S.sb2(f"y{s}", [TOK, CW, DI], NDIR) for s in range(2)]
        skip = S.sb("skip", [TOK, CW, DI])
        acc = S.sb("acc", [TOK, CW, DI])
        nrm = S.sb2("nrm", [TOK, CW, DI])
        stats = S.sb("stats", [TOK, CW, 6])
        mv = S.sb("mv", [TOK, CW, 2])
        std = S.sb("std", [TOK, CW])
        rstd = S.sb("rstd", [TOK, CW])
        z = S.sb2("z", [128, IK, BLK])
        x = S.sb2("x", [CP, KC, BLK])
        g_ = S.sb("g", [128, IK, BLK])
        o = S.sb2("o", [CP, KC, BLK])
        t_ps = [[S.ps(f"tps{s}{k}", [128, BLK]) for k in range(IK)] for s in range(2)]
        o_ps = [S.ps(f"ops{k}", [CP, BLK]) for k in range(KC)]
        c_in, built, eps_ready = S.sem("c_in"), S.sem("built"), S.sem("eps_ready")
        in_, xz_in, stored = (S.sem2(n) for n in ("in", "xz_in", "stored"))
        part_sum, link, mv_ready, std_ready, nrm_ready = (S.sem(n) for n in ("part_sum", "link", "mv_ready", "std_ready", "nrm_ready"))
        sum_all = S.sem2("sum_all")
        turned_s = S.sem2("turned")
        aff_ready, g_ready = S.sem2("aff", IK), S.sem2("g_ready", IK)
        o_psr, o_ready, xz_free = S.sem2("o_psr", KC), S.sem2("o_ready", KC), S.sem2("xz_free")
        block = ctx.enter_context(nc.Block())
        NJ = NB // 2
        ROUNDS = n_pairs * NJ

        def blocks(eng, first, second):
            first(0, 0)
            with eng.Fori(0, ROUNDS - 1) as i:
                first(i, 1)
                second(i, 0)
                first(i + 1, 0)
                second(i, 1)
            first(ROUNDS - 1, 1)
            second(ROUNDS - 1, 0)
            second(ROUNDS - 1, 1)

        @block.sync
        def _(sp):
            for t, d in ((ident, a["ident"][:]), (ng, a["ng"][:]), (nb, a["nb"][:]), (wo, a["w_out"][:])):
                sp.dma_start(t[:], d).then_inc(c_in, 16)
            sp.dma_start(dsk[:], a["ds"][0].partition_broadcast(TOK)).then_inc(c_in, 16)

            def load_scans(i, s):
                g, cols = i // NJ, bass.ds((i % NJ * 2 + s) * CW, CW)
                sp.wait_ge(sum_all[s], i)
                for k in range(NDIR):
                    sp.dma_start(ys[s][k][:], y_drams[k][g, cols].rearrange("w p c -> p w c")).then_inc(in_[s], 16)
                sp.dma_start(u[s][:], u_dram[g, cols, :, 0:DI].rearrange("w p c -> p w c")).then_inc(in_[s], 16)

            def load_gate(i, s):
                g, cols = i // NJ, bass.ds((i % NJ * 2 + s) * CW, CW)
                sp.wait_ge(xz_free[s], i)
                sp.dma_start(z[s][:], z_dram[g, :, :, cols].rearrange("k c w b h -> c k (w b h)")).then_inc(xz_in[s], 16)
                sp.dma_start(x[s][:], x_dram[g, :, :, cols].rearrange("k c w b h -> c k (w b h)")).then_inc(xz_in[s], 16)

            blocks(sp, load_scans, load_gate)

        @block.gpsimd
        def _(pool):
            pool.memset(eps[:], LN_EPS).then_inc(eps_ready, 1)
            pool.wait_ge(built, 3)
            with pool.Fori(0, n_pairs * NJ) as i:
                for s in range(2):
                    n = i * 2 + s
                    pool.wait_ge(in_[s], (i + 1) * 80)
                    pool.wait_ge(sum_all[1 - s], i + s)
                    pool.tensor_tensor(skip[:], u[s][:], dsk[:, 0].unsqueeze(1).to_broadcast([TOK, CW, DI]), ALU.mult).then_inc(part_sum, 1)
                    for k in (2, 3):
                        pool.wait_ge(part_sum, n * 3 + k - 1)
                        pool.tensor_tensor(skip[:], skip[:], ys[s][k][:], ALU.add).then_inc(part_sum, 1)

        @block.vector
        def _(dve):
            dve.wait_ge(c_in, 80)
            for k in range(1, NDIR):
                dve.tensor_tensor(dsk[:, 0], dsk[:, 0], dsk[:, k], ALU.add).then_inc(built, 1)
                dve.wait_ge(built, k)

            def sums(i, s):
                n = i * 2 + s
                L = 5
                step = [0]

                def chain(ins):
                    step[0] += 1
                    ins.then_inc(link, 1)
                    dve.wait_ge(link, n * L + step[0])

                dve.wait_ge(in_[s], (i + 1) * 80)
                chain(dve.tensor_tensor(acc[:], ys[s][0][:], ys[s][1][:], ALU.add))
                dve.wait_ge(part_sum, (n + 1) * 3)
                chain(dve.tensor_tensor(acc[:], acc[:], skip[:], ALU.add))
                dve.sem_inc(sum_all[s], 1)
                for w in range(CW):
                    ins = dve.bn_stats(stats[:, w], acc[:, w])
                chain(ins)
                dve.sem_inc(passed, 1)
                for w in range(CW):
                    ins = dve.bn_aggr(mv[:, w], stats[:, w])
                ins.then_inc(mv_ready, 1)
                dve.wait_ge(std_ready, n + 1)
                chain(dve.reciprocal(rstd[:], std[:]))
                dve.wait_ge(turned_s[s], i)
                for w in range(CW):
                    ins = dve.tensor_scalar(nrm[s][:, w], acc[:, w], mv[:, w, 0:1], rstd[:, w:w + 1], ALU.subtract, ALU.mult)
                chain(ins)
                assert step[0] == L
                dve.sem_inc(nrm_ready, 1)

            def gate(i, s):
                n = i * 2 + s
                dve.wait_ge(xz_in[s], (i + 1) * 32)
                for k in range(IK):
                    dve.wait_ge(aff_ready[k], n + 1)
                    dve.tensor_tensor(g_[:, k], g_[:, k], z[s][:, k], ALU.mult).then_inc(g_ready[k], 1)
                dve.wait_ge(stored[s], i * 16)
                for oc in range(KC):
                    dve.wait_ge(o_psr[oc], n + 1)
                    dve.tensor_tensor(o[s][:, oc], o_ps[oc][:], x[s][:, oc], ALU.add).then_inc(o_ready[oc], 1)
                dve.wait_ge(o_ready[KC - 1], n + 1)
                dve.sem_inc(xz_free[s], 1)

            blocks(dve, sums, gate)

        @block.tensor
        def _(pe):
            pe.wait_ge(c_in, 80)

            def turn(i, s):
                pe.wait_ge(nrm_ready, i * 2 + s + 1)
                for k in range(IK):
                    pe.wait_ge(aff_ready[k], i * 2)
                pe.sem_inc(passed, 1)
                for k in range(IK):
                    for w in range(CW):
                        ins = pe.transpose(t_ps[s][k][:, w * TOK:(w + 1) * TOK], nrm[s][:, w, k * 128:(k + 1) * 128], ident[0:TOK, 0:TOK])
                ins.then_inc(turned_s[s], 1)

            def project(i, s):
                n = i * 2 + s
                for k in range(IK):
                    pe.wait_ge(g_ready[k], n + 1)
                for oc in range(KC):
                    pe.wait_ge(o_ready[oc], n)
                    for k in range(IK):
                        ins = pe.matmul(o_ps[oc][:], wo[:, k, oc * CP:(oc + 1) * CP], g_[:, k], start=(k == 0), stop=(k == IK - 1))
                    ins.then_inc(o_psr[oc], 1)

            blocks(pe, turn, project)

        @block.scalar
        def _(act):
            act.wait_ge(c_in, 80)
            act.wait_ge(eps_ready, 1)

            def affine(i, s):
                n = i * 2 + s
                act.wait_ge(mv_ready, n + 1)
                act.activation(std[:], mv[:, :, 1], ACT.Sqrt, bias=eps[:, 0:1]).then_inc(std_ready, 1)
                act.wait_ge(turned_s[s], i + 1)
                for oc in range(KC):
                    act.wait_ge(o_psr[oc], n)
                for k in range(IK):
                    act.activation(g_[:, k], t_ps[s][k][:], ACT.Identity, bias=nb[:, k:k + 1], scale=ng[:, k:k + 1]).then_inc(aff_ready[k], 1)

            def store(i, s):
                n = i * 2 + s
                for oc in range(KC):
                    act.wait_ge(o_ready[oc], n + 1)
                g, j = i // NJ, i % NJ
                act.dma_start(out[g, :, :, bass.ds((j * 2 + s) * CW, CW)].rearrange("k c w b h -> c k (w b h)"), o[s][:]).then_inc(stored[s], 16)

            blocks(act, affine, store)
            for s in range(2):
                act.wait_ge(stored[s], 16 * n_pairs * NJ)


def build(nc, a, out, n_pairs):
    d = lambda n, s: nc.dram_tensor(n, s, F32, kind="Internal").ap()
    scale1, scale2 = d("scale1", (n_pairs, CP, KC * PB, 2)), d("scale2", (n_pairs, CP, KC * PB, 2))
    lag_tables, toeplitz = d("lag_tables", (2, D1, LAGS)), d("toeplitz", (2, SIDE, D1, SIDE))
    gated, mixed = d("gated", (n_pairs, TOK, SIDE, D1)), d("mixed", (n_pairs, SIDE, TOK, D1))
    x2 = d("x2", (n_pairs, KC, CP, SIDE, PB, SIDE))
    z = d("z", (n_pairs, IK, 128, SIDE, PB, SIDE))
    u = d("u", (n_pairs, SIDE, TOK, DI + NDIR * 2 * HEADS))
    bc = d("bc", (n_pairs, SIDE, TOK, NDIR * 2 * NS))
    ys = [d(f"y{k}", (n_pairs, SIDE, TOK, DI)) for k in range(NDIR)]
    toeplitz_tables(nc, a, a["lag"], lag_tables, toeplitz)
    gn_stats(nc, "gn1", a["x"], scale1, a["gavg"], n_pairs)
    mixer_qv(nc, a["x"], scale1, a["wqv"], gated, n_pairs)
    mixer_toeplitz(nc, gated, toeplitz, a["ident"], mixed, n_pairs)
    mixer_out(nc, a["x"], scale1, mixed, a["wp"], a["pb"], a["wo"], a["ob"], a["ident"], x2, n_pairs)
    gn_stats(nc, "gn2", x2, scale2, a["gavg"], n_pairs)
    scan_inputs(nc, x2, scale2, a, z, u, bc, n_pairs)
    scans(nc, a, u, bc, ys, n_pairs)
    scan_out(nc, a, x2, z, u, ys, out, n_pairs)


def lay_out_inputs(n):
    f = lambda k: np.ascontiguousarray(np.asarray(n[k]))
    x = f("x")
    pairs = x.shape[0] // PB
    arr = {}
    arr["x"] = x.reshape(pairs, PB, SIDE, SIDE, KC, CP).transpose(0, 4, 5, 3, 1, 2)
    qv = np.zeros((CP + 1, KC, 2 * D1), x.dtype)
    qv[:CP] = np.concatenate([f("L0_conv_q_w"), f("L0_conv_v_w")], 0).T.reshape(KC, CP, 2 * D1).transpose(1, 0, 2)
    qv[CP, KC - 1] = np.concatenate([f("L0_conv_q_b"), f("L0_conv_v_b")])
    arr["wqv"] = qv
    arr["wp"] = f("L0_conv_p_w").T.reshape(KC, CP, D1).transpose(1, 0, 2)
    arr["pb"] = f("L0_conv_p_b").reshape(DC, CP).T
    arr["wo"] = f("L0_conv_o_w").T.reshape(DC, CP, C).transpose(1, 0, 2)
    arr["ob"] = f("L0_conv_o_b").reshape(KC, CP).T
    arr["slope"] = f("L0_conv_slope").reshape(DC, CP).T
    t = lambda k: [f(f"L0_conv_t{i}_{k}") for i in (1, 2)]
    arr["t_w0"] = np.stack([np.stack([w[:, 0], b], 1) for w, b in zip(t("w0"), t("b0"))], 1)
    arr["t_ws"] = np.stack([w.transpose(0, 2, 1) for w in t("ws")])
    arr["t_bs"] = np.stack([b.T for b in t("bs")], 1)
    arr["t_wo"] = np.stack([w.T for w in t("wo")])
    arr["t_bo"] = np.stack([b.reshape(DC, CP).T for b in t("bo")], 1)
    arr["w_in"] = f("L1_conv_in_proj_w").T.reshape(KC, CP, 2 * DI).transpose(1, 0, 2)
    arr["cw"] = f("L1_conv_conv_w").reshape(IK, 128, 3, 3).transpose(1, 0, 2, 3)
    arr["cb"] = f("L1_conv_conv_b").reshape(IK, 128).T
    xp = f("L1_conv_x_proj_w")
    bc = xp[:, HEADS:].reshape(NDIR * 2 * NS, DI)
    dts = xp[:, :HEADS].reshape(NDIR * HEADS, DI)
    arr["wx"] = np.concatenate([bc, dts], 0).T.reshape(IK, 128, -1).transpose(1, 0, 2)
    arr["alog"] = f("L1_conv_A_logs").reshape(1, -1)
    arr["dtb"] = f("L1_conv_dt_bias").reshape(1, -1)
    arr["ds"] = f("L1_conv_Ds").reshape(1, NDIR, DI)
    arr["ng"] = f("L1_conv_out_norm_g").reshape(IK, 128).T
    arr["nb"] = f("L1_conv_out_norm_b").reshape(IK, 128).T
    arr["w_out"] = f("L1_conv_out_proj_w").T.reshape(IK, 128, C).transpose(1, 0, 2)
    lag = np.arange(-(SIDE - 1), SIDE, dtype=np.float32)
    arr["lag"] = np.stack([np.where(lag >= 0, lag, -(SIDE + lag)), np.abs(lag)])
    c = np.arange(CP)
    arr["gavg"] = (c[:, None] // 6 == c[None] // 6).astype(np.float32) / np.float32(6)
    arr["ident"] = np.eye(128, dtype=np.float32)
    i = np.arange(128)
    same = (i[:, None] // 64 == i[None] // 64)
    pos = i % 64
    q = np.arange(SIDE)
    arr["later"] = np.stack([same & (pos[:, None] > pos[None]), same & (pos[:, None] < pos[None])]).astype(np.float32)
    arr["upto"] = np.stack([same & (pos[:, None] <= pos[None]), same & (pos[:, None] >= pos[None])]).astype(np.float32)
    arr["seen"] = np.stack([pos[:, None] <= q[None], pos[:, None] >= q[None]]).astype(np.float32)
    arr["same"] = same.astype(np.float32)
    return {k: np.ascontiguousarray(v) for k, v in arr.items()}


def kernel(**inputs):
    import concourse.bacc as _bacc
    from concourse.bass_utils import run_bass_kernel_spmd as _run

    arrays = lay_out_inputs(inputs)
    nc = _bacc.Bacc("TRN2", target_bir_lowering=False, num_devices=1)
    aps = {k: nc.dram_tensor(k, v.shape, F32, kind="ExternalInput").ap() for k, v in arrays.items()}
    n_pairs = arrays["x"].shape[0]
    out = nc.dram_tensor("out", (n_pairs, KC, CP, SIDE, PB, SIDE), F32, kind="ExternalOutput").ap()
    build(nc, aps, out, n_pairs)
    r = _run(nc, [arrays], core_ids=[0])
    got = r.results[0]["out"]
    return got.transpose(0, 4, 5, 3, 1, 2).reshape(n_pairs * PB, SIDE, SIDE, C)
```

```python
from contextlib import ExitStack

import numpy as np
import concourse.bass as bass
from concourse import mybir

F32 = mybir.dt.float32
BF16 = mybir.dt.bfloat16
F32R = mybir.dt.float32r
I32 = mybir.dt.int32
ALU = mybir.AluOpType
ACT = mybir.ActivationFunctionType

PB = 2
SIDE = 56
TOK = PB * SIDE
C = 192
KC = 2
CP = C // KC
D1 = 576
DC = D1 // CP
LAGS = 2 * SIDE - 1
CW = 4
BLK = CW * TOK
NB = SIDE // CW
GC = 8
DI = 384
IK = DI // 128
NDIR = 4
HEADS = 12
HP = DI // HEADS
NS = 64
REC = 5
DT, DA_HIGH, DA_LOW, DA_REST, DA_REST2 = range(REC)
DT0 = lambda k: DI + k * REC * HEADS
GN_EPS = 1e-5
LN_EPS = 1e-5


class Scope:

    def __init__(self, nc, ctx, name):
        self.nc, self.ctx, self.name = nc, ctx, name
        self.sems = []
        ctx.callback(self.clear)

    def clear(self):
        self.nc.clear_and_free_semaphores(self.sems)
        self.nc.all_engine_barrier()

    def sb(self, name, shape, dtype=F32):
        return self.ctx.enter_context(self.nc.sbuf_tensor(f"{self.name}_{name}", shape, dtype))

    def sb2(self, name, shape, n=2, dtype=F32):
        return [self.sb(f"{name}{i}", shape, dtype) for i in range(n)]

    def ps(self, name, shape):
        return self.ctx.enter_context(self.nc.psum_tensor(f"{self.name}_{name}", shape, F32))

    def sem(self, name):
        self.sems.append(self.nc.alloc_semaphore(name=f"{self.name}_{name}"))
        return self.sems[-1]

    def sem2(self, name, n=2):
        return [self.sem(f"{name}{i}") for i in range(n)]




def gn_stats(nc, name, src, scale_dram, group_avg, n_pairs):
    with ExitStack() as ctx:
        S = Scope(nc, ctx, name)
        sb, sem = S.sb, S.sem
        x = S.sb2("x", [CP, KC, SIDE, PB, SIDE])
        gavg = sb("gavg", [CP, CP])
        stats = sb("stats", [CP, KC, PB, NB // 2, 6])
        mv = sb("mv", [CP, KC * PB, 2])
        mom = sb("mom", [CP, KC * PB, 2])
        grp = sb("grp", [CP, KC * PB, 2])
        var = sb("var", [CP, KC * PB])
        std = sb("std", [CP, KC * PB])
        sc = sb("sc", [CP, KC * PB, 2])
        grp_ps = ctx.enter_context(nc.psum_tensor(f"{name}_ps", [CP, KC * PB * 2], F32))
        gavg_in, x_in, x_used = sem("gavg_in"), S.sem2("x_in"), S.sem2("x_used")
        passed = sem("passed")
        stat, mom_ready, grp_ready, var_ready, std_ready, sc_ready, sc_out = (
            sem(n) for n in ("stat", "mom", "grpr", "varr", "stdr", "scr", "sco"))
        block = ctx.enter_context(nc.Block())
        HALF = SIDE // 2

        @block.sync
        def _(sp):
            sp.dma_start(gavg[:], group_avg[:]).then_inc(gavg_in, 16)

            with sp.Fori(0, n_pairs // 2) as i:
                for s in range(2):
                    sp.wait_ge(x_used[s], i)
                    for kc in range(KC):
                        for half in range(2):
                            part = slice(half * HALF, (half + 1) * HALF)
                            sp.dma_start(x[s][:, kc, part], src[i * 2 + s, kc, :, part]).then_inc(x_in[s], 16)

        @block.vector
        def _(dve):
            def pair(i, s):
                g = i * 2 + s
                dve.wait_ge(x_in[s], (i + 1) * 64)
                for kc in range(KC):
                    for b in range(PB):
                        for j in range(7):
                            ins = dve.bn_stats(stats[:, kc, b, j], x[s][:, kc, j * 8:j * 8 + 8, b])
                ins.then_inc(x_used[s], 1)
                dve.wait_ge(x_used[s], i + 1)
                dve.sem_inc(passed, 1)
                for kb in range(KC * PB):
                    ins = dve.bn_aggr(mv[:, kb], stats[:, kb // PB, kb % PB].rearrange("c j s -> c (j s)"))
                ins.then_inc(stat, 1)
                dve.wait_ge(stat, g * 4 + 1)
                dve.tensor_tensor(mom[:, :, 1], mv[:, :, 0], mv[:, :, 0], ALU.mult).then_inc(stat, 1)
                dve.wait_ge(stat, g * 4 + 2)
                dve.tensor_tensor(mom[:, :, 1], mom[:, :, 1], mv[:, :, 1], ALU.add)
                dve.tensor_copy(mom[:, :, 0], mv[:, :, 0]).then_inc(mom_ready, 1)
                dve.wait_ge(grp_ready, g + 1)
                dve.tensor_copy(grp[:].rearrange("c k s -> c (k s)"), grp_ps[:]).then_inc(stat, 1)
                dve.wait_ge(stat, g * 4 + 3)
                dve.tensor_tensor(var[:], grp[:, :, 0], grp[:, :, 0], ALU.mult).then_inc(stat, 1)
                dve.wait_ge(stat, g * 4 + 4)
                dve.scalar_tensor_tensor(out=var[:], in0=grp[:, :, 1], scalar=GN_EPS, in1=var[:], op0=ALU.add, op1=ALU.subtract).then_inc(var_ready, 1)
                dve.wait_ge(std_ready, g + 1)
                dve.wait_ge(sc_out, g * 16)
                dve.reciprocal(sc[:, :, 0], std[:]).then_inc(sc_ready, 1)
                dve.wait_ge(sc_ready, g * 2 + 1)
                dve.scalar_tensor_tensor(out=sc[:, :, 1], in0=grp[:, :, 0], scalar=-1.0, in1=sc[:, :, 0], op0=ALU.mult, op1=ALU.mult).then_inc(sc_ready, 1)

            with dve.Fori(0, n_pairs // 2) as i:
                pair(i, 0)
                pair(i, 1)

        @block.tensor
        def _(pe):
            pe.wait_ge(gavg_in, 16)
            with pe.Fori(0, n_pairs) as g:
                pe.wait_ge(mom_ready, g + 1)
                pe.matmul(grp_ps[:], gavg[:], mom[:].rearrange("c k s -> c (k s)"), start=True, stop=True).then_inc(grp_ready, 1)

        @block.scalar
        def _(act):
            with act.Fori(0, n_pairs) as g:
                act.wait_ge(var_ready, g + 1)
                act.activation(std[:], var[:], ACT.Sqrt).then_inc(std_ready, 1)
                act.wait_ge(sc_ready, (g + 1) * 2)
                act.dma_start(scale_dram[g], sc[:]).then_inc(sc_out, 16)
            act.wait_ge(sc_out, 16 * n_pairs)


def lag_tables(nc, a, lag_const, a_dram):
    with ExitStack() as ctx:
        R = a["t_w0"].shape[0]
        S = Scope(nc, ctx, "tt")
        sb, sem = S.sb, S.sem
        posr = sb("pos", [R, LAGS])
        absl = sb("absl", [CP, LAGS])
        w0 = sb("w0", [R, 2, 2])
        ws = sb("ws", [R, 2, 3, R])
        bs = sb("bs", [R, 2, 3])
        wo = sb("wo", [R, 2, D1])
        bo = sb("bo", [CP, 2, DC])
        slope = sb("slope", [CP, DC])
        hid = sb("hid", [R, 2, 4, LAGS])
        decay = sb("decay", [CP, DC, LAGS])
        tab = sb("tab", [CP, 2, DC, LAGS])
        h_ps = [ctx.enter_context(nc.psum_tensor(f"tt_h{i}", [R, LAGS], F32)) for i in range(2)]
        o_ps = [ctx.enter_context(nc.psum_tensor(f"tt_o{i}", [CP, 4, 128], F32)) for i in range(2)]
        loads, lin, hid_ready, sl_ready, ln_ready, dec_ready, out_ready, tab_ready, tab_out = (
            sem(n) for n in ("loads", "lin", "hid_ready", "sl_ready", "ln_ready", "dec_ready", "out_ready", "tab_ready", "tab_out"))
        block = ctx.enter_context(nc.Block())

        @block.sync
        def _(sp):
            sp.dma_start(posr[:], lag_const[0].partition_broadcast(R)).then_inc(loads, 16)
            sp.dma_start(absl[:], lag_const[1].partition_broadcast(CP)).then_inc(loads, 16)
            sp.dma_start(w0[:], a["t_w0"][:]).then_inc(loads, 16)
            for t in range(2):
                sp.dma_start(ws[:, t], a["t_ws"][t].rearrange("l i o -> i l o")).then_inc(loads, 16)
            sp.dma_start(wo[:], a["t_wo"].rearrange("t r d -> r t d")).then_inc(loads, 16)
            sp.dma_start(bs[:], a["t_bs"][:]).then_inc(loads, 16)
            sp.dma_start(bo[:], a["t_bo"][:]).then_inc(loads, 16)
            sp.dma_start(slope[:], a["slope"][:]).then_inc(loads, 16)
            sp.wait_ge(tab_ready, 2 * DC)
            for t in range(2):
                sp.dma_start(a_dram[t].rearrange("(k c) l -> c k l", c=CP), tab[:, t]).then_inc(tab_out, 16)
            sp.wait_ge(tab_out, 32)

        n_loads = 16 * 9

        @block.vector
        def _(dve):
            dve.wait_ge(loads, n_loads)
            for t in range(2):
                dve.tensor_scalar(hid[:, t, 0], posr[:], w0[:, t, 0:1], w0[:, t, 1:2], ALU.mult, ALU.add).then_inc(lin, 1)
            dve.wait_ge(lin, 2)
            for t in range(2):
                dve.tensor_scalar(hid[:, t, 0], hid[:, t, 0], 0.0, None, ALU.max).then_inc(hid_ready, 1)
            dve.tensor_scalar(slope[:], slope[:], 0.0, 1.0, ALU.max, ALU.min).then_inc(lin, 1)
            dve.wait_ge(lin, 3)
            dve.tensor_scalar(slope[:], slope[:], 1.0 - 0.95, 0.95, ALU.mult, ALU.add).then_inc(sl_ready, 1)
            for layer in range(3):
                for t in range(2):
                    dve.wait_ge(out_ready, layer * 2 + t + 1)
                    dve.tensor_scalar(hid[:, t, layer + 1], h_ps[t][:], bs[:, t, layer:layer + 1], 0.0, ALU.add, ALU.max).then_inc(hid_ready, 1)
            dve.wait_ge(dec_ready, DC)
            for t in range(2):
                for k in range(DC):
                    dve.wait_ge(out_ready, 6 + t * 2 + k // 3 + 1)
                    dve.scalar_tensor_tensor(out=tab[:, t, k], in0=o_ps[k // 3][:, k % 3, 0:LAGS], scalar=bo[:, t, k:k + 1],
                                             in1=decay[:, k], op0=ALU.add, op1=ALU.mult).then_inc(tab_ready, 1)

        @block.tensor
        def _(pe):
            pe.wait_ge(loads, n_loads)
            for layer in range(3):
                for t in range(2):
                    pe.wait_ge(hid_ready, layer * 2 + t + 1)
                    pe.matmul(h_ps[t][:], ws[:, t, layer], hid[:, t, layer], start=True, stop=True).then_inc(out_ready, 1)
            for t in range(2):
                pe.wait_ge(hid_ready, 6 + t + 1)
                for half in range(2):
                    if t == 1:
                        pe.wait_ge(tab_ready, 3 * (half + 1))
                    for k in range(3 * half, 3 * half + 3):
                        ins = pe.matmul(o_ps[half][:, k % 3, 0:LAGS], wo[:, t, k * CP:(k + 1) * CP], hid[:, t, 3], start=True, stop=True)
                    ins.then_inc(out_ready, 1)

        @block.scalar
        def _(act):
            act.wait_ge(sl_ready, 1)
            act.activation(slope[:], slope[:], ACT.Ln).then_inc(ln_ready, 1)
            act.wait_ge(ln_ready, 1)
            for k in range(DC):
                act.activation(decay[:, k], absl[:], ACT.Exp, scale=slope[:, k:k + 1]).then_inc(dec_ready, 1)


def upper_half(t):
    t = t.bitcast(BF16)
    return t[tuple([slice(None)] * (len(t.shape) - 1) + [slice(1, None, 2)])]



def high_part(eng, dst, src):
    return eng.tensor_copy(dst, src)


def low_part(eng, dst, src, high):
    return eng.tensor_tensor(dst, src, high.bitcast(F32), ALU.subtract)


def high_bits(eng, dst, src):
    return eng.tensor_scalar(dst.bitcast(I32), src.bitcast(I32), -(1 << 12), None, ALU.bitwise_and)


def split_matmul(pe, out, lhs, rhs, start, stop):
    for at, (a, b) in enumerate(((0, 0), (0, 1), (1, 0))):
        ins = pe.matmul(out, lhs[a], rhs[b], start=start and at == 0, stop=stop and at == 2)
    return ins


def load_scale(sp, sc, scale_dram, g, sem):
    sp.dma_start(sc[:].rearrange("c k b s -> c (k b) s"), scale_dram[g]).then_inc(sem, 16)


def load_block(sp, dst, src, g, block, sem):
    sp.dma_start(dst[:], src[g, :, :, bass.ds(block * CW, CW)].rearrange("k c w b h -> c k w b h")).then_inc(sem, 16)


def normalise(eng, dst, src, sc):
    for kc in range(KC):
        for b in range(PB):
            ins = eng.tensor_scalar(dst[0:CP, kc, :, b], src[:, kc, :, b], sc[:, kc, b, 0:1], sc[:, kc, b, 1:2], ALU.mult, ALU.add)
    return ins


def mixer_qv(nc, x_dram, scale_dram, wqv_dram, gated_dram, a_dram, t_dram, n_pairs):
    with ExitStack() as ctx:
        S = Scope(nc, ctx, "qv")
        passed = S.sem("passed")
        wqv = S.sb("wqv", [CP + 1, KC, 2 * D1])
        wh, wl = (S.sb(n, [CP + 1, KC, 2 * D1], F32R) for n in ("wh", "wl"))
        sc = S.sb("sc", [CP, KC, PB, 2])
        xs = S.sb2("xs", [CP, KC, CW, PB, SIDE])
        xn = S.sb2("xn", [CP + 1, KC, CW, PB, SIDE])
        xh, xl = (S.sb2(n, [CP + 1, KC, CW, PB, SIDE], dtype=F32R) for n in ("xh", "xl"))
        qv = S.sb2("qv", [TOK, 2 * D1])
        xo = S.sb2("xo", [TOK, CW, D1])
        NT = 3
        NW = 2 * D1 // NT
        ps = [S.ps(f"ps{i}", [TOK, NT, 512]) for i in range(2)]
        w_in, ones, sc_in, t_out = S.sem("w_in"), S.sem("ones"), S.sem("sc_in"), S.sem("t_out")
        x_in, normed, silu, gated, stored, block_read = (
            S.sem2(n) for n in ("x_in", "normed", "silu", "gated", "stored", "bread"))
        proj = S.sem2("proj")
        w_parts, high, parts = S.sem("w_parts"), S.sem2("high"), S.sem2("parts")
        block = ctx.enter_context(nc.Block())
        NJ = NB // 2
        ROWS = SIDE // (n_pairs * NJ)

        @block.sync
        def _(sp):
            sp.dma_start(wqv[:], wqv_dram[:]).then_inc(w_in, 16)
            with sp.Fori(0, n_pairs) as g:
                sp.wait_ge(normed[1], g * NJ)
                load_scale(sp, sc, scale_dram, g, sc_in)
                with sp.Fori(0, NJ) as j:
                    i = g * NJ + j
                    for s in range(2):
                        sp.wait_ge(normed[s], i)
                        load_block(sp, xs[s], x_dram, g, j * 2 + s, x_in[s])
                    for t in range(2):
                        for r in range(ROWS):
                            row = i * ROWS + r
                            sp.dma_start(t_dram[t, row], a_dram[t, :, bass.ds(SIDE - 1 - row, SIDE)]).then_inc(t_out, 16)
            sp.wait_ge(t_out, 2 * SIDE * 16)

        @block.gpsimd
        def _(pool):
            for s in range(2):
                pool.memset(xn[s][:], 1.0).then_inc(ones, 1)
            pool.wait_ge(ones, 2)
            with pool.Fori(0, n_pairs) as g:
                pool.wait_ge(sc_in, (g + 1) * 16)
                pool.sem_inc(passed, 1)
                with pool.Fori(0, NJ) as j:
                    i = g * NJ + j
                    for s in range(2):
                        pool.wait_ge(x_in[s], (i + 1) * 16)
                        pool.wait_ge(parts[s], i)
                        pool.sem_inc(passed, 1)
                        normalise(pool, xn[s], xs[s], sc).then_inc(normed[s], 1)

        @block.tensor
        def _(pe):
            pe.wait_ge(w_parts, 2)
            with pe.Fori(0, n_pairs * NJ) as i:
                for s in range(2):
                    pe.wait_ge(parts[s], i + 1)
                    for w in range(CW):
                        u = (s * CW + w) % 2
                        m = i * CW + (s * CW + w) // 2
                        pe.wait_ge(silu[u], m)
                        for kc in range(KC):
                            p = CP + kc
                            for n in range(NT):
                                ins = split_matmul(pe, ps[u][:, n, 0:NW], [x[s][0:p, kc, w].rearrange("p b h -> p (b h)") for x in (xh, xl)],
                                                   [part[0:p, kc, n * NW:(n + 1) * NW] for part in (wh, wl)], start=(kc == 0), stop=(kc == KC - 1))
                        ins.then_inc(block_read[s] if w == CW - 1 else proj[s], 1)

        @block.scalar
        def _(act):
            with act.Fori(0, n_pairs * NJ) as i:
                g, j = i // NJ, i % NJ
                for s in range(2):
                    for w in range(CW):
                        u = (s * CW + w) % 2
                        m = i * CW + (s * CW + w) // 2
                        if w == CW - 1:
                            act.wait_ge(block_read[s], i + 1)
                        else:
                            act.wait_ge(proj[s], i * (CW - 1) + w + 1)
                        act.wait_ge(gated[u], m)
                        act.activation(qv[u][:].rearrange("t (n c) -> t n c", n=NT), ps[u][:, :, 0:NW], ACT.Silu).then_inc(silu[u], 1)
                    act.wait_ge(gated[1], i * CW + (s * CW + CW - 1) // 2 + 1)
                    act.wait_ge(gated[0], i * CW + (s * CW + CW - 1) // 2 + 1)
                    act.dma_start(gated_dram[g, :, bass.ds(j * 2 * CW + s * CW, CW)], xo[s][:]).then_inc(stored[s], 16)
            for s in range(2):
                act.wait_ge(stored[s], 16 * n_pairs * NJ)

        @block.vector
        def _(dve):
            dve.wait_ge(w_in, 16)
            high_part(dve, wh[:], wqv[:]).then_inc(w_parts, 1)
            dve.wait_ge(w_parts, 1)
            low_part(dve, wl[:], wqv[:], wh[:]).then_inc(w_parts, 1)

            def split(i, s):
                dve.wait_ge(block_read[s], i)
                dve.wait_ge(normed[s], i + 1)
                high_part(dve, xh[s][:], xn[s][:]).then_inc(high[s], 1)
                dve.wait_ge(high[s], i + 1)
                low_part(dve, xl[s][:], xn[s][:], xh[s][:]).then_inc(parts[s], 1)

            def gates(i, s):
                dve.wait_ge(stored[s], i * 16)
                for w in range(CW):
                    u = (s * CW + w) % 2
                    m = i * CW + (s * CW + w) // 2
                    dve.wait_ge(silu[u], m + 1)
                    dve.tensor_tensor(xo[s][:, w], qv[u][:, 0:D1], qv[u][:, D1:2 * D1], ALU.mult).then_inc(gated[u], 1)

            last = n_pairs * NJ - 1
            split(0, 0)
            with dve.Fori(0, last) as i:
                split(i, 1)
                gates(i, 0)
                split(i + 1, 0)
                gates(i, 1)
            split(last, 1)
            gates(last, 0)
            gates(last, 1)


def mixer_toeplitz(nc, gated_dram, t_dram, ident_dram, mixed_dram, n_pairs):
    with ExitStack() as ctx:
        S = Scope(nc, ctx, "tp")
        passed = S.sem("passed")
        GS = 4
        HG = GC // 2
        ident = S.sb("ident", [128, 128])
        x = S.sb2("x", [TOK, SIDE, CP])
        o = S.sb2("o", [SIDE, TOK, CP])
        t2 = S.sb2("t2", [128, GC, PB, SIDE], GS)
        t1 = S.sb2("t1", [128, GC, SIDE], GS)
        xg = S.sb2("xg", [128, GC, SIDE], GS)
        xt = S.sb2("xt", [128, 2, HG, TOK], GS)
        tp = [S.ps(f"tps{i}", [SIDE, 2, 512]) for i in range(2)]
        op = [S.ps(f"ops{i}", [SIDE, 2, 512]) for i in range(2)]
        id_in, zero = S.sem("id_in"), S.sem("zero")
        x_in, chunk_out = S.sem2("x_in"), S.sem2("chunk_out")
        t_in, staged, turned, xt_ready, summed, o_ready = (S.sem2(n, GS) for n in ("t_in", "staged", "turned", "xt_ready", "summed", "o_ready"))
        block = ctx.enter_context(nc.Block())
        NCH = n_pairs * DC // 2
        NG = CP // GC // GS
        PADS = 4 * GS

        def earlier(m, q, by):
            return (q - by) % GS, m + (1 if q >= by else 0)

        @block.sync
        def _(sp):
            sp.dma_start(ident[:], ident_dram[:]).then_inc(id_in, 16)
            sp.wait_ge(zero, PADS)
            with sp.Fori(0, NCH) as i:
                for s in range(2):
                    with sp.Fori(0, NG) as j:
                        m = (i * 2 + s) * NG + j
                        for q in range(GS):
                            sp.wait_ge(summed[q], m)
                            c0 = ((i * 2 + s) % DC) * CP + (j * GS + q) * GC
                            for b in range(PB):
                                sp.dma_start(t2[q][b * SIDE:(b + 1) * SIDE, :, b], t_dram[1, :, bass.ds(c0, GC)]).then_inc(t_in[q], 16)
                            sp.dma_start(t1[q][0:SIDE], t_dram[0, :, bass.ds(c0, GC)]).then_inc(t_in[q], 16)

        @block.gpsimd
        def _(pool):
            def load(n, s):
                pool.dma_start(x[s][:], gated_dram[n // DC, :, :, bass.ds((n % DC) * CP, CP)]).then_inc(x_in[s], 16)

            def chunks(i, last):
                for s in range(2):
                    n = i * 2 + s
                    for q in range(GS):
                        pool.wait_ge(staged[q], n * NG)
                    if not (last and s):
                        load(n + 1, 1 - s)
                    pool.wait_ge(x_in[s], (i + 1) * 16)
                    pool.sem_inc(passed, 1)
                    with pool.Fori(0, NG) as j:
                        m = n * NG + j
                        for q in range(GS):
                            pool.wait_ge(summed[q], m)
                            pool.tensor_copy(xg[q][0:TOK], x[s][:, :, bass.ds((j * GS + q) * GC, GC)].rearrange("t w c -> t c w")).then_inc(staged[q], 1)

            load(0, 0)
            for q in range(GS):
                for t in (t2, t1, xg, xt):
                    pool.memset(t[q][:], 0.0).then_inc(zero, 1)
            pool.wait_ge(zero, PADS)
            with pool.Fori(0, NCH - 1) as i:
                chunks(i, False)
            chunks(NCH - 1, True)

        @block.vector
        def _(dve):
            with dve.Fori(0, NCH) as i:
                for s in range(2):
                    dve.wait_ge(chunk_out[s], i * 16)
                    dve.sem_inc(passed, 1)
                    with dve.Fori(0, NG) as j:
                        m = (i * 2 + s) * NG + j
                        for q in range(GS):
                            dve.wait_ge(summed[q], m + 1)
                            dve.tensor_copy(o[s][:, :, bass.ds((j * GS + q) * GC, GC)].rearrange("w t (h r) -> w h r t", h=2),
                                            op[q % 2][:, :, 0:HG * TOK].rearrange("w h (r t) -> w h r t", t=TOK)).then_inc(o_ready[q], 1)

        @block.tensor
        def _(pe):
            def turn(m, q):
                pe.wait_ge(staged[q], m + 1)
                at, count = earlier(m, q, 2)
                pe.wait_ge(xt_ready[at], count)
                pe.sem_inc(passed, 1)
                for c in range(GC):
                    h, r = c // HG, c % HG
                    ins = pe.transpose(tp[q % 2][:, h, r * TOK:(r + 1) * TOK], xg[q][0:TOK, c], ident[0:TOK, 0:TOK])
                ins.then_inc(turned[q], 1)

            def products(m, q):
                pe.wait_ge(t_in[q], (m + 1) * 48)
                pe.wait_ge(xt_ready[q], m + 1)
                at, count = earlier(m, q, 2)
                pe.wait_ge(o_ready[at], count)
                for c in range(GC):
                    h, r = c // HG, c % HG
                    sums = op[q % 2][:, h, r * TOK:(r + 1) * TOK]
                    pe.matmul(sums, xg[q][:, c], t2[q][:, c].rearrange("p b h -> p (b h)"), start=True, stop=False)
                    ins = pe.matmul(sums, t1[q][:, c], xt[q][:, h, r], start=False, stop=True)
                ins.then_inc(summed[q], 1)

            pe.wait_ge(id_in, 16)
            rounds = NCH * 2 * NG
            turn(0, 0)
            with pe.Fori(0, rounds - 1) as m:
                for q in range(GS):
                    turn(m + (q + 1) // GS, (q + 1) % GS)
                    products(m, q)
            for q in range(GS):
                if q + 1 < GS:
                    turn(rounds - 1, q + 1)
                products(rounds - 1, q)

        @block.scalar
        def _(act):
            act.wait_ge(zero, PADS)
            with act.Fori(0, NCH) as i:
                for s in range(2):
                    n = i * 2 + s
                    with act.Fori(0, NG) as j:
                        m = n * NG + j
                        for q in range(GS):
                            act.wait_ge(turned[q], m + 1)
                            act.wait_ge(summed[q], m)
                            act.copy(xt[q][0:SIDE].rearrange("w h r t -> w h (r t)"), tp[q % 2][:, :, 0:HG * TOK]).then_inc(xt_ready[q], 1)
                    for q in range(GS):
                        act.wait_ge(o_ready[q], (n + 1) * NG)
                    act.dma_start(mixed_dram[n // DC, :, :, bass.ds((n % DC) * CP, CP)], o[s][:]).then_inc(chunk_out[s], 16)
            for s in range(2):
                act.wait_ge(chunk_out[s], NCH * 16)


def mixer_out(nc, x_dram, scale_dram, mixed_dram, wp_dram, pb_dram, wo_dram, ob_dram, ident_dram, x2_dram, n_pairs):
    with ExitStack() as ctx:
        S = Scope(nc, ctx, "mo")
        passed = S.sem("passed")
        ident = S.sb("ident", [128, 128])
        wp = S.sb("wp", [CP, KC, D1])
        wph, wpl = (S.sb(n, [CP, KC, D1], F32R) for n in ("wph", "wpl"))
        pb = S.sb("pb", [CP, DC])
        wo = S.sb("wo", [CP, DC, C])
        ob = S.sb("ob", [CP, KC])
        sc = S.sb("sc", [CP, KC, PB, 2])
        xs = S.sb2("xs", [CP, KC, CW, PB, SIDE])
        xn = S.sb2("xn", [CP, KC, CW, PB, SIDE])
        xh, xl = (S.sb2(n, [CP, KC, CW, PB, SIDE], dtype=F32R) for n in ("xh", "xl"))
        xr = S.sb2("xr", [CP, KC, CW, PB, SIDE])
        mx = S.sb2("mx", [TOK, CW, D1])
        p = S.sb("p", [CP, DC, BLK])
        gt = S.sb("gt", [CP, DC, BLK])
        y = S.sb2("y", [CP, KC, BLK])
        pp = [S.ps(f"pp{i}", [CP, BLK]) for i in range(2)]
        tp = [S.ps(f"tp{i}", [CP, BLK]) for i in range(2)]
        yp = [S.ps(f"yp{i}", [CP, BLK]) for i in range(KC)]
        w_in, sc_in = S.sem("w_in"), S.sem("sc_in")
        w_parts, high, parts = S.sem("w_parts"), S.sem2("high"), S.sem2("parts")
        x_in, mx_in, xr_in, normed, xr_free, xn_read, mx_read, stored = (
            S.sem2(n) for n in ("x_in", "mx_in", "xr_in", "normed", "xr_free", "xn_read", "mx_read", "stored"))
        p_ps, p_ready, turned, gate, y_ps, y_ready = (
            S.sem2(n) for n in ("p_ps", "p_ready", "turned", "gate", "y_ps", "y_ready"))
        block = ctx.enter_context(nc.Block())
        NJ = NB // 2
        half = DC // 2

        @block.sync
        def _(sp):
            for t, d in ((ident, ident_dram), (wp, wp_dram), (pb, pb_dram), (wo, wo_dram), (ob, ob_dram)):
                sp.dma_start(t[:], d[:]).then_inc(w_in, 16)
            with sp.Fori(0, n_pairs) as g:
                sp.wait_ge(normed[1], g * NJ)
                load_scale(sp, sc, scale_dram, g, sc_in)
                with sp.Fori(0, NJ) as j:
                    i = g * NJ + j
                    for s in range(2):
                        sp.wait_ge(normed[s], i)
                        load_block(sp, xs[s], x_dram, g, j * 2 + s, x_in[s])
                        sp.wait_ge(mx_read[s], i)
                        sp.dma_start(mx[s][:], mixed_dram[g, bass.ds((j * 2 + s) * CW, CW)].rearrange("w t c -> t w c")).then_inc(mx_in[s], 16)
                        sp.wait_ge(xr_free[s], i)
                        load_block(sp, xr[s], x_dram, g, j * 2 + s, xr_in[s])

        @block.gpsimd
        def _(pool):
            with pool.Fori(0, n_pairs) as g:
                pool.wait_ge(sc_in, (g + 1) * 16)
                pool.sem_inc(passed, 1)
                with pool.Fori(0, NJ) as j:
                    i = g * NJ + j
                    for s in range(2):
                        pool.wait_ge(x_in[s], (i + 1) * 16)
                        pool.wait_ge(parts[s], i)
                        pool.sem_inc(passed, 1)
                        normalise(pool, xn[s], xs[s], sc).then_inc(normed[s], 1)

        @block.tensor
        def _(pe):
            pe.wait_ge(w_in, 80)
            pe.wait_ge(w_parts, 2)

            def turn_and_make(i, s, turning, making):
                n = i * 2 + s
                i2, s2 = i + s, 1 - s
                n2 = n + 1
                if not turning:
                    i2, s2, n2 = i, s, n
                if turning:
                    pe.wait_ge(mx_in[s], (i + 1) * 16)
                if making:
                    pe.wait_ge(parts[s2], i2 + 1)
                for c in range(DC):
                    q = c % 2
                    if turning:
                        pe.wait_ge(gate[q], n * half + c // 2)
                        for w in range(CW):
                            ins = pe.transpose(tp[q][:, w * TOK:(w + 1) * TOK], mx[s][:, w, c * CP:(c + 1) * CP], ident[0:TOK, 0:TOK])
                        ins.then_inc(turned[q], 1)
                    if making:
                        pe.wait_ge(p_ready[q], n2 * half + c // 2)
                        for kc in range(KC):
                            ins = split_matmul(pe, pp[q][:], [part[:, kc, c * CP:(c + 1) * CP] for part in (wph, wpl)],
                                               [x[s2][:, kc].rearrange("p w b h -> p (w b h)") for x in (xh, xl)], start=(kc == 0), stop=(kc == KC - 1))
                        ins.then_inc(p_ps[q], 1)
                if turning:
                    pe.wait_ge(turned[1], (n + 1) * half)
                    pe.sem_inc(mx_read[s], 1)
                if making:
                    pe.wait_ge(p_ps[1], (n2 + 1) * half)
                    pe.sem_inc(xn_read[s2], 1)

            def project(i, s):
                n = i * 2 + s
                for q in range(2):
                    pe.wait_ge(gate[q], (n + 1) * half)
                for oc in range(KC):
                    pe.wait_ge(y_ready[oc], n)
                    for c in range(DC):
                        ins = pe.matmul(yp[oc][:], wo[:, c, oc * CP:(oc + 1) * CP], gt[:, c], start=(c == 0), stop=(c == DC - 1))
                    ins.then_inc(y_ps[oc], 1)

            last = n_pairs * NJ - 1
            turn_and_make(0, 0, False, True)
            with pe.Fori(0, last) as i:
                for s in range(2):
                    turn_and_make(i, s, True, True)
                    project(i, s)
            turn_and_make(last, 0, True, True)
            project(last, 0)
            turn_and_make(last, 1, True, False)
            project(last, 1)

        @block.scalar
        def _(act):
            act.wait_ge(w_in, 80)

            def silu(i, s, again=True):
                n = i * 2 + s
                for c in range(DC):
                    q, m = c % 2, n * half + c // 2
                    act.wait_ge(p_ps[q], m + 1)
                    if again:
                        act.wait_ge(gate[q], (n - 1) * half + c // 2 + 1)
                    act.activation(p[:, c], pp[q][:], ACT.Silu, bias=pb[:, c:c + 1]).then_inc(p_ready[q], 1)

            def store(i, s):
                n = i * 2 + s
                for oc in range(KC):
                    act.wait_ge(y_ready[oc], n + 1)
                g, j = i // NJ, i % NJ
                act.dma_start(x2_dram[g, :, :, bass.ds((j * 2 + s) * CW, CW)].rearrange("k c w b h -> c k (w b h)"), y[s][:]).then_inc(stored[s], 16)

            last = n_pairs * NJ - 1
            silu(0, 0, again=False)
            with act.Fori(0, last) as i:
                for s in range(2):
                    silu(i + s, 1 - s)
                    store(i, s)
            silu(last, 1)
            for s in range(2):
                store(last, s)
            for s in range(2):
                act.wait_ge(stored[s], 16 * n_pairs * NJ)

        @block.vector
        def _(dve):
            dve.wait_ge(w_in, 80)
            high_part(dve, wph[:], wp[:]).then_inc(w_parts, 1)
            dve.wait_ge(w_parts, 1)
            low_part(dve, wpl[:], wp[:], wph[:]).then_inc(w_parts, 1)

            def split(i, s):
                dve.wait_ge(xn_read[s], i)
                dve.wait_ge(normed[s], i + 1)
                high_part(dve, xh[s][:], xn[s][:]).then_inc(high[s], 1)
                dve.wait_ge(high[s], i + 1)
                low_part(dve, xl[s][:], xn[s][:], xh[s][:]).then_inc(parts[s], 1)

            def gates(i, s):
                n = i * 2 + s
                for oc in range(KC):
                    dve.wait_ge(y_ps[oc], n)
                for c in range(DC):
                    q, m = c % 2, n * half + c // 2
                    dve.wait_ge(p_ready[q], m + 1)
                    dve.wait_ge(turned[q], m + 1)
                    dve.tensor_tensor(gt[:, c], tp[q][:], p[:, c], ALU.mult).then_inc(gate[q], 1)

            def residual(i, s):
                n = i * 2 + s
                dve.wait_ge(stored[s], i * 16)
                dve.wait_ge(xr_in[s], (i + 1) * 16)
                for oc in range(KC):
                    dve.wait_ge(y_ps[oc], n + 1)
                    dve.scalar_tensor_tensor(out=y[s][:, oc], in0=yp[oc][:], scalar=ob[:, oc:oc + 1], in1=xr[s][:, oc].rearrange("p w b h -> p (w b h)"),
                                             op0=ALU.add, op1=ALU.add).then_inc(y_ready[oc], 1)
                dve.wait_ge(y_ready[1], n + 1)
                dve.sem_inc(xr_free[s], 1)

            last = n_pairs * NJ - 1
            split(0, 0)
            split(0, 1)
            with dve.Fori(0, last) as i:
                for s in range(2):
                    gates(i, s)
                    split(i + 1, s)
                    residual(i, s)
            for s in range(2):
                gates(last, s)
                residual(last, s)


def scan_inputs(nc, x_dram, scale_dram, a, z_dram, u_dram, bc_dram, n_pairs):
    with ExitStack() as ctx:
        S = Scope(nc, ctx, "si")
        passed = S.sem("passed")
        N4 = NDIR * HEADS
        ROW = SIDE + 2
        ident = S.sb("ident", [128, 128])
        wh, wl = (S.sb(n, [CP, KC, 2 * DI], F32R) for n in ("wh", "wl"))
        cw = S.sb("cw", [128, IK, 3, 3])
        PE_TAPS = {1: 2, 2: 3}
        POOL_FROM = 4
        taps = S.sb("taps", [128, sum(PE_TAPS.values()), 128])
        cb = S.sb("cb", [128, IK])
        wx = S.sb("wx", [128, IK, NDIR * 2 * NS + N4])
        dtb = S.sb("dtb", [TOK, N4])
        aneg = S.sb("aneg", [TOK, N4])
        sc = S.sb("sc", [CP, KC, PB, 2])
        xs = S.sb2("xs", [CP, KC, CW, PB, SIDE])
        xn = S.sb2("xn", [CP, KC, CW, PB, SIDE])
        xh, xl = (S.sb2(n, [CP, KC, CW, PB, SIDE], dtype=F32R) for n in ("xh", "xl"))
        z = S.sb("z", [128, IK, BLK])
        xi = S.sb("xi", [128, IK, ROW, PB, ROW])
        part = S.sb2("part", [128, BLK])
        acc = S.sb2("acc", [128, IK, BLK])
        u = S.sb2("u", [128, IK, BLK])
        ut = S.sb("ut", [TOK, 2, CW, DI + N4])
        dts = S.sb("dts", [TOK, 2 * CW, NDIR, REC, HEADS])
        raw = S.sb("raw", [TOK, 2 * CW, N4])
        bc = S.sb2("bc", [TOK, CW, NDIR * 2 * NS])
        w_in = bc[0][0:CP].rearrange("p w c -> p (w c)")[:, 0:KC * 2 * DI].rearrange("p (k c) -> p k c", k=KC)
        sp_ = {n: S.sb("sp_" + n, [TOK, 2 * CW, N4]) for n in ("t", "neg", "e", "ln", "ser", "small")}
        bank = [S.ps(f"bank{i}", [128, 512]) for i in range(8)]
        w_loaded, consts, sc_in, built = S.sem("w_loaded"), S.sem("consts"), S.sem("sc_in"), S.sem("built")
        w_parts, high, parts = S.sem("w_parts"), S.sem2("high"), S.sem2("parts")
        x_in, normed, xn_read = S.sem2("x_in"), S.sem2("normed"), S.sem2("xn_read")
        z_ps, z_done, xi_ps, xi_done = (S.sem2(n, IK) for n in ("z_ps", "z_done", "xi_ps", "xi_done"))
        z_out = S.sem("z_out")
        c_ps, v_taps, c1_ready, p_taps, u_ready, u_read = (S.sem2(n) for n in ("c_ps", "v_taps", "c1_ready", "p_taps", "u_ready", "u_read"))
        N_V, N_1, N_P = 2 * 9 - PE_TAPS[2], POOL_FROM - PE_TAPS[1], 2 * (9 - POOL_FROM)
        bc_ps, t_ps, bc_done, t_done = (S.sem2(n) for n in ("bc_ps", "t_ps", "bc_done", "t_done"))
        ut_out, bc_out = S.sem2("ut_out"), S.sem2("bc_out")
        taken = S.sem2("taken")
        link, neg_ready, e_ready, ln_ready, raw_ready, dt_done, dt_out = (
            S.sem(n) for n in ("link", "neg_ready", "e_ready", "ln_ready", "raw_ready", "dt_done", "dt_out"))
        block = ctx.enter_context(nc.Block())
        NJ = NB // 2
        n_w = 16 * 7

        def window(k, g_cols, dh):
            return xi[:, k, g_cols, :, dh:dh + SIDE].rearrange("p w b h -> p (w b) h")

        def lines(t):
            return t.rearrange("p (w b h) -> p (w b) h", w=CW, b=PB)

        def blocks(eng, g, convolve, project, take, softplus, early=()):
            late = tuple(w for w in range(CW) if w not in early)

            def step(cj, cs, pj, ps):
                project(g, pj, ps, early)
                convolve(g, cj, cs)
                if ps == 0:
                    take(g, pj - 1, 1)
                    softplus(g, pj - 1)
                else:
                    take(g, pj, 0)
                project(g, pj, ps, late)

            convolve(g, 0, 0)
            project(g, 0, 0, early)
            convolve(g, 0, 1)
            project(g, 0, 0, late)
            step(1, 0, 0, 1)
            with eng.Fori(0, NJ - 2) as j:
                step(j + 1, 1, j + 1, 0)
                step(j + 2, 0, j + 1, 1)
            step(NJ - 1, 1, NJ - 1, 0)
            project(g, NJ - 1, 1, range(CW))
            take(g, NJ - 1, 0)
            take(g, NJ - 1, 1)
            softplus(g, NJ - 1)

        idle = lambda *_: None

        @block.sync
        def _(sp):
            sp.dma_start(w_in, a["w_in"][:]).then_inc(w_loaded, 16)
            for t, d in ((ident, a["ident"]), (cw, a["cw"]), (cb, a["cb"]), (wx, a["wx"])):
                sp.dma_start(t[:], d[:]).then_inc(w_loaded, 16)
            sp.dma_start(dtb[:], a["dtb"][0].partition_broadcast(TOK)).then_inc(w_loaded, 16)
            sp.dma_start(aneg[:], a["alog"][0].partition_broadcast(TOK)).then_inc(w_loaded, 16)
            with sp.Fori(0, n_pairs) as g:
                sp.wait_ge(normed[1], g * NJ)
                load_scale(sp, sc, scale_dram, g, sc_in)
                with sp.Fori(0, NJ) as j:
                    i = g * NJ + j
                    for s in range(2):
                        sp.wait_ge(normed[s], i)
                        load_block(sp, xs[s], x_dram, g, j * 2 + s, x_in[s])
                with sp.Fori(0, NJ) as j:
                    i = g * NJ + j
                    for s in range(2):
                        cols = bass.ds((j * 2 + s) * CW, CW)
                        for q in range(2):
                            sp.wait_ge(bc_done[q], (i * 2 + s + 1) * 2)
                        sp.dma_start(bc_dram[g, cols].rearrange("w p c -> p w c"), bc[s][:]).then_inc(bc_out[s], 16)
                        for q in range(2):
                            sp.wait_ge(t_done[q], (i * 2 + s + 1) * 2)
                        sp.dma_start(u_dram[g, cols, :, 0:DI].rearrange("w p c -> p w c"), ut[:, s, :, 0:DI]).then_inc(ut_out[s], 16)
                    sp.wait_ge(dt_done, (i + 1) * 4)
                    sp.dma_start(u_dram[g, bass.ds(j * 2 * CW, 2 * CW), :, DI:DI + REC * N4].rearrange("w p c -> p w c"),
                                 dts[:].rearrange("p w k t h -> p w (k t h)")).then_inc(dt_out, 16)
            sp.wait_ge(z_out, 16 * n_pairs * NB)
            sp.wait_ge(dt_out, 16 * n_pairs * NJ)
            for s in range(2):
                sp.wait_ge(bc_out[s], 16 * n_pairs * NJ)
                sp.wait_ge(ut_out[s], 16 * n_pairs * NJ)

        @block.gpsimd
        def _(pool):
            pool.memset(xi[:].rearrange("p k w b h -> p (k w b h)"), 0.0).then_inc(consts, 1)
            pool.wait_ge(w_loaded, n_w)

            def convolve(g, j, s):
                i = g * NJ + j
                steps = [(what, tap) for at in range(POOL_FROM, 10) for what, tap in (("times", at), ("plus", at - 1)) if POOL_FROM <= tap < 9]
                count = lambda step: i * N_P + steps.index(step) + 1
                for what, tap in steps:
                    dh, dw = tap // 3, tap % 3
                    if what == "times":
                        if tap >= POOL_FROM + 2:
                            pool.wait_ge(p_taps[s], count(("plus", tap - 2)))
                        xin = window(1, bass.ds((j * 2 + s) * CW + dw, CW), dh)
                        ins = pool.tensor_tensor(lines(part[tap % 2][:]), xin, cw[:, 1, dh, dw:dw + 1].unsqueeze(2).to_broadcast([128, CW * PB, SIDE]), ALU.mult)
                    else:
                        if tap == POOL_FROM:
                            pool.wait_ge(c1_ready[s], (i + 1) * N_1)
                        else:
                            pool.wait_ge(p_taps[s], count(("plus", tap - 1)))
                        pool.wait_ge(p_taps[s], count(("times", tap)))
                        ins = pool.tensor_tensor(acc[s][:, 1], acc[s][:, 1], part[tap % 2][:], ALU.add)
                    ins.then_inc(p_taps[s], 1)
                pool.wait_ge(p_taps[s], (i + 1) * N_P)
                pool.sem_inc(passed, 1)

            with pool.Fori(0, n_pairs) as g:
                pool.wait_ge(sc_in, (g + 1) * 16)
                pool.sem_inc(passed, 1)
                with pool.Fori(0, NJ) as j:
                    i = g * NJ + j
                    for s in range(2):
                        pool.wait_ge(x_in[s], (i + 1) * 16)
                        pool.wait_ge(parts[s], i)
                        pool.sem_inc(passed, 1)
                        normalise(pool, xn[s], xs[s], sc).then_inc(normed[s], 1)
                for k in range(IK):
                    pool.wait_ge(xi_done[k], (g + 1) * NB)
                pool.sem_inc(passed, 1)
                blocks(pool, g, convolve, idle, idle, idle)

        @block.tensor
        def _(pe):
            pe.wait_ge(w_loaded, n_w)
            pe.wait_ge(consts, 1)
            pe.wait_ge(built, 2)
            pe.wait_ge(w_parts, 2)

            def convolve(g, j, s):
                i = g * NJ + j
                pe.wait_ge(v_taps[s], i * N_V)
                pe.wait_ge(c1_ready[s], i * N_1)
                at = 0
                for k, count in PE_TAPS.items():
                    for tap in range(count):
                        dh, dw = tap // 3, tap % 3
                        ins = pe.matmul(lines(bank[2 * s + k - 1][:, 0:BLK]), taps[:, at], window(k, bass.ds((j * 2 + s) * CW + dw, CW), dh),
                                        start=(tap == 0), stop=(tap == count - 1))
                        at += 1
                ins.then_inc(c_ps[s], 1)

            def project(g, j, s, ws):
                i = g * NJ + j
                n = i * 2 + s
                if 0 in ws:
                    pe.wait_ge(u_ready[s], (i + 1) * IK)
                for w in ws:
                    q, m = w % 2, n * 2 + w // 2
                    pe.wait_ge(bc_done[q], m)
                    tok = lambda k: u[s][:, k, w * TOK:(w + 1) * TOK]
                    for k in range(IK):
                        ins = pe.matmul(bank[4 + 2 * q][0:TOK, 0:512], tok(k), wx[:, k, 0:512], start=(k == 0), stop=(k == IK - 1))
                    ins.then_inc(bc_ps[q], 1)
                    pe.wait_ge(t_done[q], m)
                    for k in range(IK):
                        pe.matmul(bank[5 + 2 * q][0:TOK, DI:DI + N4], tok(k), wx[:, k, 512:512 + N4], start=(k == 0), stop=(k == IK - 1))
                    for k in range(IK):
                        ins = pe.transpose(bank[5 + 2 * q][0:TOK, k * 128:(k + 1) * 128], tok(k), ident[:])
                    ins.then_inc(u_read[s] if w == CW - 1 else t_ps[q], 1)

            with pe.Fori(0, n_pairs) as g:
                for s in range(2):
                    pe.wait_ge(v_taps[s], g * NJ * N_V)
                    pe.wait_ge(c1_ready[s], g * NJ * N_1)
                    pe.wait_ge(bc_done[s], g * NB * 2)
                    pe.wait_ge(t_done[s], g * NB * 2)
                pe.sem_inc(passed, 1)
                with pe.Fori(0, NJ) as j:
                    i = g * NJ + j
                    for s in range(2):
                        n = i * 2 + s
                        pe.wait_ge(parts[s], i + 1)
                        for out, ps, done, off in ((bank[0:3], xi_ps, xi_done, 0), (bank[3:6], z_ps, z_done, DI)):
                            for k in range(IK):
                                pe.wait_ge(done[k], n)
                                for kc in range(KC):
                                    ins = split_matmul(pe, out[k][:, 0:BLK], [part[:, kc, off + k * 128:off + (k + 1) * 128] for part in (wh, wl)],
                                                       [x[s][:, kc].rearrange("p w b h -> p (w b h)") for x in (xh, xl)], start=(kc == 0), stop=(kc == KC - 1))
                                ins.then_inc(ps[k], 1)
                        pe.wait_ge(z_ps[IK - 1], n + 1)
                        pe.sem_inc(xn_read[s], 1)
                for k in range(IK):
                    pe.wait_ge(xi_done[k], (g + 1) * NB)
                    pe.wait_ge(z_done[k], (g + 1) * NB)
                pe.sem_inc(passed, 1)
                blocks(pe, g, convolve, project, idle, idle)

        @block.scalar
        def _(act):
            act.wait_ge(w_loaded, n_w)
            act.activation(aneg[:], aneg[:], ACT.Exp).then_inc(built, 1)
            act.wait_ge(w_parts, 2)

            def convolve(g, j, s):
                i = g * NJ + j
                act.wait_ge(u_read[s], i)
                act.wait_ge(v_taps[s], (i + 1) * N_V)
                for k in (0, 2):
                    act.activation(u[s][:, k], acc[s][:, k], ACT.Gelu, bias=cb[:, k:k + 1]).then_inc(u_ready[s], 1)
                act.wait_ge(p_taps[s], (i + 1) * N_P)
                act.activation(u[s][:, 1], acc[s][:, 1], ACT.Gelu, bias=cb[:, 1:2]).then_inc(u_ready[s], 1)

            def project(g, j, s, ws):
                i = g * NJ + j
                n = i * 2 + s
                if 0 in ws:
                    act.wait_ge(bc_out[s], i * 16)
                    act.wait_ge(ut_out[s], i * 16)
                    act.wait_ge(taken[s], i)
                for w in ws:
                    q, m = w % 2, n * 2 + w // 2
                    act.wait_ge(bc_ps[q], m + 1)
                    act.copy(bc[s][:, w], bank[4 + 2 * q][0:TOK, 0:512]).then_inc(bc_done[q], 1)
                    if w == CW - 1:
                        act.wait_ge(u_read[s], i + 1)
                    else:
                        act.wait_ge(t_ps[q], m + 1 if q == 0 else n + 1)
                    act.copy(ut[:, s, w], bank[5 + 2 * q][0:TOK, 0:DI + N4]).then_inc(t_done[q], 1)

            def softplus(g, j):
                i = g * NJ + j
                act.wait_ge(neg_ready, i + 1)
                act.activation(sp_["e"][:], sp_["neg"][:], ACT.Exp).then_inc(e_ready, 1)
                act.wait_ge(e_ready, i + 1)
                act.activation(sp_["ln"][:], sp_["e"][:], ACT.Ln, bias=1.0).then_inc(ln_ready, 1)

            with act.Fori(0, n_pairs) as g:
                with act.Fori(0, NJ) as j:
                    i = g * NJ + j
                    for s in range(2):
                        n = i * 2 + s
                        act.wait_ge(z_out, n * 16)
                        for k in range(IK):
                            act.wait_ge(z_ps[k], n + 1)
                            act.activation(z[:, k], bank[3 + k][:, 0:BLK], ACT.Gelu).then_inc(z_done[k], 1)
                        for k in range(IK):
                            act.wait_ge(z_done[k], n + 1)
                        act.dma_start(z_dram[g, :, :, bass.ds((j * 2 + s) * CW, CW)].rearrange("k c w b h -> c k (w b h)"), z[:]).then_inc(z_out, 16)
                blocks(act, g, convolve, project, idle, softplus, early=(0, 1))

        @block.vector
        def _(dve):
            dve.wait_ge(w_loaded, n_w)
            high_part(dve, wh[:], w_in).then_inc(w_parts, 1)
            dve.wait_ge(w_parts, 1)
            low_part(dve, wl[:], w_in, wh[:]).then_inc(w_parts, 1)
            for at, (k, tap) in enumerate([(k, tap) for k in PE_TAPS for tap in range(PE_TAPS[k])]):
                dve.tensor_scalar(taps[:, at], ident[:], cw[:, k, tap // 3, tap % 3:tap % 3 + 1], None, ALU.mult)
            dve.wait_ge(built, 1)
            dve.tensor_scalar(aneg[:], aneg[:], -1.0, None, ALU.mult).then_inc(built, 1)
            dve.wait_ge(built, 2)
            dve.wait_ge(consts, 1)

            def convolve(g, j, s):
                i = g * NJ + j
                dve.wait_ge(u_ready[s], i * IK)
                dve.wait_ge(c_ps[s], i + 1)
                order = [(k, tap) for at in range(9) for k, tap in ((1, PE_TAPS[1] + at), (0, at), (2, PE_TAPS[2] + at)) if tap < (POOL_FROM if k == 1 else 9)]
                mine = [x for x in order if x[0] != 1]
                for k, tap in order:
                    dh, dw = tap // 3, tap % 3
                    out, xin, weight = lines(acc[s][:, k]), window(k, bass.ds((j * 2 + s) * CW + dw, CW), dh), cw[:, k, dh, dw:dw + 1]
                    if k == 1 and tap > PE_TAPS[1]:
                        dve.wait_ge(c1_ready[s], i * N_1 + tap - PE_TAPS[1])
                    elif (k, tap - 1) in mine:
                        dve.wait_ge(v_taps[s], i * N_V + mine.index((k, tap - 1)) + 1)
                    if k == 0 and tap == 0:
                        ins = dve.tensor_scalar(out, xin, weight, None, ALU.mult)
                    else:
                        before = lines(bank[2 * s + k - 1][:, 0:BLK]) if k and tap == PE_TAPS[k] else out
                        ins = dve.scalar_tensor_tensor(out=out, in0=xin, scalar=weight, in1=before, op0=ALU.mult, op1=ALU.add)
                    ins.then_inc(c1_ready[s] if k == 1 else v_taps[s], 1)

            def take(g, j, s):
                i = g * NJ + j
                for q in range(2):
                    dve.wait_ge(t_done[q], i * 4 + s * 2 + 2)
                dve.wait_ge(raw_ready, i * 3)
                dve.tensor_tensor(sp_["t"][:, s * CW:(s + 1) * CW], ut[:, s, :, DI:DI + N4], dtb[:].unsqueeze(1).to_broadcast([TOK, CW, N4]), ALU.add).then_inc(taken[s], 1)

            def softplus(g, j):
                i = g * NJ + j
                L = 10
                base = i * L
                step = [0]

                def chain(ins):
                    step[0] += 1
                    ins.then_inc(link, 1)
                    dve.wait_ge(link, base + step[0])

                t, neg, e, ln, ser, small = (sp_[k] for k in ("t", "neg", "e", "ln", "ser", "small"))
                for s in range(2):
                    dve.wait_ge(taken[s], i + 1)
                chain(dve.tensor_scalar(neg[:], t[:], -1.0, None, ALU.mult))
                dve.tensor_tensor(neg[:], neg[:], t[:], ALU.min).then_inc(neg_ready, 1)
                dve.wait_ge(e_ready, i + 1)
                dve.tensor_scalar(small[:], e[:], 0.1, None, ALU.is_lt)
                chain(dve.tensor_scalar(ser[:], e[:], -1.0 / 6.0, None, ALU.mult))
                for c in (1.0 / 5.0, -1.0 / 4.0, 1.0 / 3.0, -1.0 / 2.0, 1.0):
                    chain(dve.scalar_tensor_tensor(out=ser[:], in0=ser[:], scalar=c, in1=e[:], op0=ALU.add, op1=ALU.mult))
                dve.wait_ge(ln_ready, i + 1)
                chain(dve.tensor_tensor(ser[:], ser[:], ln[:], ALU.subtract))
                chain(dve.tensor_tensor(ser[:], ser[:], small[:], ALU.mult))
                chain(dve.tensor_tensor(ser[:], ser[:], ln[:], ALU.add))
                assert step[0] == L
                dve.scalar_tensor_tensor(out=raw[:], in0=t[:], scalar=0.0, in1=ser[:], op0=ALU.max, op1=ALU.add).then_inc(raw_ready, 1)
                dve.wait_ge(raw_ready, i * 3 + 1)
                dve.wait_ge(dt_out, i * 16)
                split = lambda x: x.rearrange("p w (k h) -> p w k h", k=NDIR)
                dve.tensor_copy(dts[:, :, :, DT], split(raw[:])).then_inc(raw_ready, 1)
                dve.wait_ge(raw_ready, i * 3 + 2)
                dve.tensor_tensor(raw[:], raw[:], aneg[:].unsqueeze(1).to_broadcast([TOK, 2 * CW, N4]), ALU.mult).then_inc(raw_ready, 1)
                dve.wait_ge(raw_ready, i * 3 + 3)
                high_bits(dve, dts[:, :, :, DA_HIGH], split(raw[:])).then_inc(dt_done, 1)
                dve.tensor_tensor(dts[:, :, :, DA_REST], split(raw[:]), upper_half(split(raw[:])), ALU.subtract).then_inc(dt_done, 1)
                dve.wait_ge(dt_done, i * 4 + 2)
                low_part(dve, dts[:, :, :, DA_LOW], split(raw[:]), dts[:, :, :, DA_HIGH]).then_inc(dt_done, 1)
                dve.tensor_tensor(dts[:, :, :, DA_REST2], dts[:, :, :, DA_REST], upper_half(dts[:, :, :, DA_REST]), ALU.subtract).then_inc(dt_done, 1)

            with dve.Fori(0, n_pairs) as g:
                for s in range(2):
                    dve.wait_ge(c_ps[s], g * NJ)
                    dve.wait_ge(v_taps[s], g * NJ * N_V)
                    dve.wait_ge(c1_ready[s], g * NJ * N_1)
                    dve.wait_ge(p_taps[s], g * NJ * N_P)
                dve.sem_inc(passed, 1)

                def split(j, s):
                    i = g * NJ + j
                    dve.wait_ge(xn_read[s], i)
                    dve.wait_ge(normed[s], i + 1)
                    high_part(dve, xh[s][:], xn[s][:]).then_inc(high[s], 1)
                    dve.wait_ge(high[s], i + 1)
                    low_part(dve, xl[s][:], xn[s][:], xh[s][:]).then_inc(parts[s], 1)

                def keep(j, s):
                    n = (g * NJ + j) * 2 + s
                    for k in range(IK):
                        dve.wait_ge(xi_ps[k], n + 1)
                        dve.tensor_copy(xi[:, k, bass.ds((j * 2 + s) * CW + 1, CW), :, 1:1 + SIDE].rearrange("p w b h -> p (w b) h"), lines(bank[k][:, 0:BLK])).then_inc(xi_done[k], 1)

                split(0, 0)
                with dve.Fori(0, NJ - 1) as j:
                    split(j, 1)
                    keep(j, 0)
                    split(j + 1, 0)
                    keep(j, 1)
                split(NJ - 1, 1)
                keep(NJ - 1, 0)
                keep(NJ - 1, 1)
                for k in range(IK):
                    dve.wait_ge(xi_done[k], (g + 1) * NB)
                dve.sem_inc(passed, 1)
                blocks(dve, g, convolve, idle, take, softplus)


def scans(nc, a, u_dram, bc_dram, y_drams, n_pairs):
    with ExitStack() as ctx:
        S = Scope(nc, ctx, "sc")
        passed = S.sem("passed")
        UC = DI + NDIR * REC * HEADS
        ident = S.sb("ident", [128, 128])
        later = S.sb2("later", [128, 128])
        upto = S.sb2("upto", [128, 128])
        upto_b = [ctx.enter_context(nc.sbuf_tensor(f"sc_upto_b{i}", [128, 128], BF16)) for i in range(2)]
        same_b = ctx.enter_context(nc.sbuf_tensor("sc_same_b", [128, 128], BF16))
        seen = S.sb2("seen", [128, SIDE])
        same = S.sb("same", [128, 128])
        u = S.sb2("u", [128, UC], NDIR)
        bz = S.sb2("bz", [128, 2, PB, NS], NDIR)
        state = S.sb2("state", [128, DI], NDIR)
        kept = S.sb2("kept", [128, DI])
        w_high, w_low = (S.sb2(n, [128, HEADS, SIDE], dtype=F32R) for n in ("w_high", "w_low"))
        later_r = S.sb2("later_r", [128, 128], dtype=F32R)
        xdt = S.sb2("xdt", [128, DI])
        xbd = S.sb2("xbd", [128, HEADS, PB, HP])
        xdd = S.sb2("xdd", [128, DI])
        e = S.sb2("e", [128, HEADS, SIDE])
        m_ = S.sb2("m", [128, HEADS, SIDE])
        bct = S.sb2("bct", [128, 2, 128])
        ctc = S.sb2("ctc", [128, SIDE])
        ecum = S.sb2("ecum", [128, 2 * HEADS])
        gm = S.sb2("gm", [128, SIDE])
        toff = S.sb2("toff", [128, DI])
        y = S.sb2("y", [128, DI])
        HH = HEADS // 2
        diff_ps = S.ps("diff", [128, 2, 512])
        misc_ps = S.ps("misc", [128, 512])
        off_ps, st_ps, yd_ps = S.ps("off", [128, 512]), S.ps("st", [128, 512]), S.ps("yd", [SIDE, 2, 512])
        c_in, zero, s_init, b_ready = S.sem("c_in"), S.sem("zero"), S.sem("s_init"), S.sem("b_ready")
        loaded, st_ready, s_ready = (S.sem2(n, NDIR) for n in ("loaded", "st_ready", "s_ready"))
        w_ready, xdt_ready, xbd_ready, tr, diff_ready, e_ready, xdd_ready, m_ready = (
            S.sem2(n) for n in ("w_ready", "xdt_ready", "xbd_ready", "tr", "diff_ready", "e_ready", "xdd_ready", "m_ready"))
        off_ready, toff_ready, kept_ready, yd_ready, y_ready, stored = (
            S.sem2(n) for n in ("off_ready", "toff_ready", "kept_ready", "yd_ready", "y_ready", "stored"))
        bct_ready, ecum_ready, g_ready, gm_ready = (S.sem(n) for n in ("bct_ready", "ecum_ready", "g_ready", "gm_ready"))
        block = ctx.enter_context(nc.Block())
        STEPS = SIDE
        heads = lambda t: t.rearrange("p (h c) -> p h c", h=HEADS)
        per_head = lambda t, n: t.unsqueeze(2).to_broadcast([128, HEADS, n])
        of = lambda k, r: u[k][:, DT0(k) + r * HEADS:DT0(k) + (r + 1) * HEADS]
        back = lambda k: k // 2

        def chunk(ten, g, k, c, b):
            at = (STEPS - 1) - c if back(k) else c
            if k % 2:
                return ten[g, at, b * SIDE:(b + 1) * SIDE]
            return ten[g, :, b * SIDE + at]

        def slot(t, k):
            return k % 2, t * 2 + k // 2

        def before(t, k):
            return (1 - k % 2, t * 2 + k // 2 + (k % 2))

        def run(eng, first, second, start=None, between=None, rest=None):
            def both(g, c, k, nc, nk):
                first(g, nc, nk)
                second(g, c, k)
                if between:
                    between(g, nc, nk)
                    rest(g, c, k)

            with eng.Fori(0, n_pairs) as g:
                if start:
                    start(g)
                first(g, 0, 0)
                if between:
                    between(g, 0, 0)
                with eng.Fori(0, STEPS - 1) as c:
                    for k in range(NDIR):
                        both(g, c, k, c + (k + 1) // NDIR, (k + 1) % NDIR)
                for k in range(NDIR - 1):
                    both(g, STEPS - 1, k, STEPS - 1, k + 1)
                second(g, STEPS - 1, NDIR - 1)
                if between:
                    rest(g, STEPS - 1, NDIR - 1)

        @block.sync
        def _(sp):
            for t, d in ((ident, a["ident"][:]), (later[0], a["later"][0]), (later[1], a["later"][1]), (upto[0], a["upto"][0]),
                         (upto[1], a["upto"][1]), (seen[0], a["seen"][0]), (seen[1], a["seen"][1]), (same, a["same"][:])):
                sp.dma_start(t[:], d).then_inc(c_in, 16)
            sp.wait_ge(zero, 2 * NDIR + 2)

            def load(g, c, k):
                t = g * STEPS + c
                sp.wait_ge(st_ready[k], t)
                sp.sem_inc(passed, 1)
                for b in range(PB):
                    rows = slice(b * 64, b * 64 + SIDE)
                    sp.dma_start(u[k][rows], chunk(u_dram, g, k, c, b)).then_inc(loaded[k], 16)
                    sp.dma_start(bz[k][rows, :, b], chunk(bc_dram, g, k, c, b)[:, k * 2 * NS:(k + 1) * 2 * NS].rearrange("p (s n) -> p s n", s=2)).then_inc(loaded[k], 16)

            def store(g, c, k):
                p, m = slot(g * STEPS + c, k)
                sp.wait_ge(y_ready[p], m + 1)
                sp.sem_inc(passed, 1)
                for b in range(PB):
                    sp.dma_start(chunk(y_drams[k], g, k, c, b), y[p][b * 64:b * 64 + SIDE]).then_inc(stored[p], 16)

            with sp.Fori(0, n_pairs) as g:
                for k in range(NDIR):
                    load(g, 0, k)
                with sp.Fori(0, STEPS - 1) as c:
                    for k in range(NDIR):
                        load(g, c + 1, k)
                        store(g, c, k)
                for k in range(NDIR):
                    store(g, STEPS - 1, k)
            for p in range(2):
                sp.wait_ge(stored[p], n_pairs * STEPS * 2 * 32)

        @block.gpsimd
        def _(pool):
            for k in range(NDIR):
                pool.memset(u[k][:], 0.0).then_inc(zero, 1)
                pool.memset(bz[k][:], 0.0).then_inc(zero, 1)
            for p in range(2):
                pool.memset(xbd[p][:], 0.0).then_inc(zero, 1)
            pool.wait_ge(c_in, 16 * 8)

            def start(g):
                for k in range(NDIR):
                    pool.wait_ge(s_ready[k], g * STEPS)
                pool.sem_inc(passed, 1)
                for k in range(NDIR):
                    pool.memset(state[k][:], 0.0).then_inc(s_init, 1)

            def first(g, c, k):
                t = g * STEPS + c
                n = t * NDIR + k
                p, m = slot(t, k)
                pool.wait_ge(loaded[k], (t + 1) * 64)
                pool.wait_ge(diff_ready[p], m)
                for part, r in ((w_high, DA_HIGH), (w_low, DA_LOW)):
                    ins = pool.tensor_tensor(part[p][:], per_head(of(k, r), SIDE), seen[back(k)][:].unsqueeze(1).to_broadcast([128, HEADS, SIDE]), ALU.mult)
                ins.then_inc(w_ready[p], 1)

            def second(g, c, k):
                t = g * STEPS + c
                p, m = slot(t, k)
                pool.wait_ge(s_init, (g + 1) * NDIR)
                pool.wait_ge(s_ready[k], t)
                pool.wait_ge(ecum_ready, t * NDIR + k + 1)
                pool.wait_ge(s_ready[(k + 2) % NDIR], t + k // 2)
                pool.tensor_tensor(heads(kept[p][:]), heads(state[k][:]), per_head(ecum[p][:, HEADS:], HP), ALU.mult).then_inc(kept_ready[p], 1)

            run(pool, first, second, start)

        @block.tensor
        def _(pe):
            pe.wait_ge(c_in, 16 * 8)
            pe.wait_ge(b_ready, 1)

            def first(g, c, k):
                t = g * STEPS + c
                n = t * NDIR + k
                p, m = slot(t, k)
                pe.wait_ge(loaded[k], (t + 1) * 64)
                pe.wait_ge(gm_ready, n)
                pe.transpose(misc_ps[:, 0:128], bz[k][:, 0].rearrange("p b n -> p (b n)"), ident[:])
                pe.transpose(misc_ps[:, 128:256], bz[k][:, 1].rearrange("p b n -> p (b n)"), ident[:])
                for at, ones in ((256, upto_b[back(k)]), (256 + HEADS, same_b)):
                    for r in (DA_HIGH, DA_REST, DA_REST2):
                        ins = pe.matmul(misc_ps[:, at:at + HEADS], ones[:], upper_half(of(k, r)), start=(r == DA_HIGH), stop=(r == DA_REST2))
                ins.then_inc(tr[p], 1)
                pe.wait_ge(w_ready[p], m + 1)
                q, mq = before(t, k)
                pe.wait_ge(e_ready[q], mq)
                for half in range(2):
                    for part in (w_high, w_low):
                        ins = pe.matmul(diff_ps[:, half, 0:HH * SIDE], later_r[back(k)][:],
                                        part[p][:, half * HH:(half + 1) * HH].rearrange("p h q -> p (h q)"),
                                        start=(part is w_high), stop=(part is w_low))
                ins.then_inc(diff_ready[p], 1)

            def masked(g, c, k):
                t = g * STEPS + c
                n = t * NDIR + k
                p, m = slot(t, k)
                pe.wait_ge(bct_ready, n + 1)
                pe.wait_ge(ecum_ready, n + 1)
                pe.matmul(misc_ps[:, 288:288 + SIDE], bct[p][:, 0], ctc[p][:], start=True, stop=True).then_inc(g_ready, 1)

            def second(g, c, k):
                t = g * STEPS + c
                p, m = slot(t, k)
                q, mq = before(t, k)
                pe.wait_ge(s_init, (g + 1) * NDIR)
                pe.wait_ge(s_ready[k], t)
                pe.wait_ge(toff_ready[q], mq)
                pe.matmul(off_ps[:, 0:DI], bct[p][:, 1], state[k][:], start=True, stop=True).then_inc(off_ready[p], 1)

            def rest(g, c, k):
                t = g * STEPS + c
                p, m = slot(t, k)
                q, mq = before(t, k)
                pe.wait_ge(xdd_ready[p], m + 1)
                pe.wait_ge(s_ready[(k - 1) % NDIR], t + (1 if k else 0))
                pe.matmul(st_ps[:, 0:DI], bz[k][:, 0].rearrange("p b n -> p (b n)"), xdd[p][:], start=True, stop=True).then_inc(st_ready[k], 1)
                pe.wait_ge(xbd_ready[p], m + 1)
                pe.wait_ge(m_ready[p], m + 1)
                pe.wait_ge(y_ready[q], mq)
                pe.sem_inc(passed, 1)
                for h in range(HEADS):
                    ins = pe.matmul(yd_ps[:, h // HH, h % HH * PB * HP:(h % HH + 1) * PB * HP], m_[p][:, h], xbd[p][:, h].rearrange("p b c -> p (b c)"),
                                    start=True, stop=True)
                ins.then_inc(yd_ready[p], 1)

            run(pe, first, second, between=masked, rest=rest)

        @block.scalar
        def _(act):
            def first(g, c, k):
                t = g * STEPS + c
                n = t * NDIR + k
                p, m = slot(t, k)
                act.wait_ge(tr[p], m + 1)
                act.wait_ge(off_ready[p], m)
                act.copy(bct[p][:].rearrange("p s n -> p (s n)"), misc_ps[:, 0:256])
                act.copy(ctc[p][0:64], misc_ps[0:64, 128:128 + SIDE])
                act.copy(ctc[p][64:128], misc_ps[64:128, 192:192 + SIDE]).then_inc(bct_ready, 1)
                act.wait_ge(toff_ready[p], m)
                act.wait_ge(kept_ready[p], m)
                act.activation(ecum[p][:], misc_ps[:, 256:256 + 2 * HEADS], ACT.Exp).then_inc(ecum_ready, 1)
                act.wait_ge(diff_ready[p], m + 1)
                act.wait_ge(m_ready[p], m)
                act.wait_ge(xdd_ready[p], m)
                act.activation(e[p][:].rearrange("p (t h) q -> p t (h q)", t=2), diff_ps[:, :, 0:HH * SIDE], ACT.Exp).then_inc(e_ready[p], 1)
                act.wait_ge(xdt_ready[p], m + 1)
                act.wait_ge(yd_ready[p], m)
                for b in range(PB):
                    rows = slice(b * 64, (b + 1) * 64)
                    ins = act.copy(xbd[p][rows, :, b], heads(xdt[p][rows]))
                ins.then_inc(xbd_ready[p], 1)

            run(act, first, lambda g, c, k: None)

        @block.vector
        def _(dve):
            dve.wait_ge(c_in, 16 * 8)
            for i in range(2):
                dve.tensor_copy(later_r[i][:], later[i][:])
            dve.tensor_copy(upto_b[0][:], upto[0][:])
            dve.tensor_copy(upto_b[1][:], upto[1][:])
            dve.tensor_copy(same_b[:], same[:]).then_inc(b_ready, 1)

            def first(g, c, k):
                t = g * STEPS + c
                n = t * NDIR + k
                p, m = slot(t, k)
                dve.wait_ge(loaded[k], (t + 1) * 64)
                dve.wait_ge(xbd_ready[p], m)
                dve.wait_ge(xdd_ready[p], m)
                dve.tensor_tensor(heads(xdt[p][:]), heads(u[k][:, 0:DI]), per_head(of(k, DT), HP), ALU.mult).then_inc(xdt_ready[p], 1)
                dve.wait_ge(g_ready, n + 1)
                dve.tensor_tensor(gm[p][:], misc_ps[:, 288:288 + SIDE], seen[back(k)][:], ALU.mult).then_inc(gm_ready, 1)
                dve.wait_ge(e_ready[p], m + 1)
                dve.wait_ge(xdt_ready[p], m + 1)
                last = 0 if back(k) else SIDE - 1
                dve.tensor_tensor(heads(xdd[p][:]), heads(xdt[p][:]), per_head(e[p][:, :, last], HP), ALU.mult).then_inc(xdd_ready[p], 1)
                dve.wait_ge(gm_ready, n + 1)
                dve.tensor_tensor(m_[p][:], e[p][:], gm[p][:].unsqueeze(1).to_broadcast([128, HEADS, SIDE]), ALU.mult).then_inc(m_ready[p], 1)

            def second(g, c, k):
                t = g * STEPS + c
                p, m = slot(t, k)
                dve.wait_ge(off_ready[p], m + 1)
                dve.wait_ge(ecum_ready, t * NDIR + k + 1)
                dve.tensor_tensor(heads(toff[p][:]), heads(off_ps[:, 0:DI]), per_head(ecum[p][:, 0:HEADS], HP), ALU.mult).then_inc(toff_ready[p], 1)
                dve.wait_ge(kept_ready[p], m + 1)
                dve.wait_ge(st_ready[k], t + 1)
                dve.tensor_tensor(state[k][:], st_ps[:, 0:DI], kept[p][:], ALU.add).then_inc(s_ready[k], 1)
                dve.wait_ge(yd_ready[p], m + 1)
                dve.wait_ge(toff_ready[p], m + 1)
                dve.wait_ge(stored[p], m * 32)
                for b in range(PB):
                    rows = slice(b * 64, b * 64 + SIDE)
                    banks = lambda x: x.rearrange("q (t h c) -> q t h c", t=2, h=HH)
                    ins = dve.tensor_tensor(banks(y[p][rows]), yd_ps[:, :, 0:HH * PB * HP].rearrange("q t (h b c) -> q t h b c", h=HH, b=PB)[:, :, :, b],
                                            banks(toff[p][rows]), ALU.add)
                ins.then_inc(y_ready[p], 1)

            run(dve, first, second)


def scan_out(nc, a, x_dram, z_dram, u_dram, y_drams, out, n_pairs):
    with ExitStack() as ctx:
        S = Scope(nc, ctx, "so")
        passed = S.sem("passed")
        ident = S.sb("ident", [128, 128])
        dsk = S.sb("dsk", [TOK, NDIR, DI])
        ng, nb = S.sb("ng", [128, IK]), S.sb("nb", [128, IK])
        wo = S.sb("wo", [128, IK, C])
        eps = S.sb("eps", [TOK, 1])
        u = S.sb2("u", [TOK, CW, DI])
        ys = [S.sb2(f"y{s}", [TOK, CW, DI], NDIR) for s in range(2)]
        skip = S.sb2("skip", [TOK, CW, DI])
        acc = S.sb("acc", [TOK, CW, DI])
        nrm = S.sb2("nrm", [TOK, CW, DI])
        stats = S.sb("stats", [TOK, CW, 6])
        mv = S.sb("mv", [TOK, CW, 2])
        std = S.sb("std", [TOK, CW])
        rstd = S.sb("rstd", [TOK, CW])
        z = S.sb2("z", [128, IK, BLK])
        x = S.sb2("x", [CP, KC, BLK])
        gated = S.sb2("gated", [128, IK, BLK])
        o = S.sb2("o", [CP, KC, BLK])
        t_ps = [[S.ps(f"tps{s}{k}", [128, BLK]) for k in range(IK)] for s in range(2)]
        o_ps = [S.ps(f"ops{k}", [CP, BLK]) for k in range(KC)]
        c_in, built, eps_ready = S.sem("c_in"), S.sem("built"), S.sem("eps_ready")
        in_, xz_in, stored = (S.sem2(n) for n in ("in", "xz_in", "stored"))
        part_sum, link, mv_ready, std_ready, nrm_ready = (S.sem(n) for n in ("part_sum", "link", "mv_ready", "std_ready", "nrm_ready"))
        sum_all, projected = S.sem2("sum_all"), S.sem2("projected")
        turned_s = S.sem2("turned")
        aff_ready, g_ready = S.sem2("aff", IK), S.sem2("g_ready", IK)
        o_psr, o_ready, xz_free = S.sem2("o_psr", KC), S.sem2("o_ready", KC), S.sem2("xz_free")
        block = ctx.enter_context(nc.Block())
        NJ = NB // 2
        ROUNDS = n_pairs * NJ

        nothing = lambda *_: None

        def blocks(eng, first, second, third=nothing):
            first(0, 0)
            first(0, 1)
            second(0, 0)
            with eng.Fori(0, ROUNDS - 1) as i:
                for s in range(2):
                    first(i + 1, s)
                    third(i, s)
                    second(i + s, 1 - s)
            third(ROUNDS - 1, 0)
            second(ROUNDS - 1, 1)
            third(ROUNDS - 1, 1)

        @block.sync
        def _(sp):
            for t, d in ((ident, a["ident"][:]), (ng, a["ng"][:]), (nb, a["nb"][:]), (wo, a["w_out"][:])):
                sp.dma_start(t[:], d).then_inc(c_in, 16)
            sp.dma_start(dsk[:], a["ds"][0].partition_broadcast(TOK)).then_inc(c_in, 16)

            def load_scans(i, s):
                g, cols = i // NJ, bass.ds((i % NJ * 2 + s) * CW, CW)
                sp.wait_ge(sum_all[s], i)
                for k in range(NDIR):
                    sp.dma_start(ys[s][k][:], y_drams[k][g, cols].rearrange("w p c -> p w c")).then_inc(in_[s], 16)
                sp.dma_start(u[s][:], u_dram[g, cols, :, 0:DI].rearrange("w p c -> p w c")).then_inc(in_[s], 16)

            def load_gate(i, s):
                g, cols = i // NJ, bass.ds((i % NJ * 2 + s) * CW, CW)
                sp.wait_ge(xz_free[s], i)
                sp.dma_start(z[s][:], z_dram[g, :, :, cols].rearrange("k c w b h -> c k (w b h)")).then_inc(xz_in[s], 16)
                sp.dma_start(x[s][:], x_dram[g, :, :, cols].rearrange("k c w b h -> c k (w b h)")).then_inc(xz_in[s], 16)

            blocks(sp, load_scans, nothing, load_gate)

        @block.gpsimd
        def _(pool):
            pool.memset(eps[:], LN_EPS).then_inc(eps_ready, 1)
            pool.wait_ge(built, 3)
            with pool.Fori(0, n_pairs * NJ) as i:
                for s in range(2):
                    n = i * 2 + s
                    pool.wait_ge(in_[s], (i + 1) * 80)
                    pool.wait_ge(sum_all[s], i)
                    pool.tensor_tensor(skip[s][:], u[s][:], dsk[:, 0].unsqueeze(1).to_broadcast([TOK, CW, DI]), ALU.mult).then_inc(part_sum, 1)
                    for k in (2, 3):
                        pool.wait_ge(part_sum, n * 3 + k - 1)
                        pool.tensor_tensor(skip[s][:], skip[s][:], ys[s][k][:], ALU.add).then_inc(part_sum, 1)

        @block.vector
        def _(dve):
            dve.wait_ge(c_in, 80)
            for k in range(1, NDIR):
                dve.tensor_tensor(dsk[:, 0], dsk[:, 0], dsk[:, k], ALU.add).then_inc(built, 1)
                dve.wait_ge(built, k)

            def sums(i, s):
                n = i * 2 + s
                L = 5
                step = [0]

                def chain(ins):
                    step[0] += 1
                    ins.then_inc(link, 1)
                    dve.wait_ge(link, n * L + step[0])

                dve.wait_ge(in_[s], (i + 1) * 80)
                chain(dve.tensor_tensor(acc[:], ys[s][0][:], ys[s][1][:], ALU.add))
                dve.wait_ge(part_sum, (n + 1) * 3)
                chain(dve.tensor_tensor(acc[:], acc[:], skip[s][:], ALU.add))
                dve.sem_inc(sum_all[s], 1)
                for w in range(CW):
                    ins = dve.bn_stats(stats[:, w], acc[:, w])
                chain(ins)
                dve.sem_inc(passed, 1)
                for w in range(CW):
                    ins = dve.bn_aggr(mv[:, w], stats[:, w])
                ins.then_inc(mv_ready, 1)
                dve.wait_ge(std_ready, n + 1)
                chain(dve.reciprocal(rstd[:], std[:]))
                dve.wait_ge(turned_s[s], i)
                for w in range(CW):
                    ins = dve.tensor_scalar(nrm[s][:, w], acc[:, w], mv[:, w, 0:1], rstd[:, w:w + 1], ALU.subtract, ALU.mult)
                chain(ins)
                assert step[0] == L
                dve.sem_inc(nrm_ready, 1)

            def gate(i, s):
                n = i * 2 + s
                dve.wait_ge(xz_in[s], (i + 1) * 32)
                for k in range(IK):
                    dve.wait_ge(aff_ready[k], n + 1)
                    dve.tensor_tensor(gated[s][:, k], gated[s][:, k], z[s][:, k], ALU.mult).then_inc(g_ready[k], 1)

            def residual(i, s):
                n = i * 2 + s
                dve.wait_ge(stored[s], i * 16)
                for oc in range(KC):
                    dve.wait_ge(o_psr[oc], n + 1)
                    dve.tensor_tensor(o[s][:, oc], o_ps[oc][:], x[s][:, oc], ALU.add).then_inc(o_ready[oc], 1)
                dve.wait_ge(o_ready[KC - 1], n + 1)
                dve.sem_inc(xz_free[s], 1)

            blocks(dve, sums, gate, residual)

        @block.tensor
        def _(pe):
            pe.wait_ge(c_in, 80)

            def turn(i, s):
                pe.wait_ge(nrm_ready, i * 2 + s + 1)
                for k in range(IK):
                    pe.wait_ge(aff_ready[k], i * 2)
                pe.sem_inc(passed, 1)
                for k in range(IK):
                    for w in range(CW):
                        ins = pe.transpose(t_ps[s][k][:, w * TOK:(w + 1) * TOK], nrm[s][:, w, k * 128:(k + 1) * 128], ident[0:TOK, 0:TOK])
                ins.then_inc(turned_s[s], 1)

            def project(i, s):
                n = i * 2 + s
                for k in range(IK):
                    pe.wait_ge(g_ready[k], n + 1)
                for oc in range(KC):
                    pe.wait_ge(o_ready[oc], n)
                    for k in range(IK):
                        ins = pe.matmul(o_ps[oc][:], wo[:, k, oc * CP:(oc + 1) * CP], gated[s][:, k], start=(k == 0), stop=(k == IK - 1))
                    ins.then_inc(o_psr[oc], 1)
                for oc in range(KC):
                    pe.wait_ge(o_psr[oc], n + 1)
                pe.sem_inc(projected[s], 1)

            blocks(pe, turn, project)

        @block.scalar
        def _(act):
            act.wait_ge(c_in, 80)
            act.wait_ge(eps_ready, 1)

            def affine(i, s):
                n = i * 2 + s
                act.wait_ge(mv_ready, n + 1)
                act.activation(std[:], mv[:, :, 1], ACT.Sqrt, bias=eps[:, 0:1]).then_inc(std_ready, 1)
                act.wait_ge(turned_s[s], i + 1)
                act.wait_ge(projected[s], i)
                for k in range(IK):
                    act.activation(gated[s][:, k], t_ps[s][k][:], ACT.Identity, bias=nb[:, k:k + 1], scale=ng[:, k:k + 1]).then_inc(aff_ready[k], 1)

            def store(i, s):
                n = i * 2 + s
                for oc in range(KC):
                    act.wait_ge(o_ready[oc], n + 1)
                g, j = i // NJ, i % NJ
                act.dma_start(out[g, :, :, bass.ds((j * 2 + s) * CW, CW)].rearrange("k c w b h -> c k (w b h)"), o[s][:]).then_inc(stored[s], 16)

            blocks(act, affine, nothing, store)
            for s in range(2):
                act.wait_ge(stored[s], 16 * n_pairs * NJ)


def build(nc, a, out, n_pairs):
    d = lambda n, s: nc.dram_tensor(n, s, F32, kind="Internal").ap()
    scale1, scale2 = d("scale1", (n_pairs, CP, KC * PB, 2)), d("scale2", (n_pairs, CP, KC * PB, 2))
    tables, toeplitz = d("tables", (2, D1, LAGS)), d("toeplitz", (2, SIDE, D1, SIDE))
    gated, mixed = d("gated", (n_pairs, TOK, SIDE, D1)), d("mixed", (n_pairs, SIDE, TOK, D1))
    x2 = d("x2", (n_pairs, KC, CP, SIDE, PB, SIDE))
    z = d("z", (n_pairs, IK, 128, SIDE, PB, SIDE))
    u = d("u", (n_pairs, SIDE, TOK, DI + NDIR * REC * HEADS))
    bc = d("bc", (n_pairs, SIDE, TOK, NDIR * 2 * NS))
    ys = [d(f"y{k}", (n_pairs, SIDE, TOK, DI)) for k in range(NDIR)]
    lag_tables(nc, a, a["lag"], tables)
    gn_stats(nc, "gn1", a["x"], scale1, a["gavg"], n_pairs)
    mixer_qv(nc, a["x"], scale1, a["wqv"], gated, tables, toeplitz, n_pairs)
    mixer_toeplitz(nc, gated, toeplitz, a["ident"], mixed, n_pairs)
    mixer_out(nc, a["x"], scale1, mixed, a["wp"], a["pb"], a["wo"], a["ob"], a["ident"], x2, n_pairs)
    gn_stats(nc, "gn2", x2, scale2, a["gavg"], n_pairs)
    scan_inputs(nc, x2, scale2, a, z, u, bc, n_pairs)
    scans(nc, a, u, bc, ys, n_pairs)
    scan_out(nc, a, x2, z, u, ys, out, n_pairs)


def lay_out_inputs(n):
    f = lambda k: np.ascontiguousarray(np.asarray(n[k]))
    x = f("x")
    pairs = x.shape[0] // PB
    arr = {}
    arr["x"] = x.reshape(pairs, PB, SIDE, SIDE, KC, CP).transpose(0, 4, 5, 3, 1, 2)
    qv = np.zeros((CP + 1, KC, 2 * D1), x.dtype)
    qv[:CP] = np.concatenate([f("L0_conv_q_w"), f("L0_conv_v_w")], 0).T.reshape(KC, CP, 2 * D1).transpose(1, 0, 2)
    qv[CP, KC - 1] = np.concatenate([f("L0_conv_q_b"), f("L0_conv_v_b")])
    arr["wqv"] = qv
    arr["wp"] = f("L0_conv_p_w").T.reshape(KC, CP, D1).transpose(1, 0, 2)
    arr["pb"] = f("L0_conv_p_b").reshape(DC, CP).T
    arr["wo"] = f("L0_conv_o_w").T.reshape(DC, CP, C).transpose(1, 0, 2)
    arr["ob"] = f("L0_conv_o_b").reshape(KC, CP).T
    arr["slope"] = f("L0_conv_slope").reshape(DC, CP).T
    t = lambda k: [f(f"L0_conv_t{i}_{k}") for i in (1, 2)]
    arr["t_w0"] = np.stack([np.stack([w[:, 0], b], 1) for w, b in zip(t("w0"), t("b0"))], 1)
    arr["t_ws"] = np.stack([w.transpose(0, 2, 1) for w in t("ws")])
    arr["t_bs"] = np.stack([b.T for b in t("bs")], 1)
    arr["t_wo"] = np.stack([w.T for w in t("wo")])
    arr["t_bo"] = np.stack([b.reshape(DC, CP).T for b in t("bo")], 1)
    arr["w_in"] = f("L1_conv_in_proj_w").T.reshape(KC, CP, 2 * DI).transpose(1, 0, 2)
    arr["cw"] = f("L1_conv_conv_w").reshape(IK, 128, 3, 3).transpose(1, 0, 2, 3)
    arr["cb"] = f("L1_conv_conv_b").reshape(IK, 128).T
    xp = f("L1_conv_x_proj_w")
    bc = xp[:, HEADS:].reshape(NDIR * 2 * NS, DI)
    dts = xp[:, :HEADS].reshape(NDIR * HEADS, DI)
    arr["wx"] = np.concatenate([bc, dts], 0).T.reshape(IK, 128, -1).transpose(1, 0, 2)
    arr["alog"] = f("L1_conv_A_logs").reshape(1, -1)
    arr["dtb"] = f("L1_conv_dt_bias").reshape(1, -1)
    arr["ds"] = f("L1_conv_Ds").reshape(1, NDIR, DI)
    arr["ng"] = f("L1_conv_out_norm_g").reshape(IK, 128).T
    arr["nb"] = f("L1_conv_out_norm_b").reshape(IK, 128).T
    arr["w_out"] = f("L1_conv_out_proj_w").T.reshape(IK, 128, C).transpose(1, 0, 2)
    lag = np.arange(-(SIDE - 1), SIDE, dtype=np.float32)
    arr["lag"] = np.stack([np.where(lag >= 0, lag, -(SIDE + lag)), np.abs(lag)])
    c = np.arange(CP)
    arr["gavg"] = (c[:, None] // 6 == c[None] // 6).astype(np.float32) / np.float32(6)
    arr["ident"] = np.eye(128, dtype=np.float32)
    i = np.arange(128)
    same = (i[:, None] // 64 == i[None] // 64)
    pos = i % 64
    q = np.arange(SIDE)
    arr["later"] = np.stack([same & (pos[:, None] > pos[None]), same & (pos[:, None] < pos[None])]).astype(np.float32)
    arr["upto"] = np.stack([same & (pos[:, None] <= pos[None]), same & (pos[:, None] >= pos[None])]).astype(np.float32)
    arr["seen"] = np.stack([pos[:, None] <= q[None], pos[:, None] >= q[None]]).astype(np.float32)
    arr["same"] = same.astype(np.float32)
    return {k: np.ascontiguousarray(v) for k, v in arr.items()}


def kernel(**inputs):
    import concourse.bacc as _bacc
    from concourse.bass_utils import run_bass_kernel_spmd as _run

    arrays = lay_out_inputs(inputs)
    nc = _bacc.Bacc("TRN2", target_bir_lowering=False, num_devices=1)
    aps = {k: nc.dram_tensor(k, v.shape, F32, kind="ExternalInput").ap() for k, v in arrays.items()}
    n_pairs = arrays["x"].shape[0]
    out = nc.dram_tensor("out", (n_pairs, KC, CP, SIDE, PB, SIDE), F32, kind="ExternalOutput").ap()
    build(nc, aps, out, n_pairs)
    r = _run(nc, [arrays], core_ids=[0])
    got = r.results[0]["out"]
    return got.transpose(0, 4, 5, 3, 1, 2).reshape(n_pairs * PB, SIDE, SIDE, C)
```
